# Optimizing a Trainium2 kernel written in Bass

```python
import numpy as np
import jax
import jax.numpy as jnp

def _softmax(x, axis=-1):
    return jax.nn.softmax(x, axis=axis)

def _gelu(x):
    return jax.nn.gelu(x, approximate=True)

def _silu(x):
    return jax.nn.silu(x)

def _sigmoid(x):
    return jax.nn.sigmoid(x)

def _layernorm(x, axis=-1, eps=1e-05):
    m = jnp.mean(x, axis=axis, keepdims=True)
    v = jnp.var(x, axis=axis, keepdims=True)
    return (x - m) / jnp.sqrt(v + eps)

def _scatter_add(tgt, idx, src, axis=0):
    return tgt.at[idx].add(src)

def _segment_sum(src, seg, n):
    return jax.ops.segment_sum(src, seg, n)
kernel_name = 'mk_gnn_ffn_d4_gnn_r32_abc102'

def setup_inputs(seed: int=0):
    np.random.seed(seed)
    _w = jnp.asarray

    def _rec_inputs():
        import jax
        import jax.numpy as jnp
        _gk = jax.random.key(seed)
        x = -0.0003713 + 1 * jax.random.normal(jax.random.fold_in(_gk, 1), (3125, 256), jnp.float32)
        src = jax.random.randint(jax.random.fold_in(_gk, 2), (50000,), 0, 3125, jnp.int32)
        dst = jax.random.randint(jax.random.fold_in(_gk, 3), (50000,), 0, 3125, jnp.int32)
        _o = jnp.argsort(dst, stable=True)
        src = src[_o]
        dst = dst[_o]
        edge_attr_18 = 0.00023367 + 0.999922 * jax.random.normal(jax.random.fold_in(_gk, 12), (50000, 18), jnp.float32)
        edge_type_64 = jax.random.randint(jax.random.fold_in(_gk, 14), (50000,), 0, 64, jnp.int32)
        return (x, src, dst, edge_attr_18, edge_type_64)
    x, src, dst, edge_attr_18, edge_type_64 = _rec_inputs()

    def _L0_gnn_setup():
        import jax, jax.numpy as jnp
        import numpy as np
        N_NODES = 50000
        N_EDGES = 25000
        IN_F = 256
        HEADS = 4
        OUT_F = 64
        NEG_SLOPE = 0.2
        key = jax.random.key(seed)
        k1, k2, k3, k4, k5 = jax.random.split(key, 5)
        x = jax.random.normal(k1, (N_NODES, IN_F), dtype=jnp.float32)
        edge_index = jax.random.randint(k2, (2, N_EDGES), 0, N_NODES, dtype=jnp.int64)
        W = jax.random.normal(k3, (IN_F, HEADS * OUT_F), dtype=jnp.float32) * (1.0 / np.sqrt(IN_F))
        att_src = jax.random.normal(k4, (1, HEADS, OUT_F), dtype=jnp.float32) * (1.0 / np.sqrt(OUT_F))
        att_dst = jax.random.normal(k5, (1, HEADS, OUT_F), dtype=jnp.float32) * (1.0 / np.sqrt(OUT_F))
        bias = jnp.zeros((HEADS * OUT_F,), dtype=jnp.float32)
        return {'x': x, 'edge_index': edge_index, 'W': W, 'att_src': att_src, 'att_dst': att_dst, 'bias': bias}
    _L0_gnn_all = _L0_gnn_setup()
    _L0_gnn_in = {k: v for k, v in _L0_gnn_all.items() if k in ('W', 'att_src', 'att_dst', 'bias')}
    del _L0_gnn_all

    def _L0_ffn_setup():
        import jax, jax.numpy as jnp
        import numpy as np
        B, S, D, E, H, K = (4, 128, 256, 8, 512, 2)
        key = jax.random.key(seed)
        ks = jax.random.split(key, 6)
        x = jax.random.normal(ks[0], (B, S, D), jnp.float32)
        Wg = jax.random.normal(ks[1], (D, E), jnp.float32) * 0.02
        bg = jnp.zeros((E,), jnp.float32)
        W1 = jax.random.normal(ks[2], (E, D, H), jnp.float32) * 0.02
        b1 = jnp.zeros((E, H), jnp.float32)
        W2 = jax.random.normal(ks[3], (E, H, D), jnp.float32) * 0.02
        b2 = jnp.zeros((E, D), jnp.float32)
        return {'x': x, 'Wg': Wg, 'bg': bg, 'W1': W1, 'b1': b1, 'W2': W2, 'b2': b2}
    _L0_ffn_all = _L0_ffn_setup()
    _L0_ffn_in = {k: v for k, v in _L0_ffn_all.items() if k in ('Wg', 'bg', 'W1', 'b1', 'W2', 'b2')}
    del _L0_ffn_all

    def _L1_gnn_setup():
        import jax, jax.numpy as jnp
        import numpy as np
        N_NODES = 25000
        N_EDGES = 12500
        D = 256
        key = jax.random.key(seed)
        k1, k2, k3, k4, k5 = jax.random.split(key, 5)
        feat = jax.random.normal(k1, (N_NODES, D), dtype=jnp.float32)
        src = jax.random.randint(k2, (N_EDGES,), 0, N_NODES, dtype=jnp.int32)
        dst = jax.random.randint(k3, (N_EDGES,), 0, N_NODES, dtype=jnp.int32)
        a = float(np.sqrt(6.0 / (D + D)))
        W1 = jax.random.uniform(k4, (D, D), minval=-a, maxval=a, dtype=jnp.float32)
        W2 = jax.random.uniform(k5, (D, D), minval=-a, maxval=a, dtype=jnp.float32)
        b = jnp.zeros((D,), dtype=jnp.float32)
        return {'feat': feat, 'W1': W1, 'W2': W2, 'b': b, 'src': src, 'dst': dst}
    _L1_gnn_all = _L1_gnn_setup()
    _L1_gnn_in = {k: v for k, v in _L1_gnn_all.items() if k in ('W1', 'W2', 'b')}
    del _L1_gnn_all

    def _L1_ffn_setup():
        import jax, jax.numpy as jnp
        import numpy as np
        B, N, D = (16, 128, 256)
        NUM_EXPERTS, TOP_K, HEADS = (4, 2, 4)
        N_EDGES = 32768
        LN_EPS = 1e-05

        def _layernorm(x, g, b):
            mu = x.mean(-1, keepdims=True)
            var = ((x - mu) ** 2).mean(-1, keepdims=True)
            return (x - mu) * jax.lax.rsqrt(var + LN_EPS) * g + b

        def _forward(x, edge_index, W_gat, att_src, att_dst, b_gat, ln_gamma, ln_beta, W1, b1, W2, b2):
            Bc, Nc, Dc = x.shape
            M = Bc * Nc
            x_flat = x.reshape(M, Dc)
            h = (x_flat @ W_gat).reshape(M, HEADS, NUM_EXPERTS)
            loops = jnp.arange(M, dtype=edge_index.dtype)
            src = jnp.concatenate([edge_index[0], loops])
            dst = jnp.concatenate([edge_index[1], loops])
            a_src = (h * att_src).sum(-1)
            a_dst = (h * att_dst).sum(-1)
            e = jax.nn.leaky_relu(a_src[src] + a_dst[dst], negative_slope=0.2)
            e_max = jax.ops.segment_max(e, dst, num_segments=M)
            ee = jnp.exp(e - e_max[dst])
            denom = jax.ops.segment_sum(ee, dst, num_segments=M)
            alpha = ee / (denom[dst] + 1e-16)
            msg = h[src] * alpha[:, :, None]
            agg = jax.ops.segment_sum(msg, dst, num_segments=M).reshape(M, HEADS * NUM_EXPERTS) + b_gat
            scores = _layernorm(agg, ln_gamma, ln_beta).reshape(M, HEADS, NUM_EXPERTS).mean(1)
            scores = scores.reshape(Bc, Nc, NUM_EXPERTS)
            topk_s, topk_i = jax.lax.top_k(scores, TOP_K)
            w = jax.nn.softmax(topk_s, axis=-1)
            out = jnp.zeros_like(x)
            for ei in range(NUM_EXPERTS):
                g = jnp.where(topk_i == ei, w, 0.0).sum(-1)
                hh = jax.nn.gelu(x @ W1[ei] + b1[ei], approximate=False)
                out = out + g[..., None] * (hh @ W2[ei] + b2[ei])
            return out
        key = jax.random.key(seed)
        ks = jax.random.split(key, 8)
        s = 0.05
        return {'x': jax.random.normal(ks[0], (B, N, D), jnp.float32), 'W_gat': jax.random.normal(ks[1], (D, HEADS * NUM_EXPERTS), jnp.float32) * s, 'att_src': jax.random.normal(ks[2], (HEADS, NUM_EXPERTS), jnp.float32) * s, 'att_dst': jax.random.normal(ks[3], (HEADS, NUM_EXPERTS), jnp.float32) * s, 'b_gat': jnp.zeros((HEADS * NUM_EXPERTS,), jnp.float32), 'ln_gamma': jnp.ones((HEADS * NUM_EXPERTS,), jnp.float32), 'ln_beta': jnp.zeros((HEADS * NUM_EXPERTS,), jnp.float32), 'W1': jax.random.normal(ks[4], (NUM_EXPERTS, D, 2 * D), jnp.float32) * s, 'b1': jnp.zeros((NUM_EXPERTS, 2 * D), jnp.float32), 'W2': jax.random.normal(ks[5], (NUM_EXPERTS, 2 * D, D), jnp.float32) * s, 'b2': jnp.zeros((NUM_EXPERTS, D), jnp.float32), 'edge_index': jax.random.randint(ks[6], (2, N_EDGES), 0, B * N, jnp.int32)}
    _L1_ffn_all = _L1_ffn_setup()
    _L1_ffn_in = {k: v for k, v in _L1_ffn_all.items() if k in ('W_gat', 'att_src', 'att_dst', 'b_gat', 'ln_gamma', 'ln_beta', 'W1', 'b1', 'W2', 'b2', 'edge_index')}
    del _L1_ffn_all

    def _L2_gnn_setup():
        import jax, jax.numpy as jnp
        import numpy as np
        N_NODES = 50000
        N_EDGES = 15625
        IN_DIM = 256
        HID = 64
        HEADS = 4
        N_REL = 64
        key = jax.random.key(seed)
        ks = jax.random.split(key, 16)
        s = 0.02
        return {'node_features': jax.random.normal(ks[0], (N_NODES, IN_DIM), jnp.float32), 'edge_index': jax.random.randint(ks[1], (2, N_EDGES), 0, N_NODES, jnp.int32), 'edge_relations': jax.random.randint(ks[2], (N_EDGES,), 0, N_REL, jnp.int32), 'query_emb': jax.random.normal(ks[3], (IN_DIM,), jnp.float32), 'Wq': jax.random.normal(ks[4], (IN_DIM, HID * HEADS), jnp.float32) * s, 'bq': jnp.zeros((HID * HEADS,), jnp.float32), 'Wk': jax.random.normal(ks[5], (IN_DIM, HID * HEADS), jnp.float32) * s, 'bk': jnp.zeros((HID * HEADS,), jnp.float32), 'Wv': jax.random.normal(ks[6], (IN_DIM, HID * HEADS), jnp.float32) * s, 'bv': jnp.zeros((HID * HEADS,), jnp.float32), 'rel_w': jax.random.normal(ks[7], (N_REL, HID), jnp.float32) * s, 'Wo': jax.random.normal(ks[8], (HID * HEADS, IN_DIM), jnp.float32) * s, 'bo': jnp.zeros((IN_DIM,), jnp.float32), 'gamma': jnp.ones((IN_DIM,), jnp.float32), 'beta': jnp.zeros((IN_DIM,), jnp.float32)}
    _L2_gnn_all = _L2_gnn_setup()
    _L2_gnn_in = {k: v for k, v in _L2_gnn_all.items() if k in ('query_emb', 'Wq', 'bq', 'Wk', 'bk', 'Wv', 'bv', 'rel_w', 'Wo', 'bo', 'gamma', 'beta')}
    del _L2_gnn_all

    def _L2_ffn_setup():
        import jax, jax.numpy as jnp
        import numpy as np
        TOP_K = 2
        LN_EPS = 1e-05
        key = jax.random.key(seed)
        ks = jax.random.split(key, 8)
        B, S, D, E, H = (16, 1024, 256, 8, 1024)
        x = jax.random.normal(ks[0], (B, S, D), dtype=jnp.float32)
        Wr = jax.random.normal(ks[1], (D, E), dtype=jnp.float32) * 0.1
        br = jnp.zeros((E,), dtype=jnp.float32)
        ln_g = jnp.ones((E, D), dtype=jnp.float32)
        ln_b = jnp.zeros((E, D), dtype=jnp.float32)
        W1 = jax.random.normal(ks[2], (E, D, H), dtype=jnp.float32) * (1.0 / np.sqrt(D))
        b1 = jnp.zeros((E, H), dtype=jnp.float32)
        W2 = jax.random.normal(ks[3], (E, H, D), dtype=jnp.float32) * (1.0 / np.sqrt(H))
        b2 = jnp.zeros((E, D), dtype=jnp.float32)
        return {'x': x, 'Wr': Wr, 'br': br, 'ln_g': ln_g, 'ln_b': ln_b, 'W1': W1, 'b1': b1, 'W2': W2, 'b2': b2}
    _L2_ffn_all = _L2_ffn_setup()
    _L2_ffn_in = {k: v for k, v in _L2_ffn_all.items() if k in ('Wr', 'br', 'ln_g', 'ln_b', 'W1', 'b1', 'W2', 'b2')}
    del _L2_ffn_all

    def _L3_gnn_setup():
        import jax, jax.numpy as jnp
        import numpy as np
        N, E = (50000, 25000)
        DIM, H, D = (256, 16, 8)
        DH = D * H
        IN_RPE = 18
        SCALE = D ** (-0.5)
        EPS = 1e-16

        def _segment_softmax(compat, s, num_nodes):
            m = jax.ops.segment_max(compat, s, num_segments=num_nodes)
            ex = jnp.exp(compat - m[s])
            den = jax.ops.segment_sum(ex, s, num_segments=num_nodes)
            return ex / (den[s] + EPS)
        key = jax.random.key(seed)
        ks = jax.random.split(key, 10)
        x = jax.random.normal(ks[0], (N, DIM), dtype=jnp.float32)
        edge_index = jax.random.randint(ks[1], (2, E), 0, N, dtype=jnp.int64)
        edge_attr = jax.random.normal(ks[2], (E, IN_RPE), dtype=jnp.float32)
        Wqkv = jax.random.normal(ks[3], (DIM, 2 * DH + DIM), dtype=jnp.float32) * DIM ** (-0.5)
        bqkv = jnp.zeros((2 * DH + DIM,), dtype=jnp.float32)
        Wk_rpe = jax.random.normal(ks[4], (IN_RPE, DH), dtype=jnp.float32) * IN_RPE ** (-0.5)
        bk_rpe = jnp.zeros((DH,), dtype=jnp.float32)
        Wq_rpe = jax.random.normal(ks[5], (IN_RPE, DH), dtype=jnp.float32) * IN_RPE ** (-0.5)
        bq_rpe = jnp.zeros((DH,), dtype=jnp.float32)
        return {'x': x, 'edge_index': edge_index, 'edge_attr': edge_attr, 'Wqkv': Wqkv, 'bqkv': bqkv, 'Wk_rpe': Wk_rpe, 'bk_rpe': bk_rpe, 'Wq_rpe': Wq_rpe, 'bq_rpe': bq_rpe}
    _L3_gnn_all = _L3_gnn_setup()
    _L3_gnn_in = {k: v for k, v in _L3_gnn_all.items() if k in ('Wqkv', 'bqkv', 'Wk_rpe', 'bk_rpe', 'Wq_rpe', 'bq_rpe')}
    del _L3_gnn_all

    def _L3_ffn_setup():
        import math
        import jax, jax.numpy as jnp
        import numpy as np
        CAPACITY_FACTOR = 1.25
        TOP_K = 2
        LN_EPS = 1e-05

        def _layer_norm(x, gamma, beta):
            mu = jnp.mean(x, axis=-1, keepdims=True)
            var = jnp.var(x, axis=-1, keepdims=True)
            return (x - mu) * jax.lax.rsqrt(var + LN_EPS) * gamma + beta
        key = jax.random.key(seed)
        ks = jax.random.split(key, 4)
        B, S, D, F, E = (8, 128, 256, 512, 8)
        x = jax.random.normal(ks[0], (B, S, D), dtype=jnp.float32)
        Wr = jax.random.normal(ks[1], (D, E), dtype=jnp.float32) / np.sqrt(D)
        br = jnp.zeros((E,), jnp.float32)
        W1 = jax.random.normal(ks[2], (E, D, F), dtype=jnp.float32) / np.sqrt(D)
        b1 = jnp.zeros((E, F), jnp.float32)
        W2 = jax.random.normal(ks[3], (E, F, D), dtype=jnp.float32) / np.sqrt(F)
        b2 = jnp.zeros((E, D), jnp.float32)
        gamma = jnp.ones((D,), jnp.float32)
        beta = jnp.zeros((D,), jnp.float32)
        return {'x': x, 'Wr': Wr, 'br': br, 'W1': W1, 'b1': b1, 'W2': W2, 'b2': b2, 'gamma': gamma, 'beta': beta}
    _L3_ffn_all = _L3_ffn_setup()
    _L3_ffn_in = {k: v for k, v in _L3_ffn_all.items() if k in ('Wr', 'br', 'W1', 'b1', 'W2', 'b2', 'gamma', 'beta')}
    del _L3_ffn_all
    return {'x': x, 'src': src, 'dst': dst, 'edge_attr_18': edge_attr_18, 'edge_type_64': edge_type_64, 'L0_gnn_W': _L0_gnn_in['W'], 'L0_gnn_att_src': _L0_gnn_in['att_src'], 'L0_gnn_att_dst': _L0_gnn_in['att_dst'], 'L0_gnn_bias': _L0_gnn_in['bias'], 'L0_ffn_Wg': _L0_ffn_in['Wg'], 'L0_ffn_bg': _L0_ffn_in['bg'], 'L0_ffn_W1': _L0_ffn_in['W1'], 'L0_ffn_b1': _L0_ffn_in['b1'], 'L0_ffn_W2': _L0_ffn_in['W2'], 'L0_ffn_b2': _L0_ffn_in['b2'], 'L1_gnn_W1': _L1_gnn_in['W1'], 'L1_gnn_W2': _L1_gnn_in['W2'], 'L1_gnn_b': _L1_gnn_in['b'], 'L1_ffn_W_gat': _L1_ffn_in['W_gat'], 'L1_ffn_att_src': _L1_ffn_in['att_src'], 'L1_ffn_att_dst': _L1_ffn_in['att_dst'], 'L1_ffn_b_gat': _L1_ffn_in['b_gat'], 'L1_ffn_ln_gamma': _L1_ffn_in['ln_gamma'], 'L1_ffn_ln_beta': _L1_ffn_in['ln_beta'], 'L1_ffn_W1': _L1_ffn_in['W1'], 'L1_ffn_b1': _L1_ffn_in['b1'], 'L1_ffn_W2': _L1_ffn_in['W2'], 'L1_ffn_b2': _L1_ffn_in['b2'], 'L1_ffn_edge_index': _L1_ffn_in['edge_index'], 'L2_gnn_query_emb': _L2_gnn_in['query_emb'], 'L2_gnn_Wq': _L2_gnn_in['Wq'], 'L2_gnn_bq': _L2_gnn_in['bq'], 'L2_gnn_Wk': _L2_gnn_in['Wk'], 'L2_gnn_bk': _L2_gnn_in['bk'], 'L2_gnn_Wv': _L2_gnn_in['Wv'], 'L2_gnn_bv': _L2_gnn_in['bv'], 'L2_gnn_rel_w': _L2_gnn_in['rel_w'], 'L2_gnn_Wo': _L2_gnn_in['Wo'], 'L2_gnn_bo': _L2_gnn_in['bo'], 'L2_gnn_gamma': _L2_gnn_in['gamma'], 'L2_gnn_beta': _L2_gnn_in['beta'], 'L2_ffn_Wr': _L2_ffn_in['Wr'], 'L2_ffn_br': _L2_ffn_in['br'], 'L2_ffn_ln_g': _L2_ffn_in['ln_g'], 'L2_ffn_ln_b': _L2_ffn_in['ln_b'], 'L2_ffn_W1': _L2_ffn_in['W1'], 'L2_ffn_b1': _L2_ffn_in['b1'], 'L2_ffn_W2': _L2_ffn_in['W2'], 'L2_ffn_b2': _L2_ffn_in['b2'], 'L3_gnn_Wqkv': _L3_gnn_in['Wqkv'], 'L3_gnn_bqkv': _L3_gnn_in['bqkv'], 'L3_gnn_Wk_rpe': _L3_gnn_in['Wk_rpe'], 'L3_gnn_bk_rpe': _L3_gnn_in['bk_rpe'], 'L3_gnn_Wq_rpe': _L3_gnn_in['Wq_rpe'], 'L3_gnn_bq_rpe': _L3_gnn_in['bq_rpe'], 'L3_ffn_Wr': _L3_ffn_in['Wr'], 'L3_ffn_br': _L3_ffn_in['br'], 'L3_ffn_W1': _L3_ffn_in['W1'], 'L3_ffn_b1': _L3_ffn_in['b1'], 'L3_ffn_W2': _L3_ffn_in['W2'], 'L3_ffn_b2': _L3_ffn_in['b2'], 'L3_ffn_gamma': _L3_ffn_in['gamma'], 'L3_ffn_beta': _L3_ffn_in['beta']}

def reference(x, src, dst, edge_attr_18, edge_type_64, L0_gnn_W, L0_gnn_att_src, L0_gnn_att_dst, L0_gnn_bias, L0_ffn_Wg, L0_ffn_bg, L0_ffn_W1, L0_ffn_b1, L0_ffn_W2, L0_ffn_b2, L1_gnn_W1, L1_gnn_W2, L1_gnn_b, L1_ffn_W_gat, L1_ffn_att_src, L1_ffn_att_dst, L1_ffn_b_gat, L1_ffn_ln_gamma, L1_ffn_ln_beta, L1_ffn_W1, L1_ffn_b1, L1_ffn_W2, L1_ffn_b2, L1_ffn_edge_index, L2_gnn_query_emb, L2_gnn_Wq, L2_gnn_bq, L2_gnn_Wk, L2_gnn_bk, L2_gnn_Wv, L2_gnn_bv, L2_gnn_rel_w, L2_gnn_Wo, L2_gnn_bo, L2_gnn_gamma, L2_gnn_beta, L2_ffn_Wr, L2_ffn_br, L2_ffn_ln_g, L2_ffn_ln_b, L2_ffn_W1, L2_ffn_b1, L2_ffn_W2, L2_ffn_b2, L3_gnn_Wqkv, L3_gnn_bqkv, L3_gnn_Wk_rpe, L3_gnn_bk_rpe, L3_gnn_Wq_rpe, L3_gnn_bq_rpe, L3_ffn_Wr, L3_ffn_br, L3_ffn_W1, L3_ffn_b1, L3_ffn_W2, L3_ffn_b2, L3_ffn_gamma, L3_ffn_beta):
    import jax
    import jax.numpy as jnp

    def _L0_gnn_ref(x, edge_index, W, att_src, att_dst, bias):
        import jax, jax.numpy as jnp
        import numpy as np
        N_NODES = 50000
        N_EDGES = 25000
        IN_F = 256
        HEADS = 4
        OUT_F = 64
        NEG_SLOPE = 0.2
        N = x.shape[0]
        h = (x @ W).reshape(N, HEADS, OUT_F)
        a_src = jnp.sum(h * att_src, axis=-1)
        a_dst = jnp.sum(h * att_dst, axis=-1)
        loop = jnp.arange(N, dtype=edge_index.dtype)
        src = jnp.concatenate([edge_index[0], loop])
        dst = jnp.concatenate([edge_index[1], loop])
        e = jax.nn.leaky_relu(a_src[src] + a_dst[dst], negative_slope=NEG_SLOPE)
        e_max = jax.lax.stop_gradient(jax.ops.segment_max(e, dst, num_segments=N))
        e_max = jnp.where(jnp.isfinite(e_max), e_max, 0.0)
        ex = jnp.exp(e - e_max[dst])
        denom = jax.ops.segment_sum(ex, dst, num_segments=N)
        alpha = ex / denom[dst]
        msg = h[src] * alpha[..., None]
        out = jax.ops.segment_sum(msg, dst, num_segments=N)
        return out.reshape(N, HEADS * OUT_F) + bias

    def _L0_ffn_ref(x, Wg, bg, W1, b1, W2, b2):
        import jax, jax.numpy as jnp
        import numpy as np
        B, S, D, E, H, K = (4, 128, 256, 8, 512, 2)
        Bv, Sv, Dv = x.shape
        gate_scores = x @ Wg + bg
        _, idx = jax.lax.top_k(gate_scores, K)
        mask = jax.nn.one_hot(idx, E, dtype=x.dtype).sum(axis=-2)
        xf = x.reshape(-1, Dv)
        mf = mask.reshape(-1, E)
        h = jax.nn.gelu(jnp.einsum('td,edh->teh', xf, W1) + b1[None], approximate=False)
        y = jnp.einsum('teh,ehd->ted', h, W2) + b2[None]
        out = jnp.einsum('ted,te->td', y, mf)
        return out.reshape(Bv, Sv, Dv)

    def _L1_gnn_ref(feat, W1, W2, b, src, dst):
        import jax, jax.numpy as jnp
        import numpy as np
        N_NODES = 25000
        N_EDGES = 12500
        D = 256
        n = feat.shape[0]
        ones = jnp.ones(src.shape[0], dtype=feat.dtype)
        out_deg = jnp.maximum(jax.ops.segment_sum(ones, src, num_segments=n), 1.0)
        in_cnt = jax.ops.segment_sum(ones, dst, num_segments=n)
        t1 = feat @ W1
        msg = t1[src] + feat[src] * feat[dst] @ W2
        scale = jnp.sqrt(out_deg[src]) * jnp.sqrt(out_deg[dst])
        msg = msg / scale[:, None]
        agg = jax.ops.segment_sum(msg, dst, num_segments=n)
        embed = jnp.where(in_cnt[:, None] > 0, t1 + agg, jnp.zeros_like(t1))
        embed = embed + b
        embed = jax.nn.leaky_relu(embed, negative_slope=0.01)
        norm = jnp.linalg.norm(embed, axis=1, keepdims=True)
        embed = embed / jnp.maximum(norm, 1e-12)
        return embed

    def _L1_ffn_ref(x, W_gat, att_src, att_dst, b_gat, ln_gamma, ln_beta, W1, b1, W2, b2, edge_index):
        import jax, jax.numpy as jnp
        import numpy as np
        B, N, D = (16, 128, 256)
        NUM_EXPERTS, TOP_K, HEADS = (4, 2, 4)
        N_EDGES = 32768
        LN_EPS = 1e-05

        def _layernorm(x, g, b):
            mu = x.mean(-1, keepdims=True)
            var = ((x - mu) ** 2).mean(-1, keepdims=True)
            return (x - mu) * jax.lax.rsqrt(var + LN_EPS) * g + b

        def _forward(x, edge_index, W_gat, att_src, att_dst, b_gat, ln_gamma, ln_beta, W1, b1, W2, b2):
            Bc, Nc, Dc = x.shape
            M = Bc * Nc
            x_flat = x.reshape(M, Dc)
            h = (x_flat @ W_gat).reshape(M, HEADS, NUM_EXPERTS)
            loops = jnp.arange(M, dtype=edge_index.dtype)
            src = jnp.concatenate([edge_index[0], loops])
            dst = jnp.concatenate([edge_index[1], loops])
            a_src = (h * att_src).sum(-1)
            a_dst = (h * att_dst).sum(-1)
            e = jax.nn.leaky_relu(a_src[src] + a_dst[dst], negative_slope=0.2)
            e_max = jax.ops.segment_max(e, dst, num_segments=M)
            ee = jnp.exp(e - e_max[dst])
            denom = jax.ops.segment_sum(ee, dst, num_segments=M)
            alpha = ee / (denom[dst] + 1e-16)
            msg = h[src] * alpha[:, :, None]
            agg = jax.ops.segment_sum(msg, dst, num_segments=M).reshape(M, HEADS * NUM_EXPERTS) + b_gat
            scores = _layernorm(agg, ln_gamma, ln_beta).reshape(M, HEADS, NUM_EXPERTS).mean(1)
            scores = scores.reshape(Bc, Nc, NUM_EXPERTS)
            topk_s, topk_i = jax.lax.top_k(scores, TOP_K)
            w = jax.nn.softmax(topk_s, axis=-1)
            out = jnp.zeros_like(x)
            for ei in range(NUM_EXPERTS):
                g = jnp.where(topk_i == ei, w, 0.0).sum(-1)
                hh = jax.nn.gelu(x @ W1[ei] + b1[ei], approximate=False)
                out = out + g[..., None] * (hh @ W2[ei] + b2[ei])
            return out
        return _forward(x, edge_index, W_gat, att_src, att_dst, b_gat, ln_gamma, ln_beta, W1, b1, W2, b2)

    def _L2_gnn_ref(node_features, edge_index, edge_relations, query_emb, Wq, bq, Wk, bk, Wv, bv, rel_w, Wo, bo, gamma, beta):
        import jax, jax.numpy as jnp
        import numpy as np
        N_NODES = 50000
        N_EDGES = 15625
        IN_DIM = 256
        HID = 64
        HEADS = 4
        N_REL = 64
        N = node_features.shape[0]
        D = rel_w.shape[1]
        H = Wq.shape[1] // D
        enh = node_features + 0.1 * query_emb[None, :]
        Q = (enh @ Wq + bq).reshape(N, H, D)
        K = (enh @ Wk + bk).reshape(N, H, D)
        V = (enh @ Wv + bv).reshape(N, H, D)
        src, dst = (edge_index[0], edge_index[1])
        rel = rel_w[edge_relations]
        mod_k = K[src] + 0.2 * rel[:, None, :]
        scores = jnp.einsum('ehd,ehd->eh', Q[dst], mod_k) / D ** 0.5
        seg_max = jax.ops.segment_max(scores, dst, num_segments=N)
        ex = jnp.exp(scores - seg_max[dst])
        denom = jax.ops.segment_sum(ex, dst, num_segments=N)
        w = ex / denom[dst]
        agg = jax.ops.segment_sum(w[:, :, None] * V[src], dst, num_segments=N)
        deg = jax.ops.segment_sum(jnp.ones((src.shape[0],), jnp.float32), dst, num_segments=N)
        msgs = jnp.where(deg[:, None, None] > 0, agg, V)
        out = msgs.reshape(N, H * D) @ Wo + bo
        x = out + node_features
        mu = jnp.mean(x, axis=-1, keepdims=True)
        var = jnp.var(x, axis=-1, keepdims=True)
        return (x - mu) / jnp.sqrt(var + 1e-05) * gamma + beta

    def _L2_ffn_ref(x, Wr, br, ln_g, ln_b, W1, b1, W2, b2):
        import jax, jax.numpy as jnp
        import numpy as np
        TOP_K = 2
        LN_EPS = 1e-05
        B, S, D = x.shape
        N = B * S
        xt = x.reshape(N, D)
        logits = xt @ Wr + br
        probs = jax.nn.softmax(logits, axis=-1)
        top_p, top_idx = jax.lax.top_k(probs, TOP_K)
        weights = top_p / top_p.sum(axis=-1, keepdims=True)
        mu = xt.mean(axis=-1, keepdims=True)
        var = ((xt - mu) ** 2).mean(axis=-1, keepdims=True)
        xn = (xt - mu) * jax.lax.rsqrt(var + LN_EPS)
        xe = xn[None, :, :] * ln_g[:, None, :] + ln_b[:, None, :]
        h = jax.nn.gelu(jnp.einsum('end,edh->enh', xe, W1) + b1[:, None, :], approximate=False)
        y = jnp.einsum('enh,ehd->end', h, W2) + b2[:, None, :]
        y_tok = jnp.transpose(y, (1, 0, 2))
        sel = jnp.take_along_axis(y_tok, top_idx[:, :, None], axis=1)
        out = (weights[:, :, None] * sel).sum(axis=1)
        return out.reshape(B, S, D)

    def _L3_gnn_ref(x, edge_index, edge_attr, Wqkv, bqkv, Wk_rpe, bk_rpe, Wq_rpe, bq_rpe):
        import jax, jax.numpy as jnp
        import numpy as np
        N, E = (50000, 25000)
        DIM, H, D = (256, 16, 8)
        DH = D * H
        IN_RPE = 18
        SCALE = D ** (-0.5)
        EPS = 1e-16

        def _segment_softmax(compat, s, num_nodes):
            m = jax.ops.segment_max(compat, s, num_segments=num_nodes)
            ex = jnp.exp(compat - m[s])
            den = jax.ops.segment_sum(ex, s, num_segments=num_nodes)
            return ex / (den[s] + EPS)
        n = x.shape[0]
        e = edge_index.shape[1]
        qkv = x @ Wqkv + bqkv
        q = qkv[:, :DH].reshape(n, H, D)
        k = qkv[:, DH:2 * DH].reshape(n, H, D)
        v = qkv[:, 2 * DH:].reshape(n, H, DIM // H)
        s, t = (edge_index[0], edge_index[1])
        qe = q[s] * SCALE
        ke = k[t]
        ke = ke + (edge_attr @ Wk_rpe + bk_rpe).reshape(e, H, D)
        qe = qe + (edge_attr @ Wq_rpe + bq_rpe).reshape(e, H, D)
        compat = jnp.einsum('ehd,ehd->eh', qe, ke)
        attn = _segment_softmax(compat, s, n)
        msg = (v[t] * attn[..., None]).reshape(e, DIM)
        out = jax.ops.segment_sum(msg, s, num_segments=n)
        return out

    def _L3_ffn_ref(x, Wr, br, W1, b1, W2, b2, gamma, beta):
        import math
        import jax, jax.numpy as jnp
        import numpy as np
        CAPACITY_FACTOR = 1.25
        TOP_K = 2
        LN_EPS = 1e-05

        def _layer_norm(x, gamma, beta):
            mu = jnp.mean(x, axis=-1, keepdims=True)
            var = jnp.var(x, axis=-1, keepdims=True)
            return (x - mu) * jax.lax.rsqrt(var + LN_EPS) * gamma + beta
        B, S, D = x.shape
        E = Wr.shape[1]
        N = B * S
        K = TOP_K
        logits = jnp.mean(x, axis=1) @ Wr + br
        routing_weights = jax.nn.softmax(logits, axis=-1)
        capacity = float(math.ceil(N * CAPACITY_FACTOR / E))
        expected_loads = routing_weights.sum(axis=0) * (N / B)
        scale = jnp.where(expected_loads > capacity, capacity / expected_loads, 1.0)
        routing_weights = jax.nn.softmax(routing_weights * scale, axis=-1)
        rw_tok = jnp.broadcast_to(routing_weights[:, None, :], (B, S, E)).reshape(N, E)
        top_w, top_i = jax.lax.top_k(rw_tok, K)
        top_w = jax.nn.softmax(top_w, axis=-1)
        xf = x.reshape(N, D)
        h = jax.nn.gelu(jnp.einsum('nd,edf->enf', xf, W1) + b1[:, None, :], approximate=False)
        y = jnp.einsum('enf,efd->end', h, W2) + b2[:, None, :]
        w_dense = jnp.zeros((N, E), x.dtype).at[jnp.arange(N)[:, None], top_i].add(top_w)
        out = jnp.einsum('ne,end->nd', w_dense, y).reshape(B, S, D)
        out = _layer_norm(out + x, gamma, beta)
        return out
    edge_index = jnp.stack([src, dst])
    x = x + _L0_gnn_ref(_layernorm(x, axis=-1), edge_index, L0_gnn_W, L0_gnn_att_src, L0_gnn_att_dst, L0_gnn_bias)
    x = x + _L0_ffn_ref(_layernorm(x, axis=-1)[None], L0_ffn_Wg, L0_ffn_bg, L0_ffn_W1, L0_ffn_b1, L0_ffn_W2, L0_ffn_b2)[0]
    x = x + _L1_gnn_ref(_layernorm(x, axis=-1), L1_gnn_W1, L1_gnn_W2, L1_gnn_b, src, dst)
    x = x + _L1_ffn_ref(_layernorm(x, axis=-1)[None], L1_ffn_W_gat, L1_ffn_att_src, L1_ffn_att_dst, L1_ffn_b_gat, L1_ffn_ln_gamma, L1_ffn_ln_beta, L1_ffn_W1, L1_ffn_b1, L1_ffn_W2, L1_ffn_b2, L1_ffn_edge_index)[0]
    x = x + _L2_gnn_ref(_layernorm(x, axis=-1), edge_index, edge_type_64, L2_gnn_query_emb, L2_gnn_Wq, L2_gnn_bq, L2_gnn_Wk, L2_gnn_bk, L2_gnn_Wv, L2_gnn_bv, L2_gnn_rel_w, L2_gnn_Wo, L2_gnn_bo, L2_gnn_gamma, L2_gnn_beta)
    x = x + _L2_ffn_ref(_layernorm(x, axis=-1)[None], L2_ffn_Wr, L2_ffn_br, L2_ffn_ln_g, L2_ffn_ln_b, L2_ffn_W1, L2_ffn_b1, L2_ffn_W2, L2_ffn_b2)[0]
    x = x + _L3_gnn_ref(_layernorm(x, axis=-1), edge_index, edge_attr_18, L3_gnn_Wqkv, L3_gnn_bqkv, L3_gnn_Wk_rpe, L3_gnn_bk_rpe, L3_gnn_Wq_rpe, L3_gnn_bq_rpe)
    x = x + _L3_ffn_ref(_layernorm(x, axis=-1)[None], L3_ffn_Wr, L3_ffn_br, L3_ffn_W1, L3_ffn_b1, L3_ffn_W2, L3_ffn_b2, L3_ffn_gamma, L3_ffn_beta)[0]
    return x

_drawn_inputs = setup_inputs


def setup_inputs(seed=0):
    import zlib

    import numpy as np

    out = dict(_drawn_inputs(seed))
    spreads = {'L0_gnn_bias': (0.0, 0.1),
     'L0_ffn_bg': (0.0, 0.1),
     'L0_ffn_b1': (0.0, 0.1),
     'L0_ffn_b2': (0.0, 0.1),
     'L1_gnn_b': (0.0, 0.1),
     'L1_ffn_b_gat': (0.0, 0.1),
     'L1_ffn_ln_gamma': (1.0, 0.2),
     'L1_ffn_ln_beta': (0.0, 0.1),
     'L1_ffn_b1': (0.0, 0.1),
     'L1_ffn_b2': (0.0, 0.1),
     'L2_gnn_bq': (0.0, 0.8),
     'L2_gnn_bk': (0.0, 2.0),
     'L2_gnn_bv': (0.0, 0.315),
     'L2_gnn_bo': (0.0, 0.1),
     'L2_gnn_gamma': (1.0, 0.2),
     'L2_gnn_beta': (0.0, 0.1),
     'L2_ffn_br': (0.0, 0.1),
     'L2_ffn_ln_g': (1.0, 0.2),
     'L2_ffn_ln_b': (0.0, 0.311),
     'L2_ffn_b1': (0.0, 0.317),
     'L2_ffn_b2': (0.0, 0.1),
     'L3_gnn_bqkv': (0.0, 0.1),
     'L3_gnn_bk_rpe': (0.0, 0.1),
     'L3_gnn_bq_rpe': (0.0, 0.1),
     'L3_ffn_br': (0.0, 0.8),
     'L3_ffn_b1': (0.0, 0.57),
     'L3_ffn_b2': (0.0, 0.392),
     'L3_ffn_gamma': (1.0, 0.2),
     'L3_ffn_beta': (0.0, 0.279)}
    factors = {'L2_gnn_query_emb': 6.267, 'L2_gnn_Wq': 8.0, 'L2_gnn_Wk': 8.0, 'L2_gnn_rel_w': 195.74}
    for name, (base, spread) in spreads.items():
        noise = np.random.default_rng([zlib.crc32(name.encode()), seed]).standard_normal(out[name].shape)
        drawn = base * np.exp(spread * noise) if base else spread * noise
        out[name] = jnp.asarray(drawn.astype(out[name].dtype))
    for name, factor in factors.items():
        out[name] = (out[name] * factor).astype(out[name].dtype)
    return out
```

```python
from contextlib import ExitStack

import numpy as np

import concourse.bass as bass
from concourse import mybir

F32, BF16, I32 = mybir.dt.float32, mybir.dt.bfloat16, mybir.dt.int32
ALU, ACT, AX = mybir.AluOpType, mybir.ActivationFunctionType, mybir.AxisListType

NODES, D = 3125, 256
NP, NT = 125, 25
KC = D // 128
HALF = 8
STEP = 2 * HALF
BIG = 1e30
ROW = 32
ATTR = 18
KEY, OTHER = 20, 21
DIV_MUL, DIV_SHIFT = 1311, 15
CLEAR_AT = 60
FFN_TILES = 5
TOK = FFN_TILES * NP


class Room:

    def __init__(self, nc, stack, prefix):
        self.nc, self.stack, self.prefix = nc, stack, prefix

    def sb(self, name, shape, dt=F32):
        return self.stack.enter_context(self.nc.sbuf_tensor(f"{self.prefix}_{name}", shape, dt))

    def ps(self, name, shape, dt=F32):
        return self.stack.enter_context(self.nc.psum_tensor(f"{self.prefix}_{name}", shape, dt))

    def sem(self, name):
        return self.stack.enter_context(self.nc.semaphore(f"{self.prefix}_{name}"))


class InOrder:

    def __init__(self, engine, sem):
        self.engine, self.sem, self.n = engine, sem, 0

    def fire(self, ins):
        self.n += 1
        ins.then_inc(self.sem, 1)

    def join(self):
        self.engine.wait_ge(self.sem, self.n)

    def __call__(self, ins):
        self.fire(ins)
        self.join()

    def restart(self):
        self.engine.sem_clear(self.sem)
        self.n = 0


def bc(ap, shape):
    return ap.broadcast_to(list(shape))


def loop(engine, turns, turn):
    turn(0, True, False)
    if turns > 2:
        with engine.Fori(1, turns - 1) as i:
            turn(i, False, False)
    turn(turns - 1, False, True)


class Edges:

    def __init__(self, room, name, parts, cols):
        self.name, self.parts, self.cols = name, parts, cols
        self.first = room.sb(f"{name}_first", [parts, 1])
        self.last = room.sb(f"{name}_last", [parts, 1])
        self.closes = room.sb(f"{name}_closes", [parts, 1])
        self.before = room.sb(f"{name}_before", [parts, parts])
        self.after = room.sb(f"{name}_after", [parts, parts])
        self.end = room.sb(f"{name}_end", [NP, NT], I32)
        self.has = room.sb(f"{name}_has", [NP, NT])


class Program:
    def __init__(self, nc, A, out):
        self.nc, self.A, self.out = nc, A, out

    def clear_semaphores(self):
        ids = set(self.nc.released_uncleared_semaphores)
        if len(ids) < CLEAR_AT:
            return
        ids = sorted(ids)
        runs = []
        for k in ids:
            if runs and runs[-1][-1] == k - 1:
                runs[-1].append(k)
            else:
                runs.append([k])
        with self.nc.Block() as block:

            @block.gpsimd
            def _(pool):
                for run in runs:
                    pool.sem_clear(range(run[0], run[-1] + 1))

    def moved_sem(self, name):
        return self.room.sem(name)

    def stage(self, name):
        self.clear_semaphores()
        stack = ExitStack()
        return stack, Room(self.nc, stack, name)

    def setup(self, room):
        nc = self.nc
        self.room = room
        self.X = room.sb("X", [NP, NT, D])
        self.XH = room.sb("XH", [NP, NT, D])
        self.XT = room.sb("XT", [128, KC, NODES])
        self.ident = room.sb("ident", [128, 128])
        self.identb = room.sb("identb", [128, 128], BF16)
        self.upper = room.sb("upper", [128, 128])
        self.lower = room.sb("lower", [128, 128])
        self.hi_values = room.sb("hi_values", [128, NP])
        self.lo_values = room.sb("lo_values", [128, NT])
        self.small = room.sb("small", [128, 64])
        self.isout = room.sb("isout", [NP, NT])
        stack, r = self.stage("setup")
        with stack:
            made, loaded = r.sem("made"), r.sem("loaded")
            block = stack.enter_context(nc.Block())

            @block.gpsimd
            def _(pool):
                own = InOrder(pool, made)
                own.fire(pool.memset(self.ident[:], 0.0))
                own.fire(pool.memset(self.upper[:], 1.0))
                own.fire(pool.memset(self.lower[:], 1.0))
                own.fire(pool.iota(self.hi_values[:], [[NT, NP]], base=0, channel_multiplier=0,
                                   allow_small_or_imprecise_dtypes=True))
                own.fire(pool.iota(self.lo_values[:], [[1, NT]], base=0, channel_multiplier=0,
                                   allow_small_or_imprecise_dtypes=True))
                own(pool.iota(self.small[:], [[1, 64]], base=0, channel_multiplier=0,
                              allow_small_or_imprecise_dtypes=True))
                own.fire(pool.affine_select(out=self.ident[:], in_=self.ident[:], compare_op=ALU.not_equal,
                                            fill=1.0, base=0, pattern=[[-1, 128]], channel_multiplier=1))
                own.fire(pool.affine_select(out=self.upper[:], in_=self.upper[:], compare_op=ALU.is_gt,
                                            fill=0.0, base=0, pattern=[[1, 128]], channel_multiplier=-1))
                own(pool.affine_select(out=self.lower[:], in_=self.lower[:], compare_op=ALU.is_gt,
                                       fill=0.0, base=0, pattern=[[-1, 128]], channel_multiplier=1))
                own(pool.tensor_copy(self.identb[:], self.ident[:]))

            @block.sync
            def _(sp):
                sp.dma_start(self.X[:], self.A["x"].rearrange("(p t) d -> p t d", t=NT)).then_inc(loaded, 16)
                sp.wait_ge(loaded, 16)

    def finish(self):
        stack, r = self.stage("store")
        with stack:
            stored = r.sem("stored")
            block = stack.enter_context(self.nc.Block())

            @block.sync
            def _(sp):
                sp.dma_start(self.out.rearrange("(p t) d -> p t d", t=NT), self.X[:]).then_inc(stored, 16)
                sp.wait_ge(stored, 16)

    def rows_statistics(self, dve, own, src, r):
        nc = self.nc
        stats, mv = r.sb("stats", [NP, NT, 6]), r.sb("mv", [NP, NT, 2])
        for t in range(NT):
            own.fire(nc.vector.bn_stats(stats[:, t, :], src[:, t, :]))
        own.join()
        for t in range(NT):
            own.fire(nc.vector.bn_aggr(mv[:, t, :], stats[:, t, :]))
        own.join()
        return mv

    def normalise(self, name, src):
        nc, XH, XT = self.nc, self.XH, self.XT
        stack, r = self.stage(name)
        with stack:
            sd, rstd = r.sb("sd", [NP, NT]), r.sb("rstd", [NP, NT])
            tp = [r.ps(f"tp{k}", [128, 512]) for k in range(4)]
            own_dve = r.sem("own_dve")
            var_ready, sd_ready, rows_ready = r.sem("var_ready"), r.sem("sd_ready"), r.sem("rows_ready")
            turned, copied = r.sem("turned"), r.sem("copied")
            groups = [(t, min(t + 4, NT), c) for t in range(0, NT, 4) for c in range(KC)]
            block = stack.enter_context(nc.Block())

            @block.vector
            def _(dve):
                own = InOrder(dve, own_dve)
                mv = self.rows_statistics(dve, own, src, r)
                own(nc.vector.tensor_scalar_add(rstd[:], mv[:, :, 1], 1e-5))
                dve.sem_inc(var_ready, 1)
                dve.wait_ge(sd_ready, 1)
                own(nc.vector.reciprocal(rstd[:], sd[:]))
                for t in range(NT):
                    nc.vector.tensor_scalar(XH[:, t, :], src[:, t, :], mv[:, t, 0:1], rstd[:, t:t + 1],
                                            ALU.subtract, ALU.mult).then_inc(rows_ready, 1)

            @block.tensor
            def _(pe):
                for n, (a, b, c) in enumerate(groups):
                    pe.wait_ge(rows_ready, b)
                    if n >= 4:
                        pe.wait_ge(copied, n - 3)
                    for t in range(a, b):
                        last = nc.tensor.transpose(tp[n % 4][:, (t - a) * NP:(t - a + 1) * NP],
                                                   XH[:, t, c * 128:(c + 1) * 128], self.ident[0:NP, 0:NP])
                    last.then_inc(turned, 1)

            @block.scalar
            def _(act):
                act.wait_ge(var_ready, 1)
                nc.scalar.activation(sd[:], rstd[:], ACT.Sqrt).then_inc(sd_ready, 1)
                for n, (a, b, c) in enumerate(groups):
                    act.wait_ge(turned, n + 1)
                    nc.scalar.copy(XT[:, c, a * NP:b * NP], tp[n % 4][:, 0:(b - a) * NP]).then_inc(copied, 1)


    def split_keys(self, own, keys, quotient, hi, lo):
        nc = self.nc
        assert all(k * DIV_MUL >> DIV_SHIFT == k // NT for k in range(NODES))
        own(nc.vector.tensor_scalar(quotient[:], keys[:], DIV_MUL, None, ALU.mult))
        own(nc.vector.tensor_scalar(quotient[:], quotient[:], DIV_SHIFT, None, ALU.arith_shift_right))
        own(nc.vector.tensor_scalar(hi[:], quotient[:], float(NT), None, ALU.mult))
        own(nc.vector.tensor_tensor(lo[:], keys[:], hi[:], ALU.subtract))

    def one_hots(self, own, parts, hi, lo, at, hot_hi, hot_lo):
        nc = self.nc
        own.fire(nc.vector.tensor_tensor(
            hot_hi[:], bc(hi[:, bass.ds(at, HALF)].unsqueeze(2), (parts, HALF, NP)),
            bc(self.hi_values[0:parts, :].unsqueeze(1), (parts, HALF, NP)), ALU.is_equal))
        own.fire(nc.vector.tensor_tensor(
            hot_lo[:], bc(lo[:, bass.ds(at, HALF)].unsqueeze(2), (parts, HALF, NT)),
            bc(self.lo_values[0:parts, :].unsqueeze(1), (parts, HALF, NT)), ALU.is_equal))

    def count_keys(self, name, keys_dram, parts, cols, count, end):
        nc = self.nc
        stack, r = self.stage(name)
        with stack:
            keys = r.sb("keys", [parts, cols], I32)
            quotient = r.sb("quotient", [parts, cols], I32)
            hi, lo = r.sb("hi", [parts, cols]), r.sb("lo", [parts, cols])
            hot_hi = [r.sb(f"hot_hi{h}", [parts, HALF, NP], BF16) for h in range(2)]
            hot_lo = [r.sb(f"hot_lo{h}", [parts, HALF, NT], BF16) for h in range(2)]
            zero, within = r.sb("zero", [NP, NT]), r.sb("within", [NP, NT])
            part = [r.ps(f"part{h}", [NP, NT]) for h in range(2)]
            before = r.ps("before", [NP, 1])
            own_dve, loaded = r.sem("own_dve"), r.sem("loaded")
            built, counted = r.sem("built"), r.sem("counted")
            totals_ready, before_ready = r.sem("totals_ready"), r.sem("before_ready")
            block = stack.enter_context(nc.Block())

            @block.sync
            def _(sp):
                sp.dma_start(keys[:], keys_dram.rearrange("(p c) -> p c", c=cols)).then_inc(loaded, 16)
                sp.wait_ge(loaded, 16)

            @block.vector
            def _(dve):
                own = InOrder(dve, own_dve)
                own.fire(nc.vector.memset(count[:], 0.0))
                own.fire(nc.vector.memset(zero[:], 0.0))
                dve.wait_ge(loaded, 16)
                self.split_keys(own, keys, quotient, hi, lo)
                with dve.Fori(0, cols // STEP) as i:
                    own.restart()
                    for h in range(2):
                        self.one_hots(own, parts, hi, lo, STEP * i + HALF * h, hot_hi[h], hot_lo[h])
                        own.join()
                        dve.sem_inc(built, 1)
                    for h in range(2):
                        dve.wait_ge(counted, 2 * i + h + 1)
                        own(nc.vector.tensor_tensor(count[:], count[:], part[h][:], ALU.add))
                own.restart()
                own(nc.vector.tensor_tensor_scan(within[:], zero[:], count[:], 0.0, ALU.add, ALU.add))
                dve.sem_inc(totals_ready, 1)
                dve.wait_ge(before_ready, 1)
                own(nc.vector.tensor_scalar(end[:], within[:], before[:, 0:1], None, ALU.add))

            @block.tensor
            def _(pe):
                with pe.Fori(0, cols // STEP) as i:
                    for h in range(2):
                        pe.wait_ge(built, 2 * i + h + 1)
                        for k in range(HALF):
                            last = nc.tensor.matmul(part[h][:], hot_hi[h][:, k, :], hot_lo[h][:, k, :],
                                                    start=(k == 0), stop=(k == HALF - 1))
                        last.then_inc(counted, 1)
                pe.wait_ge(totals_ready, 1)
                nc.tensor.matmul(before[:], self.upper[0:NP, 0:NP], within[:, NT - 1:NT],
                                 start=True, stop=True).then_inc(before_ready, 1)

    def sort_edges(self, name, keys_dram, others_dram, attr_dram, parts, cols, count, end, records):
        nc = self.nc
        row = ROW if attr_dram is not None else 2
        key_at, other_at = (KEY, OTHER) if attr_dram is not None else (0, 1)
        stack, r = self.stage(name)
        with stack:
            keys, others = r.sb("keys", [parts, cols], I32), r.sb("others", [parts, cols], I32)
            quotient = r.sb("quotient", [parts, cols], I32)
            hi, lo = r.sb("hi", [parts, cols]), r.sb("lo", [parts, cols])
            hot_hi = [r.sb(f"hot_hi{h}", [parts, HALF, NP], BF16) for h in range(2)]
            hot_lo = [r.sb(f"hot_lo{h}", [parts, HALF, NT], BF16) for h in range(2)]
            turned = r.sb("turned", [NP, HALF, parts])
            earlier = r.sb("earlier", [parts, HALF, parts], BF16)
            running = r.sb("running", [NP, HALF + 1, NT])
            picked = r.sb("picked", [parts, HALF, NT])
            placef = r.sb("placef", [parts, HALF])
            place = [r.sb(f"place{h}", [parts, HALF], I32) for h in range(2)]
            record = [r.sb(f"record{h}", [parts, HALF, row]) for h in range(2)]
            turned_ps = [r.ps(f"turned_ps{h}", [NP, HALF, 128], BF16) for h in range(2)]
            here_ps = [r.ps(f"here_ps{h}", [NP, HALF, NT]) for h in range(2)]
            same_ps = r.ps("same_ps", [parts, 2, 512])
            rank_ps = r.ps("rank_ps", [parts, HALF, NT])
            own_dve, own_act = r.sem("own_dve"), r.sem("own_act")
            loaded, built, turned_out, turned_in = (r.sem(n) for n in ("loaded", "built", "turned_out", "turned_in"))
            same_ready, earlier_ready, ranked = (r.sem(n) for n in ("same_ready", "earlier_ready", "ranked"))
            placed, filled, constants = r.sem("placed"), r.sem("filled"), r.sem("constants")
            started = r.sem("started")
            scattered = [self.moved_sem(f"{name}_scattered{h}") for h in range(2)]
            attr_in = [r.sem(f"attr_in{h}") for h in range(2)]
            rec_i = [record[h][:].bitcast(I32) for h in range(2)]
            turns = cols // STEP
            block = stack.enter_context(nc.Block())

            @block.sync
            def _(sp):
                sp.dma_start(keys[:], keys_dram.rearrange("(p c) -> p c", c=cols)).then_inc(loaded, 16)
                sp.dma_start(others[:], others_dram.rearrange("(p c) -> p c", c=cols)).then_inc(loaded, 16)
                if attr_dram is not None:
                    attr = attr_dram.rearrange("(p c) w -> p c w", c=cols)
                    sp.wait_ge(constants, 1)

                    def turn(i, first, last):
                        for h in range(2):
                            if not first:
                                sp.wait_ge(scattered[h], 16 * HALF * i)
                            sp.dma_start(record[h][:, :, 0:ATTR],
                                         attr[:, bass.ds(STEP * i + HALF * h, HALF), :]).then_inc(attr_in[h], 16)

                    loop(sp, turns, turn)

            @block.vector
            def _(dve):
                own = InOrder(dve, own_dve)
                if attr_dram is not None:
                    for h in range(2):
                        own.fire(nc.vector.memset(record[h][:], 0.0))
                    own.join()
                    for h in range(2):
                        own.fire(nc.vector.memset(record[h][:, :, ATTR:ATTR + 1], 1.0))
                    own.join()
                dve.sem_inc(constants, 1)
                dve.wait_ge(loaded, 32)
                self.split_keys(own, keys, quotient, hi, lo)
                own(nc.vector.tensor_tensor(running[:, HALF, :], end[:], count[:], ALU.subtract))

                def turn(i, first, last):
                    own.restart()
                    for h in range(2):
                        self.one_hots(own, parts, hi, lo, STEP * i + HALF * h, hot_hi[h], hot_lo[h])
                        own.join()
                        dve.sem_inc(built, 1)
                    for h in range(2):
                        dve.wait_ge(turned_out, 2 * i + h + 1)
                        own(nc.vector.tensor_copy(running[:, 0, :], running[:, HALF, :]))
                        for k in range(HALF):
                            own(nc.vector.tensor_tensor(running[:, k + 1, :], running[:, k, :],
                                                        here_ps[h][:, k, :], ALU.add))
                        dve.wait_ge(same_ready, 2 * i + h + 1)
                        for b in range(2):
                            own.fire(nc.vector.tensor_tensor(
                                earlier[:, 4 * b:4 * b + 4, :],
                                same_ps[:, b, 0:4 * parts].rearrange("q (k p) -> q k p", p=parts),
                                bc(self.upper[0:parts, 0:parts].unsqueeze(1), (parts, 4, parts)), ALU.mult))
                        own.join()
                        dve.sem_inc(earlier_ready, 1)
                        dve.wait_ge(ranked, 2 * i + h + 1)
                        own(nc.vector.tensor_tensor(picked[:], rank_ps[:], hot_lo[h][:], ALU.mult))
                        own(nc.vector.tensor_reduce(placef[:], picked[:], AX.X, ALU.add))
                        if not first:
                            dve.wait_ge(scattered[h], 16 * HALF * i)
                        own(nc.vector.tensor_copy(place[h][:], placef[:]))
                        dve.sem_inc(placed, 1)

                loop(dve, turns, turn)

            @block.tensor
            def _(pe):
                with pe.Fori(0, turns) as i:
                    for h in range(2):
                        pe.wait_ge(built, 2 * i + h + 1)
                        for k in range(HALF):
                            nc.tensor.transpose(turned_ps[h][:, k, 0:parts], hot_hi[h][:, k, :],
                                                self.identb[0:parts, 0:parts])
                        for k in range(HALF):
                            last = nc.tensor.matmul(here_ps[h][:, k, :], hot_hi[h][:, k, :], hot_lo[h][:, k, :],
                                                    start=True, stop=True)
                        last.then_inc(turned_out, 1)
                    for h in range(2):
                        pe.wait_ge(turned_in, 2 * i + h + 1)
                        for k in range(HALF):
                            last = nc.tensor.matmul(same_ps[:, k // 4, (k % 4) * parts:(k % 4 + 1) * parts],
                                                    turned[:, k, :], turned[:, k, :], start=True, stop=True)
                        last.then_inc(same_ready, 1)
                        pe.wait_ge(earlier_ready, 2 * i + h + 1)
                        for k in range(HALF):
                            nc.tensor.matmul(rank_ps[:, k, :], turned[:, k, :], running[:, k, :],
                                             start=True, stop=False)
                            last = nc.tensor.matmul(rank_ps[:, k, :], earlier[:, k, :], hot_lo[h][:, k, :],
                                                    start=False, stop=True)
                        last.then_inc(ranked, 1)

            @block.scalar
            def _(act):
                own = InOrder(act, own_act)
                act.wait_ge(constants, 1)
                act.wait_ge(loaded, 32)

                def turn(i, first, last):
                    own.restart()
                    for h in range(2):
                        act.wait_ge(turned_out, 2 * i + h + 1)
                        if h == 1:
                            act.wait_ge(ranked, 2 * i + 1)
                        own(nc.scalar.copy(turned[:], turned_ps[h][:, :, 0:parts]))
                        act.sem_inc(turned_in, 1)
                        if not first:
                            act.wait_ge(scattered[h], 16 * HALF * i)
                        own.fire(nc.scalar.copy(rec_i[h][:, :, key_at], keys[:, bass.ds(STEP * i + HALF * h, HALF)]))
                        own(nc.scalar.copy(rec_i[h][:, :, other_at], others[:, bass.ds(STEP * i + HALF * h, HALF)]))
                        act.sem_inc(filled, 1)
                    act.wait_ge(ranked, 2 * i + 2)

                loop(act, turns, turn)

            @block.gpsimd
            def _(pool):
                with pool.Fori(0, turns) as i:
                    for h in range(2):
                        if attr_dram is not None:
                            pool.wait_ge(attr_in[h], 16 * i + 16)
                        pool.wait_ge(filled, 2 * i + h + 1)
                        pool.wait_ge(placed, 2 * i + h + 1)
                        pool.sem_inc(started, 1)
                        for k in range(HALF):
                            pool.indirect_dma_start(
                                records, bass.IndirectOffsetOnAxis(ap=place[h][:, k:k + 1], axis=0),
                                record[h][:, k, :], None).then_inc(scattered[h], 16)
                for h in range(2):
                    pool.wait_ge(scattered[h], 16 * HALF * turns)

    def describe_edges(self, e, first_dram, last_dram, count, end):
        nc, parts = self.nc, e.parts
        stack, r = self.stage(f"describe_{e.name}")
        with stack, nc.allow_non_contiguous_dma(reason="one word from each partition's range of edges"):
            ends = r.sb("ends", [parts, 3], I32)
            endf = r.sb("endf", [parts, 3])
            ones, diag = r.sb("ones", [parts, parts]), r.sb("diag", [parts, 2, parts])
            runs_on, last_edge = r.sb("runs_on", [parts, 2]), r.sb("last_edge", [NP, NT])
            rows = r.ps("rows", [parts, 2, parts])
            own_dve, blank, loaded, diag_ready, rows_ready = (
                r.sem(n) for n in ("own_dve", "blank", "loaded", "diag_ready", "rows_ready"))
            block = stack.enter_context(nc.Block())

            @block.sync
            def _(sp):
                sp.wait_ge(blank, 1)
                sp.dma_start(ends[:, 0:1], first_dram).then_inc(loaded, 16)
                sp.dma_start(ends[:, 1:2], last_dram).then_inc(loaded, 16)
                sp.dma_start(ends[0:parts - 1, 2:3], first_dram[1:parts, :]).then_inc(loaded, 16)
                sp.wait_ge(loaded, 48)

            @block.vector
            def _(dve):
                own = InOrder(dve, own_dve)
                own.fire(nc.vector.memset(ones[:], 1.0))
                own(nc.vector.memset(ends[:], -1))
                dve.sem_inc(blank, 1)
                dve.wait_ge(loaded, 48)
                own(nc.vector.tensor_copy(endf[:], ends[:]))
                own.fire(nc.vector.tensor_copy(e.first[:], endf[:, 0:1]))
                own.fire(nc.vector.tensor_copy(e.last[:], endf[:, 1:2]))
                for k in range(2):
                    own.fire(nc.vector.tensor_scalar(diag[:, k, :], self.ident[0:parts, 0:parts],
                                                     endf[:, k:k + 1], None, ALU.mult))
                own.fire(nc.vector.tensor_tensor(runs_on[:, 0:1], endf[:, 1:2], endf[:, 0:1], ALU.is_equal))
                own(nc.vector.tensor_tensor(runs_on[:, 1:2], endf[:, 2:3], endf[:, 1:2], ALU.is_equal))
                dve.sem_inc(diag_ready, 1)
                own(nc.vector.tensor_tensor(e.closes[:], runs_on[:, 0:1], runs_on[:, 1:2], ALU.mult))
                own(nc.vector.tensor_scalar(e.closes[:], e.closes[:], -1.0, 1.0, ALU.mult, ALU.add))
                dve.wait_ge(rows_ready, 1)
                own.fire(nc.vector.scalar_tensor_tensor(
                    out=e.after[:], in0=rows[:, 0, :], scalar=e.last[:, 0:1], in1=self.upper[0:parts, 0:parts],
                    op0=ALU.is_equal, op1=ALU.mult))
                own.fire(nc.vector.scalar_tensor_tensor(
                    out=e.before[:], in0=rows[:, 1, :], scalar=e.first[:, 0:1], in1=self.lower[0:parts, 0:parts],
                    op0=ALU.is_equal, op1=ALU.mult))
                own.fire(nc.vector.tensor_scalar_min(e.has[:], count[:], 1.0))
                own(nc.vector.tensor_scalar(last_edge[:], end[:], 1.0, 0.0, ALU.subtract, ALU.max))
                own(nc.vector.tensor_copy(e.end[:], last_edge[:]))

            @block.tensor
            def _(pe):
                pe.wait_ge(diag_ready, 1)
                nc.tensor.matmul(rows[:], ones[:], diag[:], start=True, stop=True).then_inc(rows_ready, 1)

    def out_degree_scale(self, count):
        nc = self.nc
        stack, r = self.stage("outdeg")
        with stack:
            deg = r.sb("deg", [NP, NT])
            own_dve, deg_ready, root_ready = r.sem("own_dve"), r.sem("deg_ready"), r.sem("root_ready")
            block = stack.enter_context(nc.Block())

            @block.vector
            def _(dve):
                own = InOrder(dve, own_dve)
                own(nc.vector.tensor_scalar_max(deg[:], count[:], 1.0))
                dve.sem_inc(deg_ready, 1)
                dve.wait_ge(root_ready, 1)
                own(nc.vector.reciprocal(self.isout[:], self.isout[:]))

            @block.scalar
            def _(act):
                act.wait_ge(deg_ready, 1)
                nc.scalar.activation(self.isout[:], deg[:], ACT.Sqrt).then_inc(root_ready, 1)

    def prepare_edges(self, room):
        nc, A = self.nc, self.A
        edges, gate_edges = A["src"].shape[0], A["L1_ffn_edge_index"].shape[1]
        self.by_dst = Edges(room, "by_dst", NP, edges // NP)
        self.by_src = Edges(room, "by_src", NP, edges // NP)
        self.by_gate = Edges(room, "by_gate", 128, gate_edges // 128)
        self.src_records = nc.dram_tensor("src_records", [edges, ROW], F32, kind="Internal").ap()
        self.gate_records = nc.dram_tensor("gate_records", [gate_edges, 2], F32, kind="Internal").ap()
        self.states = {}
        stack, r = self.stage("prep")
        with stack:
            cols = edges // NP
            gate_cols = gate_edges // 128
            gate_src, gate_dst = A["L1_ffn_edge_index"][0], A["L1_ffn_edge_index"][1]
            tiles = [(r.sb(f"count{k}", [NP, NT]), r.sb(f"end{k}", [NP, NT])) for k in range(3)]
            self.count_keys("count_dst", A["dst"], NP, cols, *tiles[0])
            view = A["dst"].rearrange("(p c) -> p c", c=cols)
            self.describe_edges(self.by_dst, view[:, 0:1], view[:, cols - 1:cols], *tiles[0])
            self.count_keys("count_src", A["src"], NP, cols, *tiles[1])
            self.out_degree_scale(tiles[1][0])
            self.sort_edges("sort_src", A["src"], A["dst"], A["edge_attr_18"], NP, cols, *tiles[1], self.src_records)
            view = self.src_records.bitcast(I32).rearrange("(p c) w -> p c w", c=cols)
            self.describe_edges(self.by_src, view[:, 0, KEY:KEY + 1], view[:, cols - 1, KEY:KEY + 1], *tiles[1])
            self.count_keys("count_gate", gate_dst, 128, gate_cols, *tiles[2])
            self.sort_edges("sort_gate", gate_dst, gate_src, None, 128, gate_cols, *tiles[2], self.gate_records)
            view = self.gate_records.bitcast(I32).rearrange("(p c) w -> p c w", c=gate_cols)
            self.describe_edges(self.by_gate, view[:, 0, 0:1], view[:, gate_cols - 1, 0:1], *tiles[2])

    def load_weight(self, sp, sem, dst, dram):
        sp.dma_start(dst, dram.rearrange("(c k) n -> k c n", k=128)).then_inc(sem, 16)

    def project(self, name, jobs, tables=()):
        nc = self.nc
        stack, r = self.stage(name)
        with stack:
            ps = [r.ps(f"ps{k}", [NP, 512]) for k in range(6)]
            done, stored = r.sem("done"), r.sem("stored")
            by_dve, by_act = r.sem("by_dve"), r.sem("by_act")
            plan, counts = [], {True: 0, False: 0}
            for t in range(NT):
                for w, b, out, view in jobs:
                    on_dve = b is not None
                    counts[on_dve] += 1
                    plan.append((t, w, b, out, view, on_dve, counts[on_dve]))
            block = stack.enter_context(nc.Block())

            @block.tensor
            def _(pe):
                for n, (t, w, _, _, _, _, _) in enumerate(plan):
                    if n >= 6:
                        pe.wait_ge(by_dve if plan[n - 6][5] else by_act, plan[n - 6][6])
                    parts = [(xt[:, c, t * NP:(t + 1) * NP], wt[:, c, :]) for xt, wt in w for c in range(KC)]
                    for k, (lhsT, rhs) in enumerate(parts):
                        last = nc.tensor.matmul(ps[n % 6][:, 0:rhs.shape[1]], lhsT, rhs,
                                                start=(k == 0), stop=(k == len(parts) - 1))
                    last.then_inc(done, 1)

            @block.vector
            def _(dve):
                for n, (t, w, b, out, view, on_dve, _) in enumerate(plan):
                    if on_dve:
                        dve.wait_ge(done, n + 1)
                        nc.vector.tensor_tensor(out(t), view(ps[n % 6][:, 0:w[0][1].shape[2]]), view(b),
                                                ALU.add).then_inc(by_dve, 1)

            @block.scalar
            def _(act):
                for n, (t, w, b, out, view, on_dve, _) in enumerate(plan):
                    if not on_dve:
                        act.wait_ge(done, n + 1)
                        nc.scalar.copy(out(t), view(ps[n % 6][:, 0:w[0][1].shape[2]])).then_inc(by_act, 1)

            @block.sync
            def _(sp):
                if counts[True]:
                    sp.wait_ge(by_dve, counts[True])
                if counts[False]:
                    sp.wait_ge(by_act, counts[False])
                for dram, tab in tables:
                    sp.dma_start(dram.rearrange("(p t) w -> p t w", t=NT), tab[:]).then_inc(stored, 16)
                if tables:
                    sp.wait_ge(stored, 16 * len(tables))

    def table(self, name, width):
        return self.nc.dram_tensor(name, [NODES, width], F32, kind="Internal").ap()

    def stream(self, name, e, heads, values, other_table, key_table, last_state, kind, extra=None):
        nc, A, parts, cols = self.nc, self.A, e.parts, e.cols
        width, other_w = values + heads, other_table.shape[1]
        key_w = key_table.shape[1] if key_table is not None else 0
        each = values // heads if heads else values
        self.states[name] = states = nc.dram_tensor(f"{name}_states", [parts * cols, width], F32, kind="Internal").ap()
        states_v = states.rearrange("(p c) w -> p c w", c=cols)
        turns = cols // STEP
        stack, r = self.stage(name)
        with stack:
            two = range(2)
            if e is self.by_dst:
                picks = [r.sb(f"picks{h}", [parts, 3, HALF], I32) for h in two]
                sources = [A["dst"], A["src"]] + ([A["edge_type_64"]] if kind == "relation" else [])
                sources = [s.rearrange("(p c) -> p c", c=cols) for s in sources]
                key_of = [picks[h][:, 0, :] for h in two]
                key_index = [lambda k, h=h: picks[h][:, 0, k:k + 1] for h in two]
                other_index = [lambda k, h=h: picks[h][:, 1, k:k + 1] for h in two]
                type_of = [picks[h][:, 2, :] for h in two]
                loads = [lambda at, h, n=n: (picks[h][:, n, :], sources[n][:, bass.ds(at, HALF)])
                         for n in range(len(sources))]
            else:
                dram, row = (self.src_records, ROW) if e is self.by_src else (self.gate_records, 2)
                key_at, other_at = (KEY, OTHER) if e is self.by_src else (0, 1)
                record = [r.sb(f"record{h}", [parts, HALF, row]) for h in two]
                records_v = dram.rearrange("(p c) w -> p c w", c=cols)
                key_of = [record[h][:].bitcast(I32)[:, :, key_at] for h in two]
                key_index = [lambda k, h=h: record[h][:].bitcast(I32)[:, k, key_at:key_at + 1] for h in two]
                other_index = [lambda k, h=h: record[h][:].bitcast(I32)[:, k, other_at:other_at + 1] for h in two]
                loads = [lambda at, h: (record[h][:], records_v[:, bass.ds(at, HALF), :])]
            other = [r.sb(f"other{h}", [parts, HALF, other_w]) for h in two]
            keyrow = [r.sb(f"keyrow{h}", [parts, HALF, key_w]) for h in two] if key_w else None
            state = [r.sb(f"state{h}", [parts, HALF, width]) for h in two]
            keyf = [r.sb(f"keyf{h}", [parts, HALF + 1]) for h in two]
            same, fresh = r.sb("same", [parts, HALF]), r.sb("fresh", [parts, HALF])
            if heads:
                score = r.sb("score", [parts, HALF, heads])
                grown = r.sb("grown", [parts, 2, HALF, heads])
                factor = r.sb("factor", [parts, 2, HALF, heads])
                scaled = r.sb("scaled", [parts, values])
            if kind == "relation":
                product = r.sb("product", [parts, HALF * heads, 128])
                typef, hot = r.sb("typef", [parts, HALF]), r.sb("hot", [parts, HALF, 64])
            if kind == "attributes":
                product = r.sb("product", [parts, HALF, 128])
                query = r.sb("query", [parts, HALF, 128])
                attr_ps = r.ps("attr_ps", [128, 2, 128])
                attr_t = [r.sb(f"attr_t{h}", [128, 2, 128]) for h in two]
                rpe_ps = r.ps("rpe_ps", [parts, 4, 2, 256])
                turned, turned_in, rpe_ready, rpe_used = (
                    r.sem(n) for n in ("turned", "turned_in", "rpe_ready", "rpe_used"))
            own_dve, started, picked_up = r.sem("own_dve"), r.sem("started"), [r.sem(f"picked_up{h}") for h in two]
            picks_in = [r.sem(f"picks_in{h}") for h in two]
            gathered = [self.moved_sem(f"{name}_gathered{h}") for h in two]
            rows_used = [r.sem(f"rows_used{h}") for h in two]
            args_ready, factors_ready = r.sem("args_ready"), r.sem("factors_ready")
            state_ready = [r.sem(f"state_ready{h}") for h in two]
            stored = [r.sem(f"stored{h}") for h in two]
            tables = 1 + (key_w > 0)
            block = stack.enter_context(nc.Block())

            @block.gpsimd
            def _(pool):
                def turn(i, first, last):
                    for h in two:
                        pool.wait_ge(picks_in[h], 16 * len(loads) * (i + 1))
                        if not first:
                            pool.wait_ge(rows_used[h], i)
                        pool.sem_inc(started, 1)
                        for k in range(HALF):
                            pool.indirect_dma_start(
                                other[h][:, k, :], None, other_table,
                                bass.IndirectOffsetOnAxis(ap=other_index[h](k), axis=0)).then_inc(gathered[h], 16)
                            if key_w:
                                pool.indirect_dma_start(
                                    keyrow[h][:, k, :], None, key_table,
                                    bass.IndirectOffsetOnAxis(ap=key_index[h](k), axis=0)).then_inc(gathered[h], 16)
                loop(pool, turns, turn)

            @block.scalar
            def _(act):
                def load(i, h):
                    for f in loads:
                        to, of = f(STEP * i + HALF * h, h)
                        act.dma_start(to, of).then_inc(picks_in[h], 16)

                for h in two:
                    load(0, h)

                def turn(i, first, last):
                    for h in two:
                        if kind == "attributes":
                            act.wait_ge(turned, 2 * i + h + 1)
                            nc.scalar.copy(attr_t[h][:, :, 0:parts], attr_ps[:, :, 0:parts]).then_inc(turned_in, 1)
                        if not last:
                            act.wait_ge(picked_up[h], i + 1)
                            load(i + 1, h)
                        if heads:
                            act.wait_ge(args_ready, 2 * i + h + 1)
                            nc.scalar.activation(factor[:], grown[:], ACT.Exp).then_inc(factors_ready, 1)
                loop(act, turns, turn)

            @block.sync
            def _(sp):
                def turn(i, first, last):
                    for h in two:
                        sp.wait_ge(state_ready[h], i + 1)
                        sp.dma_start(states_v[:, bass.ds(STEP * i + HALF * h, HALF), :], state[h][:])\
                          .then_inc(stored[h], 16)
                loop(sp, turns, turn)
                for h in two:
                    sp.wait_ge(stored[h], 16 * turns)

            @block.vector
            def _(dve):
                own = InOrder(dve, own_dve)
                tt, ts, stt = nc.vector.tensor_tensor, nc.vector.tensor_scalar, nc.vector.scalar_tensor_tensor
                own.fire(nc.vector.memset(keyf[1][:, HALF:HALF + 1], -1.0))
                own(nc.vector.memset(state[1][:, HALF - 1, :], 0.0))

                def relation_scores(h):
                    own(nc.vector.tensor_copy(typef[:], type_of[h]))
                    own.fire(tt(hot[:], bc(typef[:].unsqueeze(2), (parts, HALF, 64)),
                                bc(self.small[0:parts, :].unsqueeze(1), (parts, HALF, 64)), ALU.is_equal))
                    keys = keyrow[h][:].rearrange("p k (h w) -> p k h w", w=128)
                    own(tt(product[:].rearrange("p (k h) w -> p k h w", h=heads)[:, :, :, 0:64],
                           keys[:, :, :, 0:64],
                           other[h][:, :, values:values + 64 * heads].rearrange("p k (h d) -> p k h d", d=64), ALU.mult))
                    for k in range(HALF):
                        own.fire(tt(product[:, heads * k:heads * (k + 1), 64:128], keys[:, k, :, 64:128],
                                    bc(hot[:, k, :].unsqueeze(1), (parts, heads, 64)), ALU.mult))
                    own.join()
                    own(nc.vector.tensor_reduce(score[:].rearrange("p k h -> p (k h)"), product[:], AX.X, ALU.add))

                def attribute_scores(i, h):
                    dve.wait_ge(rpe_ready, 4 * (2 * i + h + 1))
                    rpe = rpe_ps[:].rearrange("p q a w -> p a q w")

                    def by_four(ap):
                        return ap.rearrange("p (a q) w -> p a q w", q=4)

                    own.fire(tt(by_four(query[:]), by_four(keyrow[h][:]), rpe[:, :, :, 0:128], ALU.add))
                    own(tt(by_four(product[:]), by_four(other[h][:, :, values:values + 128]),
                           rpe[:, :, :, 128:256], ALU.add))
                    dve.sem_inc(rpe_used, 1)
                    own(tt(product[:], product[:], query[:], ALU.mult))
                    own(nc.vector.tensor_reduce(score[:].rearrange("p k h -> p (k h)"),
                                                product[:].rearrange("p k (h d) -> p (k h) d", d=8), AX.X, ALU.add))

                def additive_scores(h):
                    own(tt(score[:], other[h][:, :, values:values + heads], keyrow[h][:], ALU.add))
                    own(stt(out=score[:], in0=score[:], scalar=0.2, in1=score[:], op0=ALU.mult, op1=ALU.max))

                def turn(i, first, last):
                    own.restart()
                    for h in two:
                        now, before = state[h], state[1 - h]
                        dve.wait_ge(gathered[h], 16 * HALF * tables * (i + 1))
                        own.fire(nc.vector.tensor_copy(keyf[h][:, 0:1], keyf[1 - h][:, HALF:HALF + 1]))
                        own(nc.vector.tensor_copy(keyf[h][:, 1:HALF + 1], key_of[h]))
                        own(tt(same[:], keyf[h][:, 1:HALF + 1], keyf[h][:, 0:HALF], ALU.is_equal))
                        if heads:
                            own.fire(ts(fresh[:], same[:], BIG, -BIG, ALU.mult, ALU.add))
                        if kind == "relation":
                            relation_scores(h)
                        elif kind == "attributes":
                            attribute_scores(i, h)
                        elif kind == "additive":
                            additive_scores(h)
                        own.join()
                        dve.sem_inc(picked_up[h], 1)
                        if not first:
                            dve.wait_ge(stored[h], 16 * i)
                        if heads:
                            top = now[:, :, values:width]
                            for k in range(HALF):
                                prev = before[:, HALF - 1, values:width] if k == 0 else top[:, k - 1, :]
                                own(stt(out=top[:, k, :], in0=prev, scalar=fresh[:, k:k + 1], in1=score[:, k, :],
                                        op0=ALU.add, op1=ALU.max))
                            own.fire(stt(out=grown[:, 0, 0, :], in0=before[:, HALF - 1, values:width],
                                         scalar=fresh[:, 0:1], in1=top[:, 0, :], op0=ALU.add, op1=ALU.subtract))
                            own.fire(tt(grown[:, 0, 1:HALF, :], top[:, 0:HALF - 1, :],
                                        bc(fresh[:, 1:HALF].unsqueeze(2), (parts, HALF - 1, heads)), ALU.add))
                            own.fire(tt(grown[:, 1, :, :], score[:], top, ALU.subtract))
                            own.join()
                            own(tt(grown[:, 0, 1:HALF, :], grown[:, 0, 1:HALF, :], top[:, 1:HALF, :], ALU.subtract))
                            dve.sem_inc(args_ready, 1)
                            dve.wait_ge(factors_ready, 2 * i + h + 1)
                            own(tt(now[:, :, 0:values].rearrange("p k (h d) -> p k h d", d=each),
                                   other[h][:, :, 0:values].rearrange("p k (h d) -> p k h d", d=each),
                                   bc(factor[:, 1, :, :].unsqueeze(3), (parts, HALF, heads, each)), ALU.mult))
                            dve.sem_inc(rows_used[h], 1)
                            for k in range(HALF):
                                prev = before[:, HALF - 1, 0:values] if k == 0 else now[:, k - 1, 0:values]
                                own(tt(scaled[:].rearrange("p (h d) -> p h d", d=each),
                                       prev.rearrange("p (h d) -> p h d", d=each),
                                       bc(factor[:, 0, k, :].unsqueeze(2), (parts, heads, each)), ALU.mult))
                                own(tt(now[:, k, 0:values], now[:, k, 0:values], scaled[:], ALU.add))
                        else:
                            for k in range(HALF):
                                prev = before[:, HALF - 1, :] if k == 0 else now[:, k - 1, :]
                                own(stt(out=now[:, k, :], in0=prev, scalar=same[:, k:k + 1], in1=other[h][:, k, :],
                                        op0=ALU.mult, op1=ALU.add))
                            dve.sem_inc(rows_used[h], 1)
                        dve.sem_inc(state_ready[h], 1)
                loop(dve, turns, turn)
                own.restart()
                own(nc.vector.tensor_copy(last_state[:], state[1][:, HALF - 1, :]))

            if kind == "attributes":
                @block.tensor
                def _(pe):
                    def turn(i, first, last):
                        for h in two:
                            pe.wait_ge(picks_in[h], 16 * len(loads) * (i + 1))
                            if not (first and h == 0):
                                pe.wait_ge(turned_in, 2 * i + h)
                            for b in two:
                                flat = record[h][:].rearrange("p k w -> p (k w)")[:, 128 * b:128 * b + 128]
                                last_ = nc.tensor.transpose(attr_ps[:, b, 0:parts], flat, self.ident[0:parts, 0:parts])
                            last_.then_inc(turned, 1)
                            pe.wait_ge(turned_in, 2 * i + h + 1)
                            if not (first and h == 0):
                                pe.wait_ge(rpe_used, 2 * i + h)
                            for k in range(HALF):
                                q = 32 * (k % 4)
                                last_ = nc.tensor.matmul(rpe_ps[:, k % 4, k // 4, :], attr_t[h][q:q + ATTR + 1, k // 4, 0:parts],
                                                         extra[q:q + ATTR + 1, :], start=True, stop=True)
                                if k >= HALF - 4:
                                    last_.then_inc(rpe_ready, 1)
                    loop(pe, turns, turn)

    def merge(self, name, e, heads, values, last_state, nodes, own_rows=None, own_score=None):
        nc, parts = self.nc, e.parts
        width = values + heads
        each = values // heads if heads else values
        stack, r = self.stage(f"{name}_merge")
        with stack:
            carried = r.sb("carried", [NP, NT, width + 1])
            number = r.sb("number", [parts, NT, NP])
            takes = r.sb("takes", [parts, NT, NP])
            carry = r.sb("carry", [parts, width + 1])
            ones = r.sb("ones", [parts, parts])
            spread = r.ps("spread", [parts, 4, 512])
            carry_ps = r.ps("carry_ps", [parts, values])
            node_ps = [r.ps(f"node_ps{k}", [NP, width + 1]) for k in range(2)]
            if heads:
                diag = r.sb("diag", [parts, heads, parts])
                shut = r.sb("shut", [parts, 2, parts])
                arg, weight = r.sb("arg", [parts, heads, parts]), r.sb("weight", [parts, heads, parts])
                top = r.sb("top", [parts, heads])
                sources = 3 if own_rows is not None else 2
                tops = r.sb("tops", [NP, sources, NT, heads])
                best = r.sb("best", [NP, NT, heads])
                shares = r.sb("shares", [NP, sources, NT, heads])
                absent = r.sb("absent", [NP, 2, NT])
            sems = ("own_dve", "numbered", "diag_ready", "spread_ready", "arg_ready", "weight_ready",
                    "carry_ready", "carry_out", "node_out", "node_in", "tops_ready", "shares_ready")
            s = {n: r.sem(n) for n in sems}
            s["gathered"] = self.moved_sem(f"{name}_gathered_ends")
            groups = [(a, min(a + 4, heads)) for a in range(0, heads, 4)]
            block = stack.enter_context(nc.Block())

            @block.gpsimd
            def _(pool):
                pool.iota(number[:], [[1, NT], [NT, NP]], base=0, channel_multiplier=0,
                          allow_small_or_imprecise_dtypes=True).then_inc(s["numbered"], 1)
                for t in range(NT):
                    pool.indirect_dma_start(nodes[:, t, :], None, self.states[name],
                                            bass.IndirectOffsetOnAxis(ap=e.end[:, t:t + 1], axis=0))\
                        .then_inc(s["gathered"], 16)

            @block.vector
            def _(dve):
                own = InOrder(dve, s["own_dve"])
                tt, ts, stt = nc.vector.tensor_tensor, nc.vector.tensor_scalar, nc.vector.scalar_tensor_tensor
                own.fire(nc.vector.memset(ones[:], 1.0))
                own.fire(nc.vector.memset(carry[:], 1.0))
                if heads:
                    m_last = last_state[:, values:width]
                    eye = bc(self.ident[0:parts, 0:parts].unsqueeze(1), (parts, heads, parts))
                    own(tt(diag[:], eye, bc(m_last.unsqueeze(2), (parts, heads, parts)), ALU.mult))
                    dve.sem_inc(s["diag_ready"], 1)
                    own.fire(ts(shut[:, 0, :], e.before[:], BIG, -BIG, ALU.mult, ALU.add))
                    own(ts(shut[:, 1, :], e.after[:], 2 * BIG, -2 * BIG, ALU.mult, ALU.add))
                    dve.wait_ge(s["spread_ready"], 1)
                    for n, (a, b) in enumerate(groups):
                        own.fire(tt(arg[:, a:b, :], spread[:, n, 0:(b - a) * parts].rearrange("p (h q) -> p h q", q=parts),
                                    bc(shut[:, 0, :].unsqueeze(1), (parts, b - a, parts)), ALU.add))
                    own.join()
                    own(nc.vector.tensor_reduce(top[:], arg[:], AX.X, ALU.max))
                    own(tt(diag[:], eye, bc(top[:].unsqueeze(2), (parts, heads, parts)), ALU.mult))
                    dve.sem_inc(s["diag_ready"], 1)
                    dve.wait_ge(s["spread_ready"], 2)
                    for n, (a, b) in enumerate(groups):
                        own.fire(stt(out=arg[:, a:b, :],
                                     in0=spread[:, n, 0:(b - a) * parts].rearrange("p (h q) -> p h q", q=parts),
                                     scalar=-1.0, in1=bc(shut[:, 1, :].unsqueeze(1), (parts, b - a, parts)),
                                     op0=ALU.mult, op1=ALU.add))
                    own.join()
                    own(tt(arg[:], arg[:], bc(m_last.unsqueeze(2), (parts, heads, parts)), ALU.add))
                    dve.sem_inc(s["arg_ready"], 1)
                dve.wait_ge(s["carry_out"], 1)
                own.join()
                own.fire(nc.vector.tensor_copy(carry[:, 0:values], carry_ps[:]))
                if heads:
                    own.fire(nc.vector.tensor_copy(carry[:, values:width], top[:]))
                dve.wait_ge(s["numbered"], 1)
                own.fire(ts(takes[:], number[:], e.first[:, 0:1], e.closes[:, 0:1], ALU.is_equal, ALU.mult))
                own.join()
                dve.sem_inc(s["carry_ready"], 1)
                dve.wait_ge(s["gathered"], 16 * NT)
                dve.wait_ge(s["node_in"], NT)
                if heads:
                    own.fire(ts(absent[:, 0, :], e.has[:], BIG, -BIG, ALU.mult, ALU.add))
                    own(ts(absent[:, 1, :], carried[:, :, width], BIG, -BIG, ALU.mult, ALU.add))
                    own.fire(tt(tops[:, 0, :, :], nodes[:, :, values:width],
                                bc(absent[:, 0, :].unsqueeze(2), (NP, NT, heads)), ALU.add))
                    own.fire(tt(tops[:, 1, :, :], carried[:, :, values:width],
                                bc(absent[:, 1, :].unsqueeze(2), (NP, NT, heads)), ALU.add))
                    if own_rows is not None:
                        own.fire(nc.vector.tensor_copy(tops[:, 2, :, :], own_score[:]))
                    own.join()
                    own(tt(best[:], tops[:, 0, :, :], tops[:, 1, :, :], ALU.max))
                    if own_rows is not None:
                        own(tt(best[:], best[:], tops[:, 2, :, :], ALU.max))
                    for k in range(sources):
                        own.fire(tt(tops[:, k, :, :], tops[:, k, :, :], best[:], ALU.subtract))
                    own.join()
                    dve.sem_inc(s["tops_ready"], 1)
                    dve.wait_ge(s["shares_ready"], 1)

                    def heads_of(ap):
                        return ap.rearrange("p t (h d) -> p t h d", d=each)

                    def share(k):
                        return bc(shares[:, k, :, :].unsqueeze(3), (NP, NT, heads, each))

                    mine, theirs = heads_of(nodes[:, :, 0:values]), heads_of(carried[:, :, 0:values])
                    own.fire(tt(mine, mine, share(0), ALU.mult))
                    own(tt(theirs, theirs, share(1), ALU.mult))
                    own(tt(mine, mine, theirs, ALU.add))
                    if own_rows is not None:
                        own(tt(theirs, heads_of(own_rows), share(2), ALU.mult))
                        own(tt(mine, mine, theirs, ALU.add))
                else:
                    own(tt(nodes[:], nodes[:], bc(e.has[:].unsqueeze(2), (NP, NT, values)), ALU.mult))
                    own(tt(nodes[:], nodes[:], carried[:, :, 0:values], ALU.add))

            @block.tensor
            def _(pe):
                if heads:
                    for n in range(2):
                        pe.wait_ge(s["diag_ready"], n + 1)
                        for b, (a, z) in enumerate(groups):
                            last = nc.tensor.matmul(spread[:, b, 0:(z - a) * parts], ones[:], diag[:, a:z, :],
                                                    start=True, stop=True)
                        last.then_inc(s["spread_ready"], 1)
                    pe.wait_ge(s["weight_ready"], 1)
                    for h in range(heads):
                        last = nc.tensor.matmul(carry_ps[:, each * h:each * (h + 1)], weight[:, h, :],
                                                last_state[:, each * h:each * (h + 1)], start=True, stop=True)
                else:
                    last = nc.tensor.matmul(carry_ps[:], e.after[:], last_state[:], start=True, stop=True)
                last.then_inc(s["carry_out"], 1)
                pe.wait_ge(s["carry_ready"], 1)
                for t in range(NT):
                    if t >= 2:
                        pe.wait_ge(s["node_in"], t - 1)
                    nc.tensor.matmul(node_ps[t % 2][:], takes[:, t, :], carry[:], start=True, stop=True)\
                        .then_inc(s["node_out"], 1)

            @block.scalar
            def _(act):
                if heads:
                    act.wait_ge(s["arg_ready"], 1)
                    nc.scalar.activation(weight[:], arg[:], ACT.Exp).then_inc(s["weight_ready"], 1)
                for t in range(NT):
                    act.wait_ge(s["node_out"], t + 1)
                    nc.scalar.copy(carried[:, t, :], node_ps[t % 2][:]).then_inc(s["node_in"], 1)
                if heads:
                    act.wait_ge(s["tops_ready"], 1)
                    nc.scalar.activation(shares[:], tops[:], ACT.Exp).then_inc(s["shares_ready"], 1)

    def additive_attention(self, name, e, w_dram, att_src, att_dst, heads, dim, result):
        nc = self.nc
        values = heads * (dim + 1)
        cols = heads * dim
        other, keys = self.table(f"{name}_other", values + heads), self.table(f"{name}_keys", heads)
        stack, r = self.stage(name)
        with stack:
            tab, keytab = r.sb("tab", [NP, NT, values + heads]), r.sb("keytab", [NP, NT, heads])
            own_score = r.sb("own_score", [NP, NT, heads])
            last_state = r.sb("last_state", [e.parts, values + heads])
            weights_stack, w = self.stage(f"{name}_w")
            with weights_stack:
                wcat = w.sb("wcat", [128, KC, cols + 2 * heads])
                att = w.sb("att", [128, 2, cols])
                weighed = w.sb("weighed", [128, 2, KC, cols])
                inner, v = self.stage(f"{name}_fold")
                with inner:
                    loaded, own_dve = v.sem("loaded"), v.sem("own_dve")
                    block = inner.enter_context(nc.Block())

                    @block.sync
                    def _(sp):
                        self.load_weight(sp, loaded, wcat[:, :, 0:cols], w_dram)
                        for k, a in enumerate((att_src, att_dst)):
                            sp.dma_start(att[:, k, :], a.partition_broadcast(128)).then_inc(loaded, 16)

                    @block.vector
                    def _(dve):
                        own = InOrder(dve, own_dve)
                        own.fire(nc.vector.memset(tab[:], 1.0))
                        dve.wait_ge(loaded, 48)
                        for k in range(2):
                            own.fire(nc.vector.tensor_tensor(weighed[:, k, :, :], wcat[:, :, 0:cols],
                                                             bc(att[:, k, :].unsqueeze(1), (128, KC, cols)), ALU.mult))
                        own.join()
                        for k in range(2):
                            own.fire(nc.vector.tensor_reduce(
                                wcat[:, :, cols + heads * k:cols + heads * (k + 1)],
                                weighed[:, k, :, :].rearrange("p c (h d) -> p c h d", d=dim), AX.X, ALU.add))
                        own.join()

                def put(t):
                    return tab[:, t, 0:values].rearrange("p (h d) -> p h d", d=dim + 1)[:, :, 0:dim]

                self.project(f"{name}_proj", [
                    ([(self.XT, wcat[:, :, 0:cols])], None, put, lambda ap: ap.rearrange("p (h d) -> p h d", d=dim)),
                    ([(self.XT, wcat[:, :, cols:cols + heads])], None, lambda t: tab[:, t, values:values + heads], lambda ap: ap),
                    ([(self.XT, wcat[:, :, cols + heads:])], None, lambda t: keytab[:, t, :], lambda ap: ap),
                ], [(other, tab), (keys, keytab)])
            self.stream(f"{name}_edges", e, heads, values, other, keys, last_state, "additive")
            nodes = r.sb("nodes", [NP, NT, values + heads])
            inner, v = self.stage(f"{name}_loops")
            with inner:
                own_dve = v.sem("own_dve")
                block = inner.enter_context(nc.Block())

                @block.vector
                def _(dve):
                    own = InOrder(dve, own_dve)
                    own(nc.vector.tensor_tensor(own_score[:], tab[:, :, values:], keytab[:], ALU.add))
                    own(nc.vector.scalar_tensor_tensor(out=own_score[:], in0=own_score[:], scalar=0.2,
                                                       in1=own_score[:], op0=ALU.mult, op1=ALU.max))
            self.merge(f"{name}_edges", e, heads, values, last_state, nodes, tab[:, :, 0:values], own_score)
            result(nodes[:, :, 0:values].rearrange("p t (h d) -> p t h d", d=dim + 1))

    def layer0_graph(self):
        nc, A = self.nc, self.A
        heads, dim = A["L0_gnn_att_src"].shape[1], A["L0_gnn_att_src"].shape[2]

        def result(nodes):
            stack, r = self.stage("L0g_result")
            with stack:
                share = r.sb("share", [NP, NT, heads])
                mean = r.sb("mean", [NP, NT, D])
                bias = r.sb("bias", [NP, D])
                own_dve, loaded = r.sem("own_dve"), r.sem("loaded")
                block = stack.enter_context(nc.Block())

                @block.sync
                def _(sp):
                    sp.dma_start(bias[:], A["L0_gnn_bias"].partition_broadcast(NP)).then_inc(loaded, 16)

                @block.vector
                def _(dve):
                    own = InOrder(dve, own_dve)
                    own(nc.vector.reciprocal(share[:], nodes[:, :, :, dim]))
                    own(nc.vector.tensor_tensor(
                        mean[:].rearrange("p t (h d) -> p t h d", d=dim), nodes[:, :, :, 0:dim],
                        bc(share[:].unsqueeze(3), (NP, NT, heads, dim)), ALU.mult))
                    own(nc.vector.tensor_tensor(self.X[:], self.X[:], mean[:], ALU.add))
                    dve.wait_ge(loaded, 16)
                    own(nc.vector.tensor_tensor(self.X[:], self.X[:], bc(bias[:].unsqueeze(1), (NP, NT, D)), ALU.add))

        self.normalise("L0g_norm", self.X)
        self.additive_attention("L0g", self.by_dst, A["L0_gnn_W"],
                                A["L0_gnn_att_src"].rearrange("a h d -> (a h d)"),
                                A["L0_gnn_att_dst"].rearrange("a h d -> (a h d)"), heads, dim, result)

    def transpose_rows(self, name, src, dst):
        nc = self.nc
        stack, r = self.stage(name)
        with stack:
            tp = [r.ps(f"tp{k}", [128, 512]) for k in range(4)]
            turned, copied = r.sem("turned"), r.sem("copied")
            groups = [(t, min(t + 4, NT), c) for t in range(0, NT, 4) for c in range(KC)]
            block = stack.enter_context(nc.Block())

            @block.tensor
            def _(pe):
                for n, (a, b, c) in enumerate(groups):
                    if n >= 4:
                        pe.wait_ge(copied, n - 3)
                    for t in range(a, b):
                        last = nc.tensor.transpose(tp[n % 4][:, (t - a) * NP:(t - a + 1) * NP],
                                                   src[:, t, c * 128:(c + 1) * 128], self.ident[0:NP, 0:NP])
                    last.then_inc(turned, 1)

            @block.scalar
            def _(act):
                for n, (a, b, c) in enumerate(groups):
                    act.wait_ge(turned, n + 1)
                    nc.scalar.copy(dst[:, c, a * NP:b * NP], tp[n % 4][:, 0:(b - a) * NP]).then_inc(copied, 1)

    def add_normalised(self, name, src, gamma_dram, beta_dram):
        nc = self.nc
        stack, r = self.stage(name)
        with stack:
            sd, rstd = r.sb("sd", [NP, NT]), r.sb("rstd", [NP, NT])
            gamma, beta = r.sb("gamma", [NP, D]), r.sb("beta", [NP, D])
            own_dve, loaded = r.sem("own_dve"), r.sem("loaded")
            var_ready, sd_ready = r.sem("var_ready"), r.sem("sd_ready")
            block = stack.enter_context(nc.Block())

            @block.sync
            def _(sp):
                sp.dma_start(gamma[:], gamma_dram.partition_broadcast(NP)).then_inc(loaded, 16)
                sp.dma_start(beta[:], beta_dram.partition_broadcast(NP)).then_inc(loaded, 16)

            @block.scalar
            def _(act):
                act.wait_ge(var_ready, 1)
                nc.scalar.activation(sd[:], rstd[:], ACT.Sqrt).then_inc(sd_ready, 1)

            @block.vector
            def _(dve):
                own = InOrder(dve, own_dve)
                mv = self.rows_statistics(dve, own, src, r)
                own(nc.vector.tensor_scalar_add(rstd[:], mv[:, :, 1], 1e-5))
                dve.sem_inc(var_ready, 1)
                dve.wait_ge(sd_ready, 1)
                own(nc.vector.reciprocal(rstd[:], sd[:]))
                for t in range(NT):
                    own.fire(nc.vector.tensor_scalar(src[:, t, :], src[:, t, :], mv[:, t, 0:1], rstd[:, t:t + 1],
                                                     ALU.subtract, ALU.mult))
                own.join()
                dve.wait_ge(loaded, 32)
                own(nc.vector.tensor_tensor(src[:], src[:], bc(gamma[:].unsqueeze(1), (NP, NT, D)), ALU.mult))
                own(nc.vector.tensor_tensor(src[:], src[:], bc(beta[:].unsqueeze(1), (NP, NT, D)), ALU.add))
                own(nc.vector.tensor_tensor(self.X[:], self.X[:], src[:], ALU.add))

    def top_two(self, own, r, scores, slots, experts):
        nc = self.nc
        shape = (NP, slots, experts)
        equal, at = r.sb("equal", list(shape)), r.sb("at", list(shape))
        hots = [r.sb(f"hot{k}", list(shape)) for k in range(2)]
        tops = [r.sb(f"top{k}", [NP, slots]) for k in range(2)]
        place = [r.sb(f"place{k}", [NP, slots]) for k in range(2)]
        for k in range(2):
            own(nc.vector.tensor_reduce(tops[k][:], scores[:], AX.X, ALU.max))
            own(nc.vector.tensor_tensor(equal[:], scores[:], bc(tops[k][:].unsqueeze(2), shape), ALU.is_equal))
            own(nc.vector.scalar_tensor_tensor(
                out=at[:], in0=equal[:], scalar=-64.0, in1=bc(self.small[0:NP, 0:experts].unsqueeze(1), shape),
                op0=ALU.mult, op1=ALU.add))
            own(nc.vector.tensor_reduce(place[k][:], at[:], AX.X, ALU.min))
            own(nc.vector.tensor_tensor(hots[k][:], at[:], bc(place[k][:].unsqueeze(2), shape), ALU.is_equal))
            if k == 0:
                own(nc.vector.scalar_tensor_tensor(out=scores[:], in0=hots[0][:], scalar=-BIG, in1=scores[:],
                                                   op0=ALU.mult, op1=ALU.add))
        return hots, tops, place

    def gate_scores(self, name, w_dram, b_dram, scores):
        nc, experts = self.nc, w_dram.shape[1]
        stack, r = self.stage(name)
        with stack:
            w, b = r.sb("w", [128, KC, experts]), r.sb("b", [NP, experts])
            inner, v = self.stage(f"{name}_load")
            with inner:
                loaded = v.sem("loaded")
                block = inner.enter_context(nc.Block())

                @block.sync
                def _(sp):
                    self.load_weight(sp, loaded, w[:], w_dram)
                    sp.dma_start(b[:], b_dram.partition_broadcast(NP)).then_inc(loaded, 16)
                    sp.wait_ge(loaded, 32)
            self.project(f"{name}_proj", [([(self.XT, w[:])], b[:], lambda t: scores[:, t, :], lambda ap: ap)])

    def transposed_rows_of(self, name, items):
        nc = self.nc
        stack, r = self.stage(name)
        with stack:
            raw = [r.sb(f"raw{k}", [v.shape[0], 128]) for k, (v, _) in enumerate(items)]
            ps = [r.ps(f"ps{k}", [128, v.shape[0]]) for k, (v, _) in enumerate(items)]
            loaded, turned = r.sem("loaded"), r.sem("turned")
            block = stack.enter_context(nc.Block())

            @block.sync
            def _(sp):
                for k, (v, _) in enumerate(items):
                    sp.dma_start(raw[k][:], v).then_inc(loaded, 16)

            @block.tensor
            def _(pe):
                pe.wait_ge(loaded, 16 * len(items))
                for k, (v, _) in enumerate(items):
                    n = v.shape[0]
                    nc.tensor.transpose(ps[k][:], raw[k][:], self.ident[0:n, 0:n]).then_inc(turned, 1)

            @block.scalar
            def _(act):
                for k, (_, tile) in enumerate(items):
                    act.wait_ge(turned, k + 1)
                    last = nc.scalar.copy(tile, ps[k][:])

    def experts(self, name, turns, w1, b1, w2, b2, gate, acc, scale=None, shift=None, chosen=None):
        nc, XT = self.nc, self.XT
        count, hidden = w1.shape[0], w1.shape[2]
        hc = hidden // 128
        blocks = NT // FFN_TILES
        left = 512 - 3 * NP
        stack, r = self.stage(name)
        with stack:
            w1s, w2s = r.sb("w1s", [128, KC, hidden]), r.sb("w2s", [128, hc, D])
            b1s, b2s = r.sb("b1s", [128, count * hc]), r.sb("b2s", [NP, D])
            hid = [r.sb(f"hid{k}", [128, hc, TOK]) for k in range(2)]
            items = [(b1.rearrange("e (c k) -> (e c) k", k=128), b1s[:])]
            if scale is not None:
                xe = r.sb("xe", [128, KC, NODES])
                scales = r.sb("scales", [128, 2, count * KC])
                items += [(v.rearrange("e (c k) -> (e c) k", k=128), scales[:, n, :])
                          for n, v in enumerate((scale, shift))]
            self.transposed_rows_of(f"{name}_bias", items)
            x_in = XT if scale is None else xe
            up = [r.ps(f"up{k}", [128, 1024]) for k in range(2)]
            down = [r.ps(f"down{k}", [NP, 512]) for k in range(4)]
            w1_in, w2_in, b2_in = r.sem("w1_in"), r.sem("w2_in"), r.sem("b2_in")
            up_done, gelu_done, down_done, summed = (r.sem(n) for n in ("up_done", "gelu_done", "down_done", "summed"))
            own_dve, scaled = r.sem("own_dve"), r.sem("scaled")
            expert_begun, bias_in = r.sem("expert_begun"), r.sem("bias_in")
            b1e = r.sb("b1e", [128, hc])
            per = blocks * hc
            block = stack.enter_context(nc.Block())

            def bank(n):
                return down[n % 4][:, 0:D]

            def picker(engine):
                if chosen is None:
                    return lambda i: i
                values = [engine.value_load(chosen[0:1, k:k + 1], min_val=0, max_val=count - 1) for k in range(turns)]
                return lambda i: values[i]

            @block.sync
            def _(sp):
                expert = picker(sp)

                def load(i):
                    e = expert(i)
                    if not isinstance(i, int) or i > 0:
                        sp.wait_ge(up_done, per * i)
                    sp.dma_start(w1s[:], w1[bass.ds(e, 1)].rearrange("e (c k) h -> k (e c) h", k=128)).then_inc(w1_in, 16)
                    if not isinstance(i, int) or i > 0:
                        sp.wait_ge(down_done, NT * i)
                        sp.wait_ge(summed, NT * i)
                    sp.dma_start(w2s[:], w2[bass.ds(e, 1)].rearrange("e (c k) d -> k (e c) d", k=128)).then_inc(w2_in, 16)
                    sp.dma_start(b2s[:], b2[bass.ds(e, 1)].rearrange("e d -> (e d)").partition_broadcast(NP)).then_inc(b2_in, 16)

                loop(sp, turns, lambda i, first, last: load(i))

            @block.tensor
            def _(pe):
                def upward(i, first, b):
                    if b == 0:
                        pe.wait_ge(w1_in, 16 * (i + 1))
                        if scale is not None:
                            pe.wait_ge(scaled, i + 1)
                    for h in range(hc):
                        m = b * hc + h
                        if not first or m >= 2:
                            pe.wait_ge(gelu_done, per * i + m - 1)
                        for c in range(KC):
                            for lo, hi, at in ((0, 3 * NP, left), (3 * NP, TOK, 512)):
                                last = nc.tensor.matmul(
                                    up[m % 2][:, at:at + hi - lo], w1s[:, c, 128 * h:128 * (h + 1)],
                                    x_in[:, c, b * TOK + lo:b * TOK + hi], start=(c == 0), stop=(c == KC - 1))
                        last.then_inc(up_done, 1)

                def downward(i, first, b):
                    if b == 0:
                        pe.wait_ge(w2_in, 16 * (i + 1))
                    pe.wait_ge(gelu_done, per * i + hc * (b + 1))
                    for k in range(FFN_TILES):
                        n = b * FFN_TILES + k
                        if n >= 4:
                            pe.wait_ge(summed, NT * i + n - 3)
                        elif n == 0 and not first:
                            pe.wait_ge(summed, NT * i)
                        for h in range(hc):
                            last = nc.tensor.matmul(bank(n), hid[b % 2][:, h, k * NP:(k + 1) * NP], w2s[:, h, :],
                                                    start=(h == 0), stop=(h == hc - 1))
                        last.then_inc(down_done, 1)

                def turn(i, first, last):
                    upward(i, first, 0)
                    for b in range(1, blocks):
                        upward(i, first, b)
                        downward(i, first, b - 1)
                    downward(i, first, blocks - 1)
                loop(pe, turns, turn)

            @block.scalar
            def _(act):
                expert = picker(act)

                def turn(i, first, last):
                    if not first:
                        act.wait_ge(gelu_done, per * i)
                    act.sem_inc(expert_begun, 1)
                    nc.scalar.copy(b1e[:], b1s[:, bass.ds(expert(i) * hc, hc)]).then_inc(bias_in, 1)
                    act.wait_ge(bias_in, i + 1)
                    for b in range(blocks):
                        for h in range(hc):
                            m = b * hc + h
                            act.wait_ge(up_done, per * i + m + 1)
                            if h == 0:
                                if b >= 2:
                                    act.wait_ge(down_done, NT * i + FFN_TILES * (b - 1))
                                elif not first:
                                    act.wait_ge(down_done, NT * i)
                            nc.scalar.activation(hid[b % 2][:, h, :], up[m % 2][:, left:left + TOK], ACT.Gelu,
                                                 bias=b1e[:, h:h + 1]).then_inc(gelu_done, 1)
                loop(act, turns, turn)

            @block.vector
            def _(dve):
                own = InOrder(dve, own_dve)

                def scale_rows(i):
                    for c in range(KC):
                        own.fire(nc.vector.tensor_scalar(
                            xe[:, c, :], XT[:, c, :], scales[:, 0, bass.ds(KC * i + c, 1)],
                            scales[:, 1, bass.ds(KC * i + c, 1)], ALU.mult, ALU.add))
                    own.join()
                    dve.sem_inc(scaled, 1)

                def turn(i, first, last):
                    own.restart()
                    if not first:
                        dve.wait_ge(summed, NT * i)
                    if first and scale is not None:
                        scale_rows(0)
                    dve.wait_ge(b2_in, 16 * (i + 1))
                    for t in range(NT):
                        own.fire(nc.vector.scalar_tensor_tensor(out=acc[:, t, :], in0=b2s[:], scalar=gate(t, i),
                                                                in1=acc[:, t, :], op0=ALU.mult, op1=ALU.add))
                    own.join()
                    for t in range(NT):
                        if t == NT - 2 * FFN_TILES and scale is not None and not last:
                            dve.wait_ge(up_done, per * (i + 1))
                            scale_rows(i + 1)
                        dve.wait_ge(down_done, NT * i + t + 1)
                        nc.vector.scalar_tensor_tensor(out=acc[:, t, :], in0=bank(t), scalar=gate(t, i),
                                                       in1=acc[:, t, :], op0=ALU.mult, op1=ALU.add).then_inc(summed, 1)
                loop(dve, turns, turn)
                dve.wait_ge(summed, NT * turns)

    def layer0_experts(self):
        nc, A = self.nc, self.A
        count = A["L0_ffn_Wg"].shape[1]
        self.normalise("L0f_norm", self.X)
        outer, o = self.stage("L0f")
        with outer:
            gates = o.sb("gates", [NP, NT, count])
            self.gate_scores("L0f_gate", A["L0_ffn_Wg"], A["L0_ffn_bg"], gates)
            stack, r = self.stage("L0f_top")
            with stack:
                own_dve = r.sem("own_dve")
                block = stack.enter_context(nc.Block())

                @block.vector
                def _(dve):
                    own = InOrder(dve, own_dve)
                    hots, _, _ = self.top_two(own, r, gates, NT, count)
                    own(nc.vector.tensor_tensor(gates[:], hots[0][:], hots[1][:], ALU.add))
            self.experts("L0f_experts", count, A["L0_ffn_W1"], A["L0_ffn_b1"], A["L0_ffn_W2"], A["L0_ffn_b2"],
                         lambda t, i: gates[:, t, bass.ds(i, 1)], self.X)

    def layer1_graph(self):
        nc, A = self.nc, self.A
        self.normalise("L1g_norm", self.X)
        rows = self.table("L1g_rows", D)
        outer, o = self.stage("L1g")
        with outer:
            last_state = o.sb("last_state", [NP, D])
            stack, r = self.stage("L1g_table")
            with stack:
                tab = r.sb("tab", [NP, NT, D])
                made, stored = r.sem("made"), r.sem("stored")
                block = stack.enter_context(nc.Block())

                @block.vector
                def _(dve):
                    nc.vector.tensor_tensor(tab[:], self.XH[:], bc(self.isout[:].unsqueeze(2), (NP, NT, D)),
                                            ALU.mult).then_inc(made, 1)

                @block.sync
                def _(sp):
                    sp.wait_ge(made, 1)
                    sp.dma_start(rows.rearrange("(p t) w -> p t w", t=NT), tab[:]).then_inc(stored, 16)
                    sp.wait_ge(stored, 16)
            self.stream("L1g_edges", self.by_dst, 0, D, rows, None, last_state, "sum")
            nodes = o.sb("nodes", [NP, NT, D])
            self.merge("L1g_edges", self.by_dst, 0, D, last_state, nodes)
            total = o.sb("total", [NP, NT, D])
            stack, r = self.stage("L1g_mix")
            with stack:
                own_dve = r.sem("own_dve")
                block = stack.enter_context(nc.Block())

                @block.vector
                def _(dve):
                    own = InOrder(dve, own_dve)
                    own(nc.vector.tensor_tensor(nodes[:], nodes[:], bc(self.isout[:].unsqueeze(2), (NP, NT, D)), ALU.mult))
                    own(nc.vector.tensor_tensor(total[:], self.XH[:], nodes[:], ALU.add))
                    own(nc.vector.tensor_tensor(nodes[:], self.XH[:], nodes[:], ALU.mult))
            mixed_t = o.sb("mixed_t", [128, KC, NODES])
            self.transpose_rows("L1g_turn0", total, self.XT)
            self.transpose_rows("L1g_turn1", nodes, mixed_t)
            w1, w2, b = o.sb("w1", [128, KC, D]), o.sb("w2", [128, KC, D]), o.sb("b", [NP, D])
            stack, r = self.stage("L1g_load")
            with stack:
                loaded = r.sem("loaded")
                block = stack.enter_context(nc.Block())

                @block.sync
                def _(sp):
                    self.load_weight(sp, loaded, w1[:], A["L1_gnn_W1"])
                    self.load_weight(sp, loaded, w2[:], A["L1_gnn_W2"])
                    sp.dma_start(b[:], A["L1_gnn_b"].partition_broadcast(NP)).then_inc(loaded, 16)
                    sp.wait_ge(loaded, 48)
            self.project("L1g_proj", [([(self.XT, w1[:]), (mixed_t, w2[:])], None, lambda t: total[:, t, :], lambda ap: ap)])
            stack, r = self.stage("L1g_result")
            with stack:
                square, norm, root = r.sb("square", [NP, NT]), r.sb("norm", [NP, NT]), r.sb("root", [NP, NT])
                own_dve, square_ready, root_ready = r.sem("own_dve"), r.sem("square_ready"), r.sem("root_ready")
                block = stack.enter_context(nc.Block())

                @block.vector
                def _(dve):
                    own = InOrder(dve, own_dve)
                    own(nc.vector.tensor_tensor(total[:], total[:], bc(self.by_dst.has[:].unsqueeze(2), (NP, NT, D)), ALU.mult))
                    own(nc.vector.tensor_tensor(total[:], total[:], bc(b[:].unsqueeze(1), (NP, NT, D)), ALU.add))
                    own(nc.vector.scalar_tensor_tensor(
                        out=total[:].rearrange("p t d -> p (t d)"), in0=total[:].rearrange("p t d -> p (t d)"),
                        scalar=0.01, in1=total[:].rearrange("p t d -> p (t d)"), op0=ALU.mult, op1=ALU.max))
                    own(nc.vector.tensor_tensor(nodes[:], total[:], total[:], ALU.mult))
                    own(nc.vector.tensor_reduce(square[:], nodes[:], AX.X, ALU.add))
                    dve.sem_inc(square_ready, 1)
                    dve.wait_ge(root_ready, 1)
                    own(nc.vector.tensor_scalar_max(norm[:], root[:], 1e-12))
                    own(nc.vector.reciprocal(norm[:], norm[:]))
                    own(nc.vector.tensor_tensor(total[:], total[:], bc(norm[:].unsqueeze(2), (NP, NT, D)), ALU.mult))
                    own(nc.vector.tensor_tensor(self.X[:], self.X[:], total[:], ALU.add))

                @block.scalar
                def _(act):
                    act.wait_ge(square_ready, 1)
                    nc.scalar.activation(root[:], square[:], ACT.Sqrt).then_inc(root_ready, 1)

    def layer1_experts(self):
        nc, A = self.nc, self.A
        heads, count = A["L1_ffn_att_src"].shape
        wide = heads * count
        self.normalise("L1f_norm", self.X)
        outer, o = self.stage("L1f")
        with outer:
            gates = o.sb("gates", [NP, NT, count])

            def result(nodes):
                stack, r = self.stage("L1f_result")
                with stack:
                    agg, dev = r.sb("agg", [NP, NT, wide]), r.sb("dev", [NP, NT, wide])
                    share = r.sb("share", [NP, NT, heads])
                    mean, var = r.sb("mean", [NP, NT]), r.sb("var", [NP, NT])
                    root, ratio = r.sb("root", [NP, NT]), r.sb("ratio", [NP, NT])
                    scores = r.sb("scores", [NP, NT, count])
                    rows = r.sb("rows", [NP, 3, wide])
                    own_dve, loaded = r.sem("own_dve"), r.sem("loaded")
                    var_ready, root_ready, gap_ready, ratio_ready = (
                        r.sem(n) for n in ("var_ready", "root_ready", "gap_ready", "ratio_ready"))
                    block = stack.enter_context(nc.Block())

                    @block.sync
                    def _(sp):
                        for k, n in enumerate(("b_gat", "ln_gamma", "ln_beta")):
                            sp.dma_start(rows[:, k, :], A[f"L1_ffn_{n}"].partition_broadcast(NP)).then_inc(loaded, 16)

                    @block.scalar
                    def _(act):
                        act.wait_ge(var_ready, 1)
                        nc.scalar.activation(root[:], var[:], ACT.Sqrt).then_inc(root_ready, 1)
                        act.wait_ge(gap_ready, 1)
                        nc.scalar.activation(ratio[:], mean[:], ACT.Exp).then_inc(ratio_ready, 1)

                    @block.vector
                    def _(dve):
                        own = InOrder(dve, own_dve)
                        tt = nc.vector.tensor_tensor

                        def row(k):
                            return bc(rows[:, k, :].unsqueeze(1), (NP, NT, wide))

                        def each(ap):
                            return bc(ap.unsqueeze(2), (NP, NT, wide))

                        own(nc.vector.tensor_scalar_add(share[:], nodes[:, :, :, count], 1e-16))
                        own(nc.vector.reciprocal(share[:], share[:]))
                        own(tt(agg[:].rearrange("p t (h d) -> p t h d", d=count), nodes[:, :, :, 0:count],
                               bc(share[:].unsqueeze(3), (NP, NT, heads, count)), ALU.mult))
                        dve.wait_ge(loaded, 48)
                        own(tt(agg[:], agg[:], row(0), ALU.add))
                        own(nc.vector.tensor_reduce(mean[:], agg[:], AX.X, ALU.add))
                        own(nc.vector.tensor_scalar(mean[:], mean[:], 1.0 / wide, None, ALU.mult))
                        own(tt(agg[:], agg[:], each(mean[:]), ALU.subtract))
                        own(tt(dev[:], agg[:], agg[:], ALU.mult))
                        own(nc.vector.tensor_reduce(var[:], dev[:], AX.X, ALU.add))
                        own(nc.vector.tensor_scalar(var[:], var[:], 1.0 / wide, 1e-5, ALU.mult, ALU.add))
                        dve.sem_inc(var_ready, 1)
                        dve.wait_ge(root_ready, 1)
                        own(nc.vector.reciprocal(var[:], root[:]))
                        own(tt(agg[:], agg[:], each(var[:]), ALU.mult))
                        own(tt(agg[:], agg[:], row(1), ALU.mult))
                        own(tt(agg[:], agg[:], row(2), ALU.add))
                        own(nc.vector.tensor_reduce(scores[:], agg[:].rearrange("p t (h d) -> p t d h", d=count),
                                                    AX.X, ALU.add))
                        own(nc.vector.tensor_scalar(scores[:], scores[:], 1.0 / heads, None, ALU.mult))
                        hots, tops, _ = self.top_two(own, r, scores, NT, count)
                        own(tt(mean[:], tops[1][:], tops[0][:], ALU.subtract))
                        dve.sem_inc(gap_ready, 1)
                        dve.wait_ge(ratio_ready, 1)
                        own(nc.vector.tensor_scalar_add(var[:], ratio[:], 1.0))
                        own(nc.vector.reciprocal(var[:], var[:]))
                        own(tt(ratio[:], ratio[:], var[:], ALU.mult))
                        own.fire(tt(hots[0][:], hots[0][:], bc(var[:].unsqueeze(2), (NP, NT, count)), ALU.mult))
                        own.fire(tt(hots[1][:], hots[1][:], bc(ratio[:].unsqueeze(2), (NP, NT, count)), ALU.mult))
                        own.join()
                        own(tt(gates[:], hots[0][:], hots[1][:], ALU.add))

            self.additive_attention("L1f_gat", self.by_gate, A["L1_ffn_W_gat"],
                                    A["L1_ffn_att_src"].rearrange("h d -> (h d)"),
                                    A["L1_ffn_att_dst"].rearrange("h d -> (h d)"), heads, count, result)
            self.experts("L1f_experts", count, A["L1_ffn_W1"], A["L1_ffn_b1"], A["L1_ffn_W2"], A["L1_ffn_b2"],
                         lambda t, i: gates[:, t, bass.ds(i, 1)], self.X)

    def layer2_graph(self):
        nc, A, XT = self.nc, self.A, self.XT
        rels, dim = A["L2_gnn_rel_w"].shape
        heads = D // dim
        values = heads * (dim + 1)
        self.normalise("L2g_norm", self.X)
        other, keys = self.table("L2g_other", values + D), self.table("L2g_keys", heads * 2 * dim)
        root = float(dim) ** -0.5
        assert root == 0.125
        outer, o = self.stage("L2g")
        with outer:
            last_state = o.sb("last_state", [NP, values + heads])
            stack, r = self.stage("L2g_tables")
            with stack:
                tab, keytab = r.sb("tab", [NP, NT, values + D]), r.sb("keytab", [NP, NT, heads * 2 * dim])
                wv, wk = r.sb("wv", [128, KC, D]), r.sb("wk", [128, KC, D])
                wkey = r.sb("wkey", [128, KC, heads, 2 * dim])
                bv, bk, bkey = r.sb("bv", [NP, D]), r.sb("bk", [NP, D]), r.sb("bkey", [NP, heads, 2 * dim])
                inner, v = self.stage("L2g_fold")
                with inner, nc.allow_non_contiguous_dma(reason="vectors of 256 words, one to a partition"):
                    wq, wq_t = v.sb("wq", [128, KC, D]), v.sb("wq_t", [128, KC, D])
                    rel2, rel_t = v.sb("rel2", [rels, 2, dim]), v.sb("rel_t", [2 * dim, rels])
                    bq, bq_col, bq_wide = v.sb("bq", [NP, D]), v.sb("bq_col", [128, KC]), v.sb("bq_wide", [128, KC, NP])
                    emb = v.sb("emb", [128, KC])
                    rel_ps, wq_ps = v.ps("rel_ps", [2 * dim, rels]), v.ps("wq_ps", [128, KC, D])
                    wr_ps, br_ps = v.ps("wr_ps", [128, 2, 512]), v.ps("br_ps", [NP, 2, 512])
                    loaded, turned, copied, folded, own_dve = (
                        v.sem(n) for n in ("loaded", "turned", "copied", "folded", "own_dve"))
                    block = inner.enter_context(nc.Block())

                    @block.sync
                    def _(sp):
                        self.load_weight(sp, loaded, wq[:], A["L2_gnn_Wq"])
                        self.load_weight(sp, loaded, wk[:], A["L2_gnn_Wk"])
                        self.load_weight(sp, loaded, wv[:], A["L2_gnn_Wv"])
                        for k in range(2):
                            sp.dma_start(rel2[:, k, :], A["L2_gnn_rel_w"]).then_inc(loaded, 16)
                        for to, n in ((bq, "bq"), (bk, "bk"), (bv, "bv")):
                            sp.dma_start(to[:], A[f"L2_gnn_{n}"].partition_broadcast(NP)).then_inc(loaded, 16)
                        for to, n in ((bq_col, "bq"), (emb, "query_emb")):
                            sp.dma_start(to[:], A[f"L2_gnn_{n}"].rearrange("(c k) -> k c", k=128)).then_inc(loaded, 16)

                    @block.tensor
                    def _(pe):
                        pe.wait_ge(loaded, 160)
                        nc.tensor.transpose(rel_ps[:], rel2[:].rearrange("r k d -> r (k d)"), self.ident[0:rels, 0:rels])
                        for j in range(KC):
                            for c in range(KC):
                                last = nc.tensor.transpose(wq_ps[:, j, 128 * c:128 * (c + 1)],
                                                           wq[:, c, 128 * j:128 * (j + 1)], self.ident[:])
                        last.then_inc(turned, 1)
                        pe.wait_ge(copied, 1)
                        for h in range(heads):
                            j, q = dim * h // 128, dim * h % 128
                            for c in range(KC):
                                at = dim * (2 * c + j)
                                nc.tensor.matmul(wr_ps[:, q // dim, at:at + dim], wq_t[q:q + dim, j, 128 * c:128 * (c + 1)],
                                                 rel_t[q:q + dim, :], start=True, stop=True)
                            nc.tensor.matmul(br_ps[:, q // dim, dim * j:dim * (j + 1)], bq_wide[q:q + dim, j, :],
                                             rel_t[q:q + dim, :], start=True, stop=True).then_inc(folded, 1)

                    @block.vector
                    def _(dve):
                        own = InOrder(dve, own_dve)
                        ts = nc.vector.tensor_scalar
                        dve.wait_ge(loaded, 160)
                        own.fire(nc.vector.memset(tab[:], 1.0))
                        own.fire(ts(emb[:], emb[:], 0.1, None, ALU.mult))
                        own.fire(nc.vector.tensor_copy(bq_wide[:], bc(bq_col[:].unsqueeze(2), (128, KC, NP))))
                        dve.wait_ge(turned, 1)
                        own.fire(ts(rel_t[:], rel_ps[:], 0.2, None, ALU.mult))
                        own(nc.vector.tensor_copy(wq_t[:], wq_ps[:]))
                        dve.sem_inc(copied, 1)
                        for c in range(KC):
                            own.fire(ts(XT[:, c, :], XT[:, c, :], emb[:, c:c + 1], None, ALU.add))
                        own.fire(ts(wkey[:, :, :, 0:dim], wq[:].rearrange("k c (h d) -> k c h d", d=dim), root, None, ALU.mult))
                        own.fire(ts(bkey[:, :, 0:dim], bq[:].rearrange("p (h d) -> p h d", d=dim), root, None, ALU.mult))
                        dve.wait_ge(folded, heads)
                        for q in range(2):
                            own.fire(ts(wkey[:, :, q::2, dim:],
                                        wr_ps[:, q, 0:4 * dim].rearrange("k (c j d) -> k c j d", c=KC, d=dim), root, None, ALU.mult))
                            own.fire(ts(bkey[:, q::2, dim:],
                                        br_ps[:, q, 0:2 * dim].rearrange("p (j d) -> p j d", d=dim), root, None, ALU.mult))
                        own.join()

                def head_view(ap):
                    return ap.rearrange("p (h d) -> p h d", d=dim)

                self.project("L2g_proj", [
                    ([(XT, wv[:])], bv[:], lambda t: tab[:, t, 0:values].rearrange("p (h d) -> p h d", d=dim + 1)[:, :, 0:dim],
                     head_view),
                    ([(XT, wk[:])], bk[:], lambda t: tab[:, t, values:], lambda ap: ap),
                    ([(XT, wkey[:].rearrange("k c h d -> k c (h d)"))], bkey[:].rearrange("p h d -> p (h d)"),
                     lambda t: keytab[:, t, :], lambda ap: ap),
                ], [(other, tab), (keys, keytab)])
            self.stream("L2g_edges", self.by_dst, heads, values, other, keys, last_state, "relation")
            nodes = o.sb("nodes", [NP, NT, values + heads])
            self.merge("L2g_edges", self.by_dst, heads, values, last_state, nodes)
            mean = o.sb("mean", [NP, NT, D])
            stack, r = self.stage("L2g_mean")
            with stack:
                v = r.sb("v", [NP, NT, values])
                share, without = r.sb("share", [NP, NT, heads]), r.sb("without", [NP, NT])
                own_dve, loaded = r.sem("own_dve"), r.sem("loaded")
                block = stack.enter_context(nc.Block())

                @block.sync
                def _(sp):
                    sp.dma_start(v[:], other.rearrange("(p t) w -> p t w", t=NT)[:, :, 0:values]).then_inc(loaded, 16)

                @block.vector
                def _(dve):
                    own = InOrder(dve, own_dve)
                    tt = nc.vector.tensor_tensor
                    heads_of = nodes[:, :, 0:values].rearrange("p t (h d) -> p t h d", d=dim + 1)
                    mean_of = mean[:].rearrange("p t (h d) -> p t h d", d=dim)
                    own(nc.vector.reciprocal(share[:], heads_of[:, :, :, dim]))
                    own(tt(share[:], share[:], bc(self.by_dst.has[:].unsqueeze(2), (NP, NT, heads)), ALU.mult))
                    own(tt(mean_of, heads_of[:, :, :, 0:dim], bc(share[:].unsqueeze(3), (NP, NT, heads, dim)), ALU.mult))
                    own(nc.vector.tensor_scalar(without[:], self.by_dst.has[:], -1.0, 1.0, ALU.mult, ALU.add))
                    dve.wait_ge(loaded, 16)
                    own(tt(v[:], v[:], bc(without[:].unsqueeze(2), (NP, NT, values)), ALU.mult))
                    own(tt(mean_of, mean_of, v[:].rearrange("p t (h d) -> p t h d", d=dim + 1)[:, :, :, 0:dim], ALU.add))
            self.transpose_rows("L2g_turn", mean, XT)
            wo, bo = o.sb("wo", [128, KC, D]), o.sb("bo", [NP, D])
            stack, r = self.stage("L2g_load")
            with stack:
                loaded = r.sem("loaded")
                block = stack.enter_context(nc.Block())

                @block.sync
                def _(sp):
                    self.load_weight(sp, loaded, wo[:], A["L2_gnn_Wo"])
                    sp.dma_start(bo[:], A["L2_gnn_bo"].partition_broadcast(NP)).then_inc(loaded, 16)
                    sp.wait_ge(loaded, 32)
            self.project("L2g_out", [([(XT, wo[:])], bo[:], lambda t: mean[:, t, :], lambda ap: ap)])
            stack, r = self.stage("L2g_residual")
            with stack:
                own_dve = r.sem("own_dve")
                block = stack.enter_context(nc.Block())

                @block.vector
                def _(dve):
                    own = InOrder(dve, own_dve)
                    own(nc.vector.tensor_tensor(mean[:], mean[:], self.XH[:], ALU.add))
            self.add_normalised("L2g_add", mean, A["L2_gnn_gamma"], A["L2_gnn_beta"])

    def layer2_experts(self):
        nc, A = self.nc, self.A
        count = A["L2_ffn_Wr"].shape[1]
        self.normalise("L2f_norm", self.X)
        outer, o = self.stage("L2f")
        with outer:
            gates = o.sb("gates", [NP, NT, count])
            self.gate_scores("L2f_gate", A["L2_ffn_Wr"], A["L2_ffn_br"], gates)
            stack, r = self.stage("L2f_top")
            with stack:
                shape = (NP, NT, count)
                powers, probs = r.sb("powers", list(shape)), r.sb("probs", list(shape))
                one = r.sb("one", [NP, NT])
                own_dve, args_ready, powers_ready = r.sem("own_dve"), r.sem("args_ready"), r.sem("powers_ready")
                block = stack.enter_context(nc.Block())

                @block.scalar
                def _(act):
                    act.wait_ge(args_ready, 1)
                    nc.scalar.activation(powers[:], gates[:], ACT.Exp).then_inc(powers_ready, 1)

                @block.vector
                def _(dve):
                    own = InOrder(dve, own_dve)
                    tt = nc.vector.tensor_tensor
                    own(nc.vector.tensor_reduce(one[:], gates[:], AX.X, ALU.max))
                    own(tt(gates[:], gates[:], bc(one[:].unsqueeze(2), shape), ALU.subtract))
                    dve.sem_inc(args_ready, 1)
                    dve.wait_ge(powers_ready, 1)
                    own(nc.vector.tensor_reduce(one[:], powers[:], AX.X, ALU.add))
                    own(nc.vector.reciprocal(one[:], one[:]))
                    own(tt(powers[:], powers[:], bc(one[:].unsqueeze(2), shape), ALU.mult))
                    own(nc.vector.tensor_copy(probs[:], powers[:]))
                    hots, tops, _ = self.top_two(own, r, probs, NT, count)
                    own(tt(one[:], tops[0][:], tops[1][:], ALU.add))
                    own(nc.vector.reciprocal(one[:], one[:]))
                    own(tt(hots[0][:], hots[0][:], hots[1][:], ALU.add))
                    own(tt(powers[:], powers[:], hots[0][:], ALU.mult))
                    own(tt(gates[:], powers[:], bc(one[:].unsqueeze(2), shape), ALU.mult))
            self.normalise("L2f_norm2", self.XH)
            self.experts("L2f_experts", count, A["L2_ffn_W1"], A["L2_ffn_b1"], A["L2_ffn_W2"], A["L2_ffn_b2"],
                         lambda t, i: gates[:, t, bass.ds(i, 1)], self.X, A["L2_ffn_ln_g"], A["L2_ffn_ln_b"])

    def layer3_graph(self):
        nc, A, XT = self.nc, self.A, self.XT
        heads, dim = 16, 8
        wide = heads * dim
        vdim = D // heads
        values = heads * (vdim + 1)
        self.normalise("L3g_norm", self.X)
        other, keys = self.table("L3g_other", values + wide), self.table("L3g_keys", wide)
        outer, o = self.stage("L3g")
        with outer:
            last_state = o.sb("last_state", [NP, values + heads])
            rpe = o.sb("rpe", [128, 2 * wide])
            stack, r = self.stage("L3g_tables")
            with stack:
                tab, keytab = r.sb("tab", [NP, NT, values + wide]), r.sb("keytab", [NP, NT, wide])
                w, b = r.sb("w", [128, KC, 2 * wide + D]), r.sb("b", [NP, 2 * wide + D])
                inner, v = self.stage("L3g_load")
                with inner:
                    loaded, own_dve = v.sem("loaded"), v.sem("own_dve")
                    block = inner.enter_context(nc.Block())

                    @block.sync
                    def _(sp):
                        self.load_weight(sp, loaded, w[:], A["L3_gnn_Wqkv"])
                        sp.dma_start(b[:], A["L3_gnn_bqkv"].partition_broadcast(NP)).then_inc(loaded, 16)
                        for q in range(0, 128, ROW):
                            for k, n in enumerate(("q", "k")):
                                at = slice(wide * k, wide * (k + 1))
                                sp.dma_start(rpe[q:q + ATTR, at], A[f"L3_gnn_W{n}_rpe"]).then_inc(loaded, 16)
                                sp.dma_start(rpe[q + ATTR:q + ATTR + 1, at],
                                             A[f"L3_gnn_b{n}_rpe"].partition_broadcast(1)).then_inc(loaded, 16)
                        sp.wait_ge(loaded, 16 * 18)

                    @block.vector
                    def _(dve):
                        own = InOrder(dve, own_dve)
                        own.fire(nc.vector.memset(tab[:], 1.0))
                        dve.wait_ge(loaded, 16 * 18)
                        for part in (w[:, :, 0:wide], b[:, 0:wide]):
                            own.fire(nc.vector.tensor_scalar(part, part, float(dim) ** -0.5, None, ALU.mult))
                        own.join()
                self.project("L3g_proj", [
                    ([(XT, w[:, :, 0:wide])], b[:, 0:wide], lambda t: keytab[:, t, :], lambda ap: ap),
                    ([(XT, w[:, :, wide:2 * wide])], b[:, wide:2 * wide], lambda t: tab[:, t, values:], lambda ap: ap),
                    ([(XT, w[:, :, 2 * wide:])], b[:, 2 * wide:],
                     lambda t: tab[:, t, 0:values].rearrange("p (h d) -> p h d", d=vdim + 1)[:, :, 0:vdim],
                     lambda ap: ap.rearrange("p (h d) -> p h d", d=vdim)),
                ], [(other, tab), (keys, keytab)])
            self.stream("L3g_edges", self.by_src, heads, values, other, keys, last_state, "attributes", rpe)
            nodes = o.sb("nodes", [NP, NT, values + heads])
            self.merge("L3g_edges", self.by_src, heads, values, last_state, nodes)
            stack, r = self.stage("L3g_result")
            with stack:
                share, mean = r.sb("share", [NP, NT, heads]), r.sb("mean", [NP, NT, D])
                own_dve = r.sem("own_dve")
                block = stack.enter_context(nc.Block())

                @block.vector
                def _(dve):
                    own = InOrder(dve, own_dve)
                    tt = nc.vector.tensor_tensor
                    heads_of = nodes[:, :, 0:values].rearrange("p t (h d) -> p t h d", d=vdim + 1)
                    own(nc.vector.tensor_scalar_add(share[:], heads_of[:, :, :, vdim], 1e-16))
                    own(nc.vector.reciprocal(share[:], share[:]))
                    own(tt(share[:], share[:], bc(self.by_src.has[:].unsqueeze(2), (NP, NT, heads)), ALU.mult))
                    own(tt(mean[:].rearrange("p t (h d) -> p t h d", d=vdim), heads_of[:, :, :, 0:vdim],
                           bc(share[:].unsqueeze(3), (NP, NT, heads, vdim)), ALU.mult))
                    own(tt(self.X[:], self.X[:], mean[:], ALU.add))

    def layer3_experts(self):
        nc, A = self.nc, self.A
        count = A["L3_ffn_Wr"].shape[1]
        capacity = float(-(-NODES * 5 // (4 * count)))
        self.normalise("L3f_norm", self.X)
        outer, o = self.stage("L3f")
        with outer:
            gates, chosen = o.sb("gates", [NP, 2]), o.sb("chosen", [NP, 2], I32)
            stack, r = self.stage("L3f_route")
            with stack:
                shape = (NP, 1, count)
                wr, br = r.sb("wr", [128, KC, count]), r.sb("br", [NP, count])
                ones = r.sb("ones", [NP, 1])
                mean, wide = r.sb("mean", [128, KC]), r.sb("wide", [128, KC, NP])
                p, load, one = r.sb("p", list(shape)), r.sb("load", list(shape)), r.sb("one", [NP, 1])
                pick = r.sb("pick", [NP, 2])
                mean_ps, logit_ps = r.ps("mean_ps", [128, KC]), r.ps("logit_ps", [NP, count])
                own_dve, loaded, ones_made, summed, wide_ready, logits, arg_ready, exp_ready = (
                    r.sem(n) for n in ("own_dve", "loaded", "ones_made", "summed", "wide_ready", "logits",
                                       "arg_ready", "exp_ready"))
                block = stack.enter_context(nc.Block())

                @block.sync
                def _(sp):
                    self.load_weight(sp, loaded, wr[:], A["L3_ffn_Wr"])
                    sp.dma_start(br[:], A["L3_ffn_br"].partition_broadcast(NP)).then_inc(loaded, 16)

                @block.tensor
                def _(pe):
                    pe.wait_ge(ones_made, 1)
                    for c in range(KC):
                        for t in range(NT):
                            last = nc.tensor.matmul(mean_ps[:, c:c + 1], self.XH[:, t, 128 * c:128 * (c + 1)], ones[:],
                                                    start=(t == 0), stop=(t == NT - 1))
                    last.then_inc(summed, 1)
                    pe.wait_ge(wide_ready, 1)
                    pe.wait_ge(loaded, 32)
                    for c in range(KC):
                        last = nc.tensor.matmul(logit_ps[:], wide[:, c, :], wr[:, c, :], start=(c == 0), stop=(c == KC - 1))
                    last.then_inc(logits, 1)

                @block.scalar
                def _(act):
                    for k in range(2):
                        act.wait_ge(arg_ready, k + 1)
                        nc.scalar.activation(p[:], load[:], ACT.Exp).then_inc(exp_ready, 1)
                    act.wait_ge(arg_ready, 3)
                    nc.scalar.activation(pick[:, 1:2], one[:], ACT.Exp).then_inc(exp_ready, 1)

                @block.vector
                def _(dve):
                    own = InOrder(dve, own_dve)
                    tt, ts = nc.vector.tensor_tensor, nc.vector.tensor_scalar
                    own(nc.vector.memset(ones[:], 1.0))
                    dve.sem_inc(ones_made, 1)
                    dve.wait_ge(summed, 1)
                    own(ts(mean[:], mean_ps[:], 1.0 / NODES, None, ALU.mult))
                    own(nc.vector.tensor_copy(wide[:], bc(mean[:].unsqueeze(2), (128, KC, NP))))
                    dve.sem_inc(wide_ready, 1)
                    dve.wait_ge(logits, 1)
                    dve.wait_ge(loaded, 32)
                    own(tt(p[:, 0, :], logit_ps[:], br[:], ALU.add))

                    def softmax(k):
                        own(nc.vector.tensor_reduce(one[:], p[:, 0, :], AX.X, ALU.max))
                        own(tt(load[:, 0, :], p[:, 0, :], bc(one[:], (NP, count)), ALU.subtract))
                        dve.sem_inc(arg_ready, 1)
                        dve.wait_ge(exp_ready, k)
                        own(nc.vector.tensor_reduce(one[:], p[:, 0, :], AX.X, ALU.add))
                        own(nc.vector.reciprocal(one[:], one[:]))
                        own(tt(p[:, 0, :], p[:, 0, :], bc(one[:], (NP, count)), ALU.mult))

                    softmax(1)
                    own(ts(load[:], p[:], float(NODES), 1e-30, ALU.mult, ALU.max))
                    own(nc.vector.reciprocal(load[:], load[:]))
                    own(ts(load[:], load[:], capacity, 1.0, ALU.mult, ALU.min))
                    own(tt(p[:], p[:], load[:], ALU.mult))
                    softmax(2)
                    _, tops, place = self.top_two(own, r, p, 1, count)
                    for k in range(2):
                        own(ts(one[:], place[k][:], 64.0, None, ALU.add))
                        own(nc.vector.tensor_copy(chosen[:, k:k + 1], one[:]))
                    own(tt(one[:], tops[1][:], tops[0][:], ALU.subtract))
                    dve.sem_inc(arg_ready, 1)
                    dve.wait_ge(exp_ready, 3)
                    own(ts(one[:], pick[:, 1:2], 1.0, None, ALU.add))
                    own(nc.vector.reciprocal(gates[:, 0:1], one[:]))
                    own(tt(gates[:, 1:2], pick[:, 1:2], gates[:, 0:1], ALU.mult))
            self.experts("L3f_experts", 2, A["L3_ffn_W1"], A["L3_ffn_b1"], A["L3_ffn_W2"], A["L3_ffn_b2"],
                         lambda t, i: gates[:, i:i + 1], self.XH, chosen=chosen)
            self.add_normalised("L3f_add", self.XH, A["L3_ffn_gamma"], A["L3_ffn_beta"])


def build(nc, arrays, out):
    program = Program(nc, arrays, out)
    with ExitStack() as stack:
        room = Room(nc, stack, "all")
        program.setup(room)
        program.prepare_edges(room)
        program.layer0_graph()
        program.layer0_experts()
        program.layer1_graph()
        program.layer1_experts()
        program.layer2_graph()
        program.layer2_experts()
        program.layer3_graph()
        program.layer3_experts()
        program.finish()


def kernel(**inputs):
    import concourse.bacc as bacc
    from concourse.bass_utils import run_bass_kernel_spmd

    nc = bacc.Bacc("TRN2", target_bir_lowering=False, num_devices=1)
    given = {name: np.ascontiguousarray(a) for name, a in inputs.items()}
    arrays = {name: nc.dram_tensor(f"in_{name}", a.shape, mybir.dt.from_np(a.dtype), kind="ExternalInput").ap()
              for name, a in given.items()}
    out = nc.dram_tensor("out", (NODES, D), F32, kind="ExternalOutput").ap()
    build(nc, arrays, out)
    r = run_bass_kernel_spmd(nc, [{f"in_{name}": a for name, a in given.items()}], core_ids=[0])
    return r.results[0]["out"]
```

```python
from contextlib import ExitStack

import numpy as np

import concourse.bass as bass
from concourse import mybir

F32, BF16, I32 = mybir.dt.float32, mybir.dt.bfloat16, mybir.dt.int32
ALU, ACT, AX = mybir.AluOpType, mybir.ActivationFunctionType, mybir.AxisListType

NODES, D = 3125, 256
NP, NT = 125, 25
KC = D // 128
HALF = 8
STEP = 2 * HALF
SPAN = 1 + HALF
BIG = 1e30
ROW = 32
ATTR = 18
KEY, OTHER = 20, 21
DIV_MUL, DIV_SHIFT = 1311, 15
CLEAR_AT = 60
SLOTS_SHIFT = 8
SLOTS = 1 << SLOTS_SHIFT
FFN_TILES = 5
TOK = FFN_TILES * NP


class Room:

    def __init__(self, nc, stack, prefix):
        self.nc, self.stack, self.prefix = nc, stack, prefix

    def sb(self, name, shape, dt=F32):
        return self.stack.enter_context(self.nc.sbuf_tensor(f"{self.prefix}_{name}", shape, dt))

    def ps(self, name, shape, dt=F32):
        return self.stack.enter_context(self.nc.psum_tensor(f"{self.prefix}_{name}", shape, dt))

    def sem(self, name):
        return self.stack.enter_context(self.nc.semaphore(f"{self.prefix}_{name}"))


class InOrder:

    def __init__(self, engine, sem):
        self.engine, self.sem, self.n = engine, sem, 0

    def fire(self, ins):
        self.n += 1
        ins.then_inc(self.sem, 1)

    def join(self):
        self.engine.wait_ge(self.sem, self.n)

    def __call__(self, ins):
        self.fire(ins)
        self.join()

    def restart(self):
        self.engine.sem_clear(self.sem)
        self.n = 0


def bc(ap, shape):
    return ap.broadcast_to(list(shape))


def loop(engine, turns, turn):
    turn(0, True, False)
    if turns > 2:
        with engine.Fori(1, turns - 1) as i:
            turn(i, False, False)
    turn(turns - 1, False, True)


class Edges:

    def __init__(self, room, name, parts, cols):
        self.name, self.parts, self.cols = name, parts, cols
        self.first = room.sb(f"{name}_first", [parts, 1])
        self.last = room.sb(f"{name}_last", [parts, 1])
        self.closes = room.sb(f"{name}_closes", [parts, 1])
        self.before = room.sb(f"{name}_before", [parts, parts])
        self.after = room.sb(f"{name}_after", [parts, parts])
        self.end = room.sb(f"{name}_end", [NP, NT], I32)
        self.has = room.sb(f"{name}_has", [NP, NT])


class Program:
    def __init__(self, nc, A, out):
        self.nc, self.A, self.out = nc, A, out

    def clear_semaphores(self):
        ids = set(self.nc.released_uncleared_semaphores)
        if len(ids) < CLEAR_AT:
            return
        ids = sorted(ids)
        runs = []
        for k in ids:
            if runs and runs[-1][-1] == k - 1:
                runs[-1].append(k)
            else:
                runs.append([k])
        with self.nc.Block() as block:

            @block.gpsimd
            def _(pool):
                for run in runs:
                    pool.sem_clear(range(run[0], run[-1] + 1))

    def moved_sem(self, name):
        return self.room.sem(name)

    def stage(self, name):
        self.clear_semaphores()
        stack = ExitStack()
        return stack, Room(self.nc, stack, name)

    def setup(self, room):
        nc = self.nc
        self.room = room
        self.X = room.sb("X", [NP, NT, D])
        self.XH = room.sb("XH", [NP, NT, D])
        self.XT = room.sb("XT", [128, KC, NODES])
        self.ident = room.sb("ident", [128, 128])
        self.identb = room.sb("identb", [128, 128], BF16)
        self.upper = room.sb("upper", [128, 128])
        self.lower = room.sb("lower", [128, 128])
        self.hi_values = room.sb("hi_values", [128, NP])
        self.lo_values = room.sb("lo_values", [128, NT])
        self.small = room.sb("small", [128, 64])
        self.isout = room.sb("isout", [NP, NT])
        stack, r = self.stage("setup")
        with stack:
            made, loaded = r.sem("made"), r.sem("loaded")
            block = stack.enter_context(nc.Block())

            @block.gpsimd
            def _(pool):
                own = InOrder(pool, made)
                own.fire(pool.memset(self.ident[:], 0.0))
                own.fire(pool.memset(self.upper[:], 1.0))
                own.fire(pool.memset(self.lower[:], 1.0))
                own.fire(pool.iota(self.hi_values[:], [[NT, NP]], base=0, channel_multiplier=0,
                                   allow_small_or_imprecise_dtypes=True))
                own.fire(pool.iota(self.lo_values[:], [[1, NT]], base=0, channel_multiplier=0,
                                   allow_small_or_imprecise_dtypes=True))
                own(pool.iota(self.small[:], [[1, 64]], base=0, channel_multiplier=0,
                              allow_small_or_imprecise_dtypes=True))
                own.fire(pool.affine_select(out=self.ident[:], in_=self.ident[:], compare_op=ALU.not_equal,
                                            fill=1.0, base=0, pattern=[[-1, 128]], channel_multiplier=1))
                own.fire(pool.affine_select(out=self.upper[:], in_=self.upper[:], compare_op=ALU.is_gt,
                                            fill=0.0, base=0, pattern=[[1, 128]], channel_multiplier=-1))
                own(pool.affine_select(out=self.lower[:], in_=self.lower[:], compare_op=ALU.is_gt,
                                       fill=0.0, base=0, pattern=[[-1, 128]], channel_multiplier=1))
                own(pool.tensor_copy(self.identb[:], self.ident[:]))

            @block.sync
            def _(sp):
                sp.dma_start(self.X[:], self.A["x"].rearrange("(p t) d -> p t d", t=NT)).then_inc(loaded, 16)
                sp.wait_ge(loaded, 16)

    def finish(self):
        stack, r = self.stage("store")
        with stack:
            stored = r.sem("stored")
            block = stack.enter_context(self.nc.Block())

            @block.sync
            def _(sp):
                sp.dma_start(self.out.rearrange("(p t) d -> p t d", t=NT), self.X[:]).then_inc(stored, 16)
                sp.wait_ge(stored, 16)

    def rows_statistics(self, dve, own, src, r):
        nc = self.nc
        stats, mv = r.sb("stats", [NP, NT, 6]), r.sb("mv", [NP, NT, 2])
        for t in range(NT):
            own.fire(nc.vector.bn_stats(stats[:, t, :], src[:, t, :]))
        own.join()
        for t in range(NT):
            own.fire(nc.vector.bn_aggr(mv[:, t, :], stats[:, t, :]))
        own.join()
        return mv

    def normalise(self, name, src):
        nc, XH, XT = self.nc, self.XH, self.XT
        stack, r = self.stage(name)
        with stack:
            sd, rstd = r.sb("sd", [NP, NT]), r.sb("rstd", [NP, NT])
            tp = [r.ps(f"tp{k}", [128, 512]) for k in range(4)]
            own_dve = r.sem("own_dve")
            var_ready, sd_ready, rows_ready = r.sem("var_ready"), r.sem("sd_ready"), r.sem("rows_ready")
            turned, copied = r.sem("turned"), r.sem("copied")
            groups = [(t, min(t + 4, NT), c) for t in range(0, NT, 4) for c in range(KC)]
            block = stack.enter_context(nc.Block())

            @block.vector
            def _(dve):
                own = InOrder(dve, own_dve)
                mv = self.rows_statistics(dve, own, src, r)
                own(nc.vector.tensor_scalar_add(rstd[:], mv[:, :, 1], 1e-5))
                dve.sem_inc(var_ready, 1)
                dve.wait_ge(sd_ready, 1)
                own(nc.vector.reciprocal(rstd[:], sd[:]))
                for t in range(NT):
                    nc.vector.tensor_scalar(XH[:, t, :], src[:, t, :], mv[:, t, 0:1], rstd[:, t:t + 1],
                                            ALU.subtract, ALU.mult).then_inc(rows_ready, 1)

            @block.tensor
            def _(pe):
                for n, (a, b, c) in enumerate(groups):
                    pe.wait_ge(rows_ready, b)
                    if n >= 4:
                        pe.wait_ge(copied, n - 3)
                    for t in range(a, b):
                        last = nc.tensor.transpose(tp[n % 4][:, (t - a) * NP:(t - a + 1) * NP],
                                                   XH[:, t, c * 128:(c + 1) * 128], self.ident[0:NP, 0:NP])
                    last.then_inc(turned, 1)

            @block.scalar
            def _(act):
                act.wait_ge(var_ready, 1)
                nc.scalar.activation(sd[:], rstd[:], ACT.Sqrt).then_inc(sd_ready, 1)
                for n, (a, b, c) in enumerate(groups):
                    act.wait_ge(turned, n + 1)
                    nc.scalar.copy(XT[:, c, a * NP:b * NP], tp[n % 4][:, 0:(b - a) * NP]).then_inc(copied, 1)


    def split_keys(self, own, keys, quotient, hi, lo):
        nc = self.nc
        assert all(k * DIV_MUL >> DIV_SHIFT == k // NT for k in range(NODES))
        own(nc.vector.tensor_scalar(quotient[:], keys[:], DIV_MUL, None, ALU.mult))
        own(nc.vector.tensor_scalar(quotient[:], quotient[:], DIV_SHIFT, None, ALU.arith_shift_right))
        own(nc.vector.tensor_scalar(hi[:], quotient[:], float(NT), None, ALU.mult))
        own(nc.vector.tensor_tensor(lo[:], keys[:], hi[:], ALU.subtract))

    def one_hots(self, own, parts, hi, lo, at, hot_hi, hot_lo):
        nc = self.nc
        own.fire(nc.vector.tensor_tensor(
            hot_hi[:], bc(hi[:, bass.ds(at, HALF)].unsqueeze(2), (parts, HALF, NP)),
            bc(self.hi_values[0:parts, :].unsqueeze(1), (parts, HALF, NP)), ALU.is_equal))
        own.fire(nc.vector.tensor_tensor(
            hot_lo[:], bc(lo[:, bass.ds(at, HALF)].unsqueeze(2), (parts, HALF, NT)),
            bc(self.lo_values[0:parts, :].unsqueeze(1), (parts, HALF, NT)), ALU.is_equal))

    def count_keys(self, name, keys_dram, parts, cols, count, end):
        nc = self.nc
        stack, r = self.stage(name)
        with stack:
            keys = r.sb("keys", [parts, cols], I32)
            quotient = r.sb("quotient", [parts, cols], I32)
            hi, lo = r.sb("hi", [parts, cols]), r.sb("lo", [parts, cols])
            hot_hi = [r.sb(f"hot_hi{h}", [parts, HALF, NP], BF16) for h in range(2)]
            hot_lo = [r.sb(f"hot_lo{h}", [parts, HALF, NT], BF16) for h in range(2)]
            zero, within = r.sb("zero", [NP, NT]), r.sb("within", [NP, NT])
            total = r.ps("total", [NP, NT])
            turns = cols // STEP
            before = r.ps("before", [NP, 1])
            own_dve, loaded = r.sem("own_dve"), r.sem("loaded")
            built, counted = r.sem("built"), r.sem("counted")
            totals_ready, before_ready = r.sem("totals_ready"), r.sem("before_ready")
            block = stack.enter_context(nc.Block())

            @block.sync
            def _(sp):
                sp.dma_start(keys[:], keys_dram.rearrange("(p c) -> p c", c=cols)).then_inc(loaded, 16)
                sp.wait_ge(loaded, 16)

            @block.vector
            def _(dve):
                own = InOrder(dve, own_dve)
                own.fire(nc.vector.memset(zero[:], 0.0))
                dve.wait_ge(loaded, 16)
                self.split_keys(own, keys, quotient, hi, lo)

                def turn(i, first, last):
                    own.restart()
                    for h in range(2):
                        if not first:
                            dve.wait_ge(counted, 2 * i + h - 1)
                        self.one_hots(own, parts, hi, lo, STEP * i + HALF * h, hot_hi[h], hot_lo[h])
                        own.join()
                        dve.sem_inc(built, 1)

                loop(dve, turns, turn)
                own.restart()
                dve.wait_ge(counted, 2 * turns)
                own(nc.vector.tensor_copy(count[:], total[:]))
                own(nc.vector.tensor_tensor_scan(within[:], zero[:], count[:], 0.0, ALU.add, ALU.add))
                dve.sem_inc(totals_ready, 1)
                dve.wait_ge(before_ready, 1)
                own(nc.vector.tensor_scalar(end[:], within[:], before[:, 0:1], None, ALU.add))

            @block.tensor
            def _(pe):
                def turn(i, first, last):
                    for h in range(2):
                        pe.wait_ge(built, 2 * i + h + 1)
                        for k in range(HALF):
                            ins = nc.tensor.matmul(total[:], hot_hi[h][:, k, :], hot_lo[h][:, k, :],
                                                   start=(first and h == 0 and k == 0),
                                                   stop=(last and h == 1 and k == HALF - 1))
                        ins.then_inc(counted, 1)

                loop(pe, turns, turn)
                pe.wait_ge(totals_ready, 1)
                nc.tensor.matmul(before[:], self.upper[0:NP, 0:NP], within[:, NT - 1:NT],
                                 start=True, stop=True).then_inc(before_ready, 1)

    def sort_edges(self, name, keys_dram, others_dram, attr_dram, parts, cols, count, end, records):
        nc = self.nc
        row = ROW if attr_dram is not None else 2
        key_at, other_at = (KEY, OTHER) if attr_dram is not None else (0, 1)
        stack, r = self.stage(name)
        with stack:
            keys, others = r.sb("keys", [parts, cols], I32), r.sb("others", [parts, cols], I32)
            quotient = r.sb("quotient", [parts, cols], I32)
            hi, lo = r.sb("hi", [parts, cols]), r.sb("lo", [parts, cols])
            hot_hi = [r.sb(f"hot_hi{h}", [parts, HALF, NP], BF16) for h in range(2)]
            hot_lo = [r.sb(f"hot_lo{h}", [parts, HALF, NT], BF16) for h in range(2)]
            turned = [r.sb(f"turned{h}", [NP, HALF, parts]) for h in range(2)]
            earlier = r.sb("earlier", [parts, HALF, parts], BF16)
            running = [r.sb(f"running{h}", [NP, HALF + 1, NT]) for h in range(2)]
            picked = r.sb("picked", [parts, HALF, NT])
            placef = r.sb("placef", [parts, HALF])
            place = [r.sb(f"place{h}", [parts, HALF], I32) for h in range(2)]
            record = [r.sb(f"record{h}", [parts, HALF, row]) for h in range(2)]
            turned_ps = [r.ps(f"turned_ps{h}", [NP, HALF, 128], BF16) for h in range(2)]
            here_ps = [r.ps(f"here_ps{h}", [NP, HALF, NT]) for h in range(2)]
            same_ps = r.ps("same_ps", [parts, 2, 512])
            rank_ps = r.ps("rank_ps", [parts, HALF, NT])
            own_dve, own_act = r.sem("own_dve"), r.sem("own_act")
            loaded, built, turned_out, turned_in = (r.sem(n) for n in ("loaded", "built", "turned_out", "turned_in"))
            same_ready, earlier_ready, ranked = (r.sem(n) for n in ("same_ready", "earlier_ready", "ranked"))
            placed, filled, constants = r.sem("placed"), r.sem("filled"), r.sem("constants")
            started = r.sem("started")
            scattered = [self.moved_sem(f"{name}_scattered{h}") for h in range(2)]
            attr_in = [r.sem(f"attr_in{h}") for h in range(2)]
            rec_i = [record[h][:].bitcast(I32) for h in range(2)]
            turns = cols // STEP
            block = stack.enter_context(nc.Block())

            @block.sync
            def _(sp):
                sp.dma_start(keys[:], keys_dram.rearrange("(p c) -> p c", c=cols)).then_inc(loaded, 16)
                sp.dma_start(others[:], others_dram.rearrange("(p c) -> p c", c=cols)).then_inc(loaded, 16)
                if attr_dram is not None:
                    attr = attr_dram.rearrange("(p c) w -> p c w", c=cols)
                    sp.wait_ge(constants, 1)

                    def turn(i, first, last):
                        for h in range(2):
                            if not first:
                                sp.wait_ge(scattered[h], 16 * HALF * i)
                            sp.dma_start(record[h][:, :, 0:ATTR],
                                         attr[:, bass.ds(STEP * i + HALF * h, HALF), :]).then_inc(attr_in[h], 16)

                    loop(sp, turns, turn)

            @block.vector
            def _(dve):
                own = InOrder(dve, own_dve)
                if attr_dram is not None:
                    for h in range(2):
                        own.fire(nc.vector.memset(record[h][:], 0.0))
                    own.join()
                    for h in range(2):
                        own.fire(nc.vector.memset(record[h][:, :, ATTR:ATTR + 1], 1.0))
                    own.join()
                dve.sem_inc(constants, 1)
                dve.wait_ge(loaded, 32)
                self.split_keys(own, keys, quotient, hi, lo)
                own(nc.vector.tensor_tensor(running[1][:, HALF, :], end[:], count[:], ALU.subtract))

                def build(i, h):
                    self.one_hots(own, parts, hi, lo, STEP * i + HALF * h, hot_hi[h], hot_lo[h])
                    own.join()
                    dve.sem_inc(built, 1)

                def run_on(i, h):
                    dve.wait_ge(turned_out, 2 * i + h + 1)
                    own(nc.vector.tensor_copy(running[h][:, 0, :], running[1 - h][:, HALF, :]))
                    for k in range(HALF):
                        own(nc.vector.tensor_tensor(running[h][:, k + 1, :], running[h][:, k, :],
                                                    here_ps[h][:, k, :], ALU.add))

                build(0, 0)
                run_on(0, 0)

                def turn(i, first, last):
                    own.restart()
                    for h in range(2):
                        more = not (last and h == 1)
                        if more:
                            build(i + h, 1 - h)
                        dve.wait_ge(same_ready, 2 * i + h + 1)
                        for b in range(2):
                            own.fire(nc.vector.tensor_tensor(
                                earlier[:, 4 * b:4 * b + 4, :],
                                same_ps[:, b, 0:4 * parts].rearrange("q (k p) -> q k p", p=parts),
                                bc(self.upper[0:parts, 0:parts].unsqueeze(1), (parts, 4, parts)), ALU.mult))
                        own.join()
                        dve.sem_inc(earlier_ready, 1)
                        if more:
                            run_on(i + h, 1 - h)
                        dve.wait_ge(ranked, 2 * i + h + 1)
                        own(nc.vector.tensor_tensor(picked[:], rank_ps[:], hot_lo[h][:], ALU.mult))
                        own(nc.vector.tensor_reduce(placef[:], picked[:], AX.X, ALU.add))
                        if not first:
                            dve.wait_ge(scattered[h], 16 * HALF * i)
                        own(nc.vector.tensor_copy(place[h][:], placef[:]))
                        dve.sem_inc(placed, 1)

                loop(dve, turns, turn)

            @block.tensor
            def _(pe):
                def transpose_and_count(i, h):
                    pe.wait_ge(built, 2 * i + h + 1)
                    for k in range(HALF):
                        nc.tensor.transpose(turned_ps[h][:, k, 0:parts], hot_hi[h][:, k, :],
                                            self.identb[0:parts, 0:parts])
                    for k in range(HALF):
                        ins = nc.tensor.matmul(here_ps[h][:, k, :], hot_hi[h][:, k, :], hot_lo[h][:, k, :],
                                               start=True, stop=True)
                    ins.then_inc(turned_out, 1)

                transpose_and_count(0, 0)

                def turn(i, first, last):
                    for h in range(2):
                        pe.wait_ge(turned_in, 2 * i + h + 1)
                        for k in range(HALF):
                            ins = nc.tensor.matmul(same_ps[:, k // 4, (k % 4) * parts:(k % 4 + 1) * parts],
                                                   turned[h][:, k, :], turned[h][:, k, :], start=True, stop=True)
                        ins.then_inc(same_ready, 1)
                        if not (last and h == 1):
                            transpose_and_count(i + h, 1 - h)
                        pe.wait_ge(earlier_ready, 2 * i + h + 1)
                        for k in range(HALF):
                            nc.tensor.matmul(rank_ps[:, k, :], turned[h][:, k, :], running[h][:, k, :],
                                             start=True, stop=False)
                            ins = nc.tensor.matmul(rank_ps[:, k, :], earlier[:, k, :], hot_lo[h][:, k, :],
                                                   start=False, stop=True)
                        ins.then_inc(ranked, 1)

                loop(pe, turns, turn)

            @block.scalar
            def _(act):
                own = InOrder(act, own_act)
                act.wait_ge(constants, 1)
                act.wait_ge(loaded, 32)

                def copy_turned(i, h):
                    act.wait_ge(turned_out, 2 * i + h + 1)
                    own(nc.scalar.copy(turned[h][:], turned_ps[h][:, :, 0:parts]))
                    act.sem_inc(turned_in, 1)

                copy_turned(0, 0)

                def turn(i, first, last):
                    own.restart()
                    for h in range(2):
                        if not (last and h == 1):
                            if not (first and h == 0):
                                act.wait_ge(ranked, 2 * i + h)
                            copy_turned(i + h, 1 - h)
                        if not first:
                            act.wait_ge(scattered[h], 16 * HALF * i)
                        own.fire(nc.scalar.copy(rec_i[h][:, :, key_at], keys[:, bass.ds(STEP * i + HALF * h, HALF)]))
                        own(nc.scalar.copy(rec_i[h][:, :, other_at], others[:, bass.ds(STEP * i + HALF * h, HALF)]))
                        act.sem_inc(filled, 1)

                loop(act, turns, turn)

            @block.gpsimd
            def _(pool):
                with pool.Fori(0, turns) as i:
                    for h in range(2):
                        if attr_dram is not None:
                            pool.wait_ge(attr_in[h], 16 * i + 16)
                        pool.wait_ge(filled, 2 * i + h + 1)
                        pool.wait_ge(placed, 2 * i + h + 1)
                        pool.sem_inc(started, 1)
                        for k in range(HALF):
                            pool.indirect_dma_start(
                                records, bass.IndirectOffsetOnAxis(ap=place[h][:, k:k + 1], axis=0),
                                record[h][:, k, :], None).then_inc(scattered[h], 16)
                for h in range(2):
                    pool.wait_ge(scattered[h], 16 * HALF * turns)

    def describe_edges(self, e, first_dram, last_dram, count, end):
        nc, parts = self.nc, e.parts
        stack, r = self.stage(f"describe_{e.name}")
        with stack, nc.allow_non_contiguous_dma(reason="one word from each partition's range of edges"):
            ends = r.sb("ends", [parts, 3], I32)
            endf = r.sb("endf", [parts, 3])
            ones, diag = r.sb("ones", [parts, parts]), r.sb("diag", [parts, 2, parts])
            runs_on, last_edge = r.sb("runs_on", [parts, 2]), r.sb("last_edge", [NP, NT])
            rows = r.ps("rows", [parts, 2, parts])
            own_dve, blank, loaded, diag_ready, rows_ready = (
                r.sem(n) for n in ("own_dve", "blank", "loaded", "diag_ready", "rows_ready"))
            block = stack.enter_context(nc.Block())

            @block.sync
            def _(sp):
                sp.wait_ge(blank, 1)
                sp.dma_start(ends[:, 0:1], first_dram).then_inc(loaded, 16)
                sp.dma_start(ends[:, 1:2], last_dram).then_inc(loaded, 16)
                sp.dma_start(ends[0:parts - 1, 2:3], first_dram[1:parts, :]).then_inc(loaded, 16)
                sp.wait_ge(loaded, 48)

            @block.vector
            def _(dve):
                own = InOrder(dve, own_dve)
                own.fire(nc.vector.memset(ones[:], 1.0))
                own(nc.vector.memset(ends[:], -1))
                dve.sem_inc(blank, 1)
                dve.wait_ge(loaded, 48)
                own(nc.vector.tensor_copy(endf[:], ends[:]))
                own.fire(nc.vector.tensor_copy(e.first[:], endf[:, 0:1]))
                own.fire(nc.vector.tensor_copy(e.last[:], endf[:, 1:2]))
                for k in range(2):
                    own.fire(nc.vector.tensor_scalar(diag[:, k, :], self.ident[0:parts, 0:parts],
                                                     endf[:, k:k + 1], None, ALU.mult))
                own.fire(nc.vector.tensor_tensor(runs_on[:, 0:1], endf[:, 1:2], endf[:, 0:1], ALU.is_equal))
                own(nc.vector.tensor_tensor(runs_on[:, 1:2], endf[:, 2:3], endf[:, 1:2], ALU.is_equal))
                dve.sem_inc(diag_ready, 1)
                own(nc.vector.tensor_tensor(e.closes[:], runs_on[:, 0:1], runs_on[:, 1:2], ALU.mult))
                own(nc.vector.tensor_scalar(e.closes[:], e.closes[:], -1.0, 1.0, ALU.mult, ALU.add))
                dve.wait_ge(rows_ready, 1)
                own.fire(nc.vector.scalar_tensor_tensor(
                    out=e.after[:], in0=rows[:, 0, :], scalar=e.last[:, 0:1], in1=self.upper[0:parts, 0:parts],
                    op0=ALU.is_equal, op1=ALU.mult))
                own.fire(nc.vector.scalar_tensor_tensor(
                    out=e.before[:], in0=rows[:, 1, :], scalar=e.first[:, 0:1], in1=self.lower[0:parts, 0:parts],
                    op0=ALU.is_equal, op1=ALU.mult))
                own.fire(nc.vector.tensor_scalar_min(e.has[:], count[:], 1.0))
                own(nc.vector.tensor_scalar(last_edge[:], end[:], 1.0, 0.0, ALU.subtract, ALU.max))
                own(nc.vector.tensor_copy(e.end[:], last_edge[:]))

            @block.tensor
            def _(pe):
                pe.wait_ge(diag_ready, 1)
                nc.tensor.matmul(rows[:], ones[:], diag[:], start=True, stop=True).then_inc(rows_ready, 1)

    def out_degree_scale(self, count):
        nc = self.nc
        stack, r = self.stage("outdeg")
        with stack:
            deg = r.sb("deg", [NP, NT])
            own_dve, deg_ready, root_ready = r.sem("own_dve"), r.sem("deg_ready"), r.sem("root_ready")
            block = stack.enter_context(nc.Block())

            @block.vector
            def _(dve):
                own = InOrder(dve, own_dve)
                own(nc.vector.tensor_scalar_max(deg[:], count[:], 1.0))
                dve.sem_inc(deg_ready, 1)
                dve.wait_ge(root_ready, 1)
                own(nc.vector.reciprocal(self.isout[:], self.isout[:]))

            @block.scalar
            def _(act):
                act.wait_ge(deg_ready, 1)
                nc.scalar.activation(self.isout[:], deg[:], ACT.Sqrt).then_inc(root_ready, 1)

    def prepare_edges(self, room):
        nc, A = self.nc, self.A
        edges, gate_edges = A["src"].shape[0], A["L1_ffn_edge_index"].shape[1]
        self.by_dst = Edges(room, "by_dst", NP, edges // NP)
        self.by_src = Edges(room, "by_src", NP, edges // NP)
        self.by_gate = Edges(room, "by_gate", 128, gate_edges // 128)
        self.src_records = nc.dram_tensor("src_records", [edges, ROW], F32, kind="Internal").ap()
        self.gate_records = nc.dram_tensor("gate_records", [gate_edges, 2], F32, kind="Internal").ap()
        self.states = {}
        stack, r = self.stage("prep")
        with stack:
            cols = edges // NP
            gate_cols = gate_edges // 128
            gate_src, gate_dst = A["L1_ffn_edge_index"][0], A["L1_ffn_edge_index"][1]
            tiles = [(r.sb(f"count{k}", [NP, NT]), r.sb(f"end{k}", [NP, NT])) for k in range(3)]
            self.count_keys("count_dst", A["dst"], NP, cols, *tiles[0])
            view = A["dst"].rearrange("(p c) -> p c", c=cols)
            self.describe_edges(self.by_dst, view[:, 0:1], view[:, cols - 1:cols], *tiles[0])
            self.count_keys("count_src", A["src"], NP, cols, *tiles[1])
            self.out_degree_scale(tiles[1][0])
            self.sort_edges("sort_src", A["src"], A["dst"], A["edge_attr_18"], NP, cols, *tiles[1], self.src_records)
            view = self.src_records.bitcast(I32).rearrange("(p c) w -> p c w", c=cols)
            self.describe_edges(self.by_src, view[:, 0, KEY:KEY + 1], view[:, cols - 1, KEY:KEY + 1], *tiles[1])
            self.count_keys("count_gate", gate_dst, 128, gate_cols, *tiles[2])
            self.sort_edges("sort_gate", gate_dst, gate_src, None, 128, gate_cols, *tiles[2], self.gate_records)
            view = self.gate_records.bitcast(I32).rearrange("(p c) w -> p c w", c=gate_cols)
            self.describe_edges(self.by_gate, view[:, 0, 0:1], view[:, gate_cols - 1, 0:1], *tiles[2])

    def load_weight(self, sp, sem, dst, dram):
        sp.dma_start(dst, dram.rearrange("(c k) n -> k c n", k=128)).then_inc(sem, 16)

    def project(self, name, jobs, tables=()):
        nc = self.nc
        stack, r = self.stage(name)
        with stack:
            ps = [r.ps(f"ps{k}", [NP, 512]) for k in range(6)]
            done, stored = r.sem("done"), r.sem("stored")
            by_dve, by_act = r.sem("by_dve"), r.sem("by_act")
            plan, counts = [], {True: 0, False: 0}
            for t in range(NT):
                for w, b, out, view in jobs:
                    on_dve = b is not None
                    counts[on_dve] += 1
                    plan.append((t, w, b, out, view, on_dve, counts[on_dve]))
            block = stack.enter_context(nc.Block())

            @block.tensor
            def _(pe):
                for n, (t, w, _, _, _, _, _) in enumerate(plan):
                    if n >= 6:
                        pe.wait_ge(by_dve if plan[n - 6][5] else by_act, plan[n - 6][6])
                    parts = [(xt[:, c, t * NP:(t + 1) * NP], wt[:, c, :]) for xt, wt in w for c in range(KC)]
                    for k, (lhsT, rhs) in enumerate(parts):
                        last = nc.tensor.matmul(ps[n % 6][:, 0:rhs.shape[1]], lhsT, rhs,
                                                start=(k == 0), stop=(k == len(parts) - 1))
                    last.then_inc(done, 1)

            @block.vector
            def _(dve):
                for n, (t, w, b, out, view, on_dve, _) in enumerate(plan):
                    if on_dve:
                        dve.wait_ge(done, n + 1)
                        nc.vector.tensor_tensor(out(t), view(ps[n % 6][:, 0:w[0][1].shape[2]]), view(b),
                                                ALU.add).then_inc(by_dve, 1)

            @block.scalar
            def _(act):
                for n, (t, w, b, out, view, on_dve, _) in enumerate(plan):
                    if not on_dve:
                        act.wait_ge(done, n + 1)
                        nc.scalar.copy(out(t), view(ps[n % 6][:, 0:w[0][1].shape[2]])).then_inc(by_act, 1)

            @block.sync
            def _(sp):
                if counts[True]:
                    sp.wait_ge(by_dve, counts[True])
                if counts[False]:
                    sp.wait_ge(by_act, counts[False])
                for dram, tab in tables:
                    sp.dma_start(dram.rearrange("(p t) w -> p t w", t=NT), tab[:]).then_inc(stored, 16)
                if tables:
                    sp.wait_ge(stored, 16 * len(tables))

    def table(self, name, width):
        return self.nc.dram_tensor(name, [NODES, width], F32, kind="Internal").ap()

    def stream(self, name, e, heads, values, other_table, key_table, last_state, kind, extra=None):
        nc, A, parts, cols = self.nc, self.A, e.parts, e.cols
        width, other_w = values + heads, other_table.shape[1]
        key_w = key_table.shape[1] if key_table is not None else 0
        each = values // heads if heads else values
        self.states[name] = states = nc.dram_tensor(f"{name}_states", [parts * cols, width], F32, kind="Internal").ap()
        states_v = states.rearrange("(p c) w -> p c w", c=cols)
        turns = cols // STEP
        stack, r = self.stage(name)
        with stack:
            two = range(2)
            if e is self.by_dst:
                picks = [r.sb(f"picks{h}", [parts, 3, HALF], I32) for h in two]
                sources = [A["dst"], A["src"]] + ([A["edge_type_64"]] if kind == "relation" else [])
                sources = [s.rearrange("(p c) -> p c", c=cols) for s in sources]
                key_of = [picks[h][:, 0, :] for h in two]
                key_index = [lambda k, h=h: picks[h][:, 0, k:k + 1] for h in two]
                other_index = [lambda k, h=h: picks[h][:, 1, k:k + 1] for h in two]
                type_of = [picks[h][:, 2, :] for h in two]
                loads = [lambda at, h, n=n: (picks[h][:, n, :], sources[n][:, bass.ds(at, HALF)])
                         for n in range(len(sources))]
            else:
                dram, row = (self.src_records, ROW) if e is self.by_src else (self.gate_records, 2)
                key_at, other_at = (KEY, OTHER) if e is self.by_src else (0, 1)
                record = [r.sb(f"record{h}", [parts, HALF, row]) for h in two]
                records_v = dram.rearrange("(p c) w -> p c w", c=cols)
                key_of = [record[h][:].bitcast(I32)[:, :, key_at] for h in two]
                key_index = [lambda k, h=h: record[h][:].bitcast(I32)[:, k, key_at:key_at + 1] for h in two]
                other_index = [lambda k, h=h: record[h][:].bitcast(I32)[:, k, other_at:other_at + 1] for h in two]
                loads = [lambda at, h: (record[h][:], records_v[:, bass.ds(at, HALF), :])]
            other = [r.sb(f"other{h}", [parts, HALF, other_w]) for h in two]
            keyrow = [r.sb(f"keyrow{h}", [parts, HALF, key_w]) for h in two] if key_w else None
            state = [r.sb(f"state{h}", [parts, HALF, width]) for h in two]
            keyf = [r.sb(f"keyf{h}", [parts, HALF + 1]) for h in two]
            same = r.sb("same", [parts, HALF])
            if heads:
                score = r.sb("score", [parts, heads, SPAN])
                reach = r.sb("reach", [parts, heads, SPAN])
                most = r.sb("most", [parts, heads, SPAN])
                opens = r.sb("opens", [parts, heads * SPAN + 1])
                grown = r.sb("grown", [parts, heads, SPAN])
                factor = r.sb("factor", [parts, heads, SPAN])
                by_column = score[:, :, 1:].rearrange("p h k -> p k h")
                scaled = r.sb("scaled", [parts, values])
            looks = kind in ("relation", "additive")
            if kind == "relation":
                product = r.sb("product", [parts, HALF, D])
                typef, hot = r.sb("typef", [parts, HALF]), r.sb("hot", [parts, HALF, 64], BF16)
                groups, rows, per = HALF // 2, 128, 2
                found = r.ps("found", [parts, 2, HALF // 2, D])
            if kind == "additive":
                table_w = NT * heads
                picked = r.sb("picked", [parts, HALF, NT, heads])
                key_score = r.sb("key_score", [parts, HALF, heads])
                key_rows = r.sb("key_rows", [parts, cols, 1 if e is self.by_dst else 2], I32)
                keys, quotient = r.sb("keys", [parts, cols], I32), r.sb("quotient", [parts, cols], I32)
                hi, lo = r.sb("hi", [parts, cols]), r.sb("lo", [parts, cols])
                hot, hot_lo = r.sb("hot", [parts, HALF, NP], BF16), r.sb("hot_lo", [parts, HALF, NT])
                groups, rows, per = HALF, NP, 1
                found = r.ps("found", [parts, HALF, 128])
            if looks:
                hot_ps, hot_t = r.ps("hot_ps", [rows, groups, 128], BF16), r.sb("hot_t", [rows, groups, 128])
                hot_ready, turned, turned_in, found_ready, found_used, keys_in = (
                    r.sem(n) for n in ("hot_ready", "turned", "turned_in", "found_ready", "found_used", "keys_in"))
            if kind == "attributes":
                product = r.sb("product", [parts, HALF, 128])
                query = r.sb("query", [parts, HALF, 128])
                attr_ps = r.ps("attr_ps", [128, 2, 128])
                attr_t = [r.sb(f"attr_t{h}", [128, 2, 128]) for h in two]
                rpe_ps = r.ps("rpe_ps", [parts, 4, 2, 256])
                turned, turned_in, rpe_ready, rpe_used = (
                    r.sem(n) for n in ("turned", "turned_in", "rpe_ready", "rpe_used"))
            own_dve, started, picked_up = r.sem("own_dve"), r.sem("started"), [r.sem(f"picked_up{h}") for h in two]
            picks_in = [r.sem(f"picks_in{h}") for h in two]
            gathered = [self.moved_sem(f"{name}_gathered{h}") for h in two]
            rows_used = [r.sem(f"rows_used{h}") for h in two]
            args_ready, factors_ready = r.sem("args_ready"), r.sem("factors_ready")
            state_ready = [r.sem(f"state_ready{h}") for h in two]
            stored = [r.sem(f"stored{h}") for h in two]
            tables = 1 + (key_w > 0)
            block = stack.enter_context(nc.Block())

            @block.gpsimd
            def _(pool):
                def turn(i, first, last):
                    for h in two:
                        pool.wait_ge(picks_in[h], 16 * len(loads) * (i + 1))
                        if not first:
                            pool.wait_ge(rows_used[h], i)
                        pool.sem_inc(started, 1)
                        for k in range(HALF):
                            pool.indirect_dma_start(
                                other[h][:, k, :], None, other_table,
                                bass.IndirectOffsetOnAxis(ap=other_index[h](k), axis=0)).then_inc(gathered[h], 16)
                            if key_w:
                                pool.indirect_dma_start(
                                    keyrow[h][:, k, :], None, key_table,
                                    bass.IndirectOffsetOnAxis(ap=key_index[h](k), axis=0)).then_inc(gathered[h], 16)
                loop(pool, turns, turn)

            @block.scalar
            def _(act):
                def load(i, h):
                    for f in loads:
                        to, of = f(STEP * i + HALF * h, h)
                        act.dma_start(to, of).then_inc(picks_in[h], 16)

                def copy_hot(n):
                    act.wait_ge(turned, n + 1)
                    nc.scalar.copy(hot_t[:, :, 0:parts], hot_ps[:, :, 0:parts]).then_inc(turned_in, 1)

                for h in two:
                    load(0, h)
                if looks:
                    copy_hot(0)

                def turn(i, first, last):
                    for h in two:
                        if kind == "attributes":
                            act.wait_ge(turned, 2 * i + h + 1)
                            nc.scalar.copy(attr_t[h][:, :, 0:parts], attr_ps[:, :, 0:parts]).then_inc(turned_in, 1)
                        if not last:
                            act.wait_ge(picked_up[h], i + 1)
                            load(i + 1, h)
                        if heads:
                            act.wait_ge(args_ready, 2 * i + h + 1)
                            nc.scalar.activation(factor[:], grown[:], ACT.Exp).then_inc(factors_ready, 1)
                        if looks and not (last and h == 1):
                            copy_hot(2 * i + h + 1)
                loop(act, turns, turn)

            @block.sync
            def _(sp):
                if kind == "additive":
                    source = A["dst"].rearrange("(p c w) -> p c w", c=cols, w=1) if e is self.by_dst \
                        else records_v.bitcast(I32)
                    sp.dma_start(key_rows[:], source).then_inc(keys_in, 16)

                def turn(i, first, last):
                    for h in two:
                        sp.wait_ge(state_ready[h], i + 1)
                        sp.dma_start(states_v[:, bass.ds(STEP * i + HALF * h, HALF), :], state[h][:])\
                          .then_inc(stored[h], 16)
                loop(sp, turns, turn)
                for h in two:
                    sp.wait_ge(stored[h], 16 * turns)

            @block.vector
            def _(dve):
                own = InOrder(dve, own_dve)
                tt, ts, stt = nc.vector.tensor_tensor, nc.vector.tensor_scalar, nc.vector.scalar_tensor_tensor
                own.fire(nc.vector.memset(keyf[1][:, HALF:HALF + 1], -1.0))
                own.fire(nc.vector.memset(state[1][:, HALF - 1, :], 0.0))
                if heads:
                    own.fire(nc.vector.memset(opens[:], -BIG))
                own.join()

                def build_hot(i, h):
                    if kind == "relation":
                        dve.wait_ge(picks_in[h], 16 * len(loads) * (i + 1))
                        own(nc.vector.tensor_copy(typef[:], type_of[h]))
                        own(tt(hot[:], bc(typef[:].unsqueeze(2), (parts, HALF, 64)),
                               bc(self.small[0:parts, :].unsqueeze(1), (parts, HALF, 64)), ALU.is_equal))
                    else:
                        self.one_hots(own, parts, hi, lo, STEP * i + HALF * h, hot, hot_lo)
                        own.join()
                    dve.sem_inc(hot_ready, 1)

                def relation_scores(i, h):
                    dve.wait_ge(found_ready, 2 * (2 * i + h + 1))
                    own(tt(product[:].rearrange("p (q a) w -> p a q w", a=2),
                           other[h][:, :, values:values + D].rearrange("p (q a) w -> p a q w", a=2),
                           found[:], ALU.add))
                    dve.sem_inc(found_used, 1)
                    own(tt(product[:], product[:], keyrow[h][:], ALU.mult))
                    own(nc.vector.tensor_reduce(by_column, product[:].rearrange("p k (h d) -> p k h d", h=heads),
                                                AX.X, ALU.add))

                def attribute_scores(i, h):
                    dve.wait_ge(rpe_ready, 4 * (2 * i + h + 1))
                    rpe = rpe_ps[:].rearrange("p q a w -> p a q w")

                    def by_four(ap):
                        return ap.rearrange("p (a q) w -> p a q w", q=4)

                    own.fire(tt(by_four(query[:]), by_four(keyrow[h][:]), rpe[:, :, :, 0:128], ALU.add))
                    own(tt(by_four(product[:]), by_four(other[h][:, :, values:values + 128]),
                           rpe[:, :, :, 128:256], ALU.add))
                    dve.sem_inc(rpe_used, 1)
                    own(tt(product[:], product[:], query[:], ALU.mult))
                    own(nc.vector.tensor_reduce(by_column, product[:].rearrange("p k (h d) -> p k h d", h=heads),
                                                AX.X, ALU.add))

                def additive_scores(i, h):
                    dve.wait_ge(found_ready, 2 * i + h + 1)
                    own(tt(picked[:], found[:, :, 0:table_w].rearrange("p k (t h) -> p k t h", h=heads),
                           bc(hot_lo[:].unsqueeze(3), (parts, HALF, NT, heads)), ALU.mult))
                    dve.sem_inc(found_used, 1)
                    own(nc.vector.tensor_reduce(key_score[:], picked[:].rearrange("p k t h -> p k h t"), AX.X, ALU.add))
                    own(tt(by_column, other[h][:, :, values:values + heads], key_score[:], ALU.add))
                    own(stt(out=by_column, in0=by_column, scalar=0.2, in1=by_column, op0=ALU.mult, op1=ALU.max))

                if kind == "additive":
                    dve.wait_ge(keys_in, 16)
                    own(nc.vector.tensor_copy(keys[:], key_rows[:, :, 0]))
                    self.split_keys(own, keys, quotient, hi, lo)
                    own.join()
                if looks:
                    build_hot(0, 0)

                def turn(i, first, last):
                    own.restart()
                    for h in two:
                        now, before = state[h], state[1 - h]
                        dve.wait_ge(gathered[h], 16 * HALF * tables * (i + 1))
                        own.fire(nc.vector.tensor_copy(keyf[h][:, 0:1], keyf[1 - h][:, HALF:HALF + 1]))
                        own(nc.vector.tensor_copy(keyf[h][:, 1:HALF + 1], key_of[h]))
                        own(tt(same[:], keyf[h][:, 1:HALF + 1], keyf[h][:, 0:HALF], ALU.is_equal))
                        if heads:
                            own.fire(ts(opens[:, 0:heads * SPAN].rearrange("p (h k) -> p h k", k=SPAN)[:, :, 1:],
                                        bc(same[:].unsqueeze(1), (parts, heads, HALF)), BIG, -BIG, ALU.mult, ALU.add))
                            own.fire(nc.vector.tensor_copy(score[:, :, 0], before[:, HALF - 1, values:width]))
                        if kind == "relation":
                            relation_scores(i, h)
                        elif kind == "attributes":
                            attribute_scores(i, h)
                        elif kind == "additive":
                            additive_scores(i, h)
                        own.join()
                        dve.sem_inc(picked_up[h], 1)
                        if looks and not (last and h == 1):
                            build_hot(i + h, 1 - h)
                        if not first:
                            dve.wait_ge(stored[h], 16 * i)
                        if heads:
                            flat = [ap[:].rearrange("p h k -> p (h k)") for ap in (score, reach, most)]
                            size = heads * SPAN
                            own(nc.vector.tensor_tensor_scan(flat[1], opens[:, 0:size], flat[0], 0.0, ALU.add, ALU.max))
                            own(nc.vector.tensor_tensor_scan(flat[2][:, ::-1], opens[:, 1:size + 1][:, ::-1],
                                                             flat[1][:, ::-1], 0.0, ALU.add, ALU.max))
                            own.fire(stt(out=grown[:, :, 0], in0=score[:, :, 0], scalar=opens[:, 1:2],
                                         in1=most[:, :, 1], op0=ALU.add, op1=ALU.subtract))
                            own.fire(tt(grown[:, :, 1:], score[:, :, 1:], most[:, :, 1:], ALU.subtract))
                            own.fire(nc.vector.tensor_copy(now[:, :, values:width],
                                                           most[:, :, 1:].rearrange("p h k -> p k h")))
                            own.join()
                            dve.sem_inc(args_ready, 1)
                            dve.wait_ge(factors_ready, 2 * i + h + 1)
                            own.fire(tt(now[:, :, 0:values].rearrange("p k (h d) -> p k h d", d=each),
                                        other[h][:, :, 0:values].rearrange("p k (h d) -> p k h d", d=each),
                                        bc(factor[:, :, 1:].rearrange("p h k -> p k h").unsqueeze(3), (parts, HALF, heads, each)),
                                        ALU.mult))
                            own.fire(tt(scaled[:].rearrange("p (h d) -> p h d", d=each),
                                        before[:, HALF - 1, 0:values].rearrange("p (h d) -> p h d", d=each),
                                        bc(factor[:, :, 0:1], (parts, heads, each)), ALU.mult))
                            own.join()
                            dve.sem_inc(rows_used[h], 1)
                            own(tt(now[:, 0, 0:values], now[:, 0, 0:values], scaled[:], ALU.add))
                            for k in range(1, HALF):
                                own(stt(out=now[:, k, 0:values], in0=now[:, k - 1, 0:values], scalar=same[:, k:k + 1],
                                        in1=now[:, k, 0:values], op0=ALU.mult, op1=ALU.add))
                        else:
                            for k in range(HALF):
                                prev = before[:, HALF - 1, :] if k == 0 else now[:, k - 1, :]
                                own(stt(out=now[:, k, :], in0=prev, scalar=same[:, k:k + 1], in1=other[h][:, k, :],
                                        op0=ALU.mult, op1=ALU.add))
                            dve.sem_inc(rows_used[h], 1)
                        dve.sem_inc(state_ready[h], 1)
                loop(dve, turns, turn)
                own.restart()
                own(nc.vector.tensor_copy(last_state[:], state[1][:, HALF - 1, :]))

            if looks:
                @block.tensor
                def _(pe):
                    def turn(i, first, last):
                        for h in two:
                            n = 2 * i + h
                            pe.wait_ge(hot_ready, n + 1)
                            if not (first and h == 0):
                                pe.wait_ge(turned_in, n)
                            flat = hot[:].rearrange("p k w -> p (k w)")
                            for g in range(groups):
                                last_ = nc.tensor.transpose(hot_ps[:, g, 0:parts], flat[:, rows * g:rows * (g + 1)],
                                                            self.identb[0:parts, 0:parts])
                            last_.then_inc(turned, 1)
                            pe.wait_ge(turned_in, n + 1)
                            if not (first and h == 0):
                                pe.wait_ge(found_used, n)
                            for k in range(HALF):
                                if kind == "relation":
                                    q = 64 * (k % 2)
                                    last_ = nc.tensor.matmul(found[:, k % 2, k // 2, :], hot_t[q:q + 64, k // 2, 0:parts],
                                                             extra[q:q + 64, :], start=True, stop=True)
                                else:
                                    last_ = nc.tensor.matmul(found[:, k, 0:table_w], hot_t[:, k, 0:parts],
                                                             extra, start=True, stop=True)
                                if k >= HALF - per:
                                    last_.then_inc(found_ready, 1)
                    loop(pe, turns, turn)

            if kind == "attributes":
                @block.tensor
                def _(pe):
                    def turn(i, first, last):
                        for h in two:
                            pe.wait_ge(picks_in[h], 16 * len(loads) * (i + 1))
                            if not (first and h == 0):
                                pe.wait_ge(turned_in, 2 * i + h)
                            for b in two:
                                flat = record[h][:].rearrange("p k w -> p (k w)")[:, 128 * b:128 * b + 128]
                                last_ = nc.tensor.transpose(attr_ps[:, b, 0:parts], flat, self.ident[0:parts, 0:parts])
                            last_.then_inc(turned, 1)
                            pe.wait_ge(turned_in, 2 * i + h + 1)
                            if not (first and h == 0):
                                pe.wait_ge(rpe_used, 2 * i + h)
                            for k in range(HALF):
                                q = 32 * (k % 4)
                                last_ = nc.tensor.matmul(rpe_ps[:, k % 4, k // 4, :], attr_t[h][q:q + ATTR + 1, k // 4, 0:parts],
                                                         extra[q:q + ATTR + 1, :], start=True, stop=True)
                                if k >= HALF - 4:
                                    last_.then_inc(rpe_ready, 1)
                    loop(pe, turns, turn)

    def merge(self, name, e, heads, values, last_state, nodes, own_rows=None, own_score=None):
        nc, parts = self.nc, e.parts
        width = values + heads
        each = values // heads if heads else values
        stack, r = self.stage(f"{name}_merge")
        with stack:
            carried = r.sb("carried", [NP, NT, width + 1])
            number = r.sb("number", [parts, NT, NP])
            takes = r.sb("takes", [parts, NT, NP])
            carry = r.sb("carry", [parts, width + 1])
            ones = r.sb("ones", [parts, parts])
            spread = r.ps("spread", [parts, 4, 512])
            carry_ps = r.ps("carry_ps", [parts, values])
            node_ps = [r.ps(f"node_ps{k}", [NP, width + 1]) for k in range(2)]
            if heads:
                diag = r.sb("diag", [parts, heads, parts])
                shut = r.sb("shut", [parts, 2, parts])
                arg, weight = r.sb("arg", [parts, heads, parts]), r.sb("weight", [parts, heads, parts])
                top = r.sb("top", [parts, heads])
                sources = 3 if own_rows is not None else 2
                tops = r.sb("tops", [NP, sources, NT, heads])
                best = r.sb("best", [NP, NT, heads])
                shares = r.sb("shares", [NP, sources, NT, heads])
                absent = r.sb("absent", [NP, 2, NT])
            sems = ("own_dve", "numbered", "diag_ready", "spread_ready", "arg_ready", "weight_ready",
                    "carry_ready", "carry_out", "node_out", "node_in", "tops_ready", "shares_ready")
            s = {n: r.sem(n) for n in sems}
            s["gathered"] = self.moved_sem(f"{name}_gathered_ends")
            groups = [(a, min(a + 4, heads)) for a in range(0, heads, 4)]
            block = stack.enter_context(nc.Block())

            @block.gpsimd
            def _(pool):
                pool.iota(number[:], [[1, NT], [NT, NP]], base=0, channel_multiplier=0,
                          allow_small_or_imprecise_dtypes=True).then_inc(s["numbered"], 1)
                for t in range(NT):
                    pool.indirect_dma_start(nodes[:, t, :], None, self.states[name],
                                            bass.IndirectOffsetOnAxis(ap=e.end[:, t:t + 1], axis=0))\
                        .then_inc(s["gathered"], 16)

            @block.vector
            def _(dve):
                own = InOrder(dve, s["own_dve"])
                tt, ts, stt = nc.vector.tensor_tensor, nc.vector.tensor_scalar, nc.vector.scalar_tensor_tensor
                own.fire(nc.vector.memset(ones[:], 1.0))
                own.fire(nc.vector.memset(carry[:], 1.0))
                if heads:
                    m_last = last_state[:, values:width]
                    eye = bc(self.ident[0:parts, 0:parts].unsqueeze(1), (parts, heads, parts))
                    own(tt(diag[:], eye, bc(m_last.unsqueeze(2), (parts, heads, parts)), ALU.mult))
                    dve.sem_inc(s["diag_ready"], 1)
                    own.fire(ts(shut[:, 0, :], e.before[:], BIG, -BIG, ALU.mult, ALU.add))
                    own(ts(shut[:, 1, :], e.after[:], 2 * BIG, -2 * BIG, ALU.mult, ALU.add))
                    dve.wait_ge(s["spread_ready"], 1)
                    for n, (a, b) in enumerate(groups):
                        own.fire(tt(arg[:, a:b, :], spread[:, n, 0:(b - a) * parts].rearrange("p (h q) -> p h q", q=parts),
                                    bc(shut[:, 0, :].unsqueeze(1), (parts, b - a, parts)), ALU.add))
                    own.join()
                    own(nc.vector.tensor_reduce(top[:], arg[:], AX.X, ALU.max))
                    own(tt(diag[:], eye, bc(top[:].unsqueeze(2), (parts, heads, parts)), ALU.mult))
                    dve.sem_inc(s["diag_ready"], 1)
                    dve.wait_ge(s["spread_ready"], 2)
                    for n, (a, b) in enumerate(groups):
                        own.fire(stt(out=arg[:, a:b, :],
                                     in0=spread[:, n, 0:(b - a) * parts].rearrange("p (h q) -> p h q", q=parts),
                                     scalar=-1.0, in1=bc(shut[:, 1, :].unsqueeze(1), (parts, b - a, parts)),
                                     op0=ALU.mult, op1=ALU.add))
                    own.join()
                    own(tt(arg[:], arg[:], bc(m_last.unsqueeze(2), (parts, heads, parts)), ALU.add))
                    dve.sem_inc(s["arg_ready"], 1)
                dve.wait_ge(s["carry_out"], 1)
                own.join()
                own.fire(nc.vector.tensor_copy(carry[:, 0:values], carry_ps[:]))
                if heads:
                    own.fire(nc.vector.tensor_copy(carry[:, values:width], top[:]))
                dve.wait_ge(s["numbered"], 1)
                own.fire(ts(takes[:], number[:], e.first[:, 0:1], e.closes[:, 0:1], ALU.is_equal, ALU.mult))
                own.join()
                dve.sem_inc(s["carry_ready"], 1)
                dve.wait_ge(s["gathered"], 16 * NT)
                dve.wait_ge(s["node_in"], NT)
                if heads:
                    own.fire(ts(absent[:, 0, :], e.has[:], BIG, -BIG, ALU.mult, ALU.add))
                    own(ts(absent[:, 1, :], carried[:, :, width], BIG, -BIG, ALU.mult, ALU.add))
                    own.fire(tt(tops[:, 0, :, :], nodes[:, :, values:width],
                                bc(absent[:, 0, :].unsqueeze(2), (NP, NT, heads)), ALU.add))
                    own.fire(tt(tops[:, 1, :, :], carried[:, :, values:width],
                                bc(absent[:, 1, :].unsqueeze(2), (NP, NT, heads)), ALU.add))
                    if own_rows is not None:
                        own.fire(nc.vector.tensor_copy(tops[:, 2, :, :], own_score[:]))
                    own.join()
                    own(tt(best[:], tops[:, 0, :, :], tops[:, 1, :, :], ALU.max))
                    if own_rows is not None:
                        own(tt(best[:], best[:], tops[:, 2, :, :], ALU.max))
                    for k in range(sources):
                        own.fire(tt(tops[:, k, :, :], tops[:, k, :, :], best[:], ALU.subtract))
                    own.join()
                    dve.sem_inc(s["tops_ready"], 1)
                    dve.wait_ge(s["shares_ready"], 1)

                    def heads_of(ap):
                        return ap.rearrange("p t (h d) -> p t h d", d=each)

                    def share(k):
                        return bc(shares[:, k, :, :].unsqueeze(3), (NP, NT, heads, each))

                    mine, theirs = heads_of(nodes[:, :, 0:values]), heads_of(carried[:, :, 0:values])
                    own.fire(tt(mine, mine, share(0), ALU.mult))
                    own(tt(theirs, theirs, share(1), ALU.mult))
                    own(tt(mine, mine, theirs, ALU.add))
                    if own_rows is not None:
                        own(tt(theirs, heads_of(own_rows), share(2), ALU.mult))
                        own(tt(mine, mine, theirs, ALU.add))
                else:
                    own(tt(nodes[:], nodes[:], bc(e.has[:].unsqueeze(2), (NP, NT, values)), ALU.mult))
                    own(tt(nodes[:], nodes[:], carried[:, :, 0:values], ALU.add))

            @block.tensor
            def _(pe):
                if heads:
                    for n in range(2):
                        pe.wait_ge(s["diag_ready"], n + 1)
                        for b, (a, z) in enumerate(groups):
                            last = nc.tensor.matmul(spread[:, b, 0:(z - a) * parts], ones[:], diag[:, a:z, :],
                                                    start=True, stop=True)
                        last.then_inc(s["spread_ready"], 1)
                    pe.wait_ge(s["weight_ready"], 1)
                    for h in range(heads):
                        last = nc.tensor.matmul(carry_ps[:, each * h:each * (h + 1)], weight[:, h, :],
                                                last_state[:, each * h:each * (h + 1)], start=True, stop=True)
                else:
                    last = nc.tensor.matmul(carry_ps[:], e.after[:], last_state[:], start=True, stop=True)
                last.then_inc(s["carry_out"], 1)
                pe.wait_ge(s["carry_ready"], 1)
                for t in range(NT):
                    if t >= 2:
                        pe.wait_ge(s["node_in"], t - 1)
                    nc.tensor.matmul(node_ps[t % 2][:], takes[:, t, :], carry[:], start=True, stop=True)\
                        .then_inc(s["node_out"], 1)

            @block.scalar
            def _(act):
                if heads:
                    act.wait_ge(s["arg_ready"], 1)
                    nc.scalar.activation(weight[:], arg[:], ACT.Exp).then_inc(s["weight_ready"], 1)
                for t in range(NT):
                    act.wait_ge(s["node_out"], t + 1)
                    nc.scalar.copy(carried[:, t, :], node_ps[t % 2][:]).then_inc(s["node_in"], 1)
                if heads:
                    act.wait_ge(s["tops_ready"], 1)
                    nc.scalar.activation(shares[:], tops[:], ACT.Exp).then_inc(s["shares_ready"], 1)

    def additive_attention(self, name, e, w_dram, att_src, att_dst, heads, dim, result):
        nc = self.nc
        values = heads * (dim + 1)
        cols = heads * dim
        other = self.table(f"{name}_other", values + heads)
        stack, r = self.stage(name)
        with stack:
            tab, keytab = r.sb("tab", [NP, NT, values + heads]), r.sb("keytab", [NP, NT, heads])
            own_score = r.sb("own_score", [NP, NT, heads])
            last_state = r.sb("last_state", [e.parts, values + heads])
            weights_stack, w = self.stage(f"{name}_w")
            with weights_stack:
                wcat = w.sb("wcat", [128, KC, cols + 2 * heads])
                att = w.sb("att", [128, 2, cols])
                weighed = w.sb("weighed", [128, 2, KC, cols])
                inner, v = self.stage(f"{name}_fold")
                with inner:
                    loaded, own_dve = v.sem("loaded"), v.sem("own_dve")
                    block = inner.enter_context(nc.Block())

                    @block.sync
                    def _(sp):
                        self.load_weight(sp, loaded, wcat[:, :, 0:cols], w_dram)
                        for k, a in enumerate((att_src, att_dst)):
                            sp.dma_start(att[:, k, :], a.partition_broadcast(128)).then_inc(loaded, 16)

                    @block.vector
                    def _(dve):
                        own = InOrder(dve, own_dve)
                        own.fire(nc.vector.memset(tab[:], 1.0))
                        dve.wait_ge(loaded, 48)
                        for k in range(2):
                            own.fire(nc.vector.tensor_tensor(weighed[:, k, :, :], wcat[:, :, 0:cols],
                                                             bc(att[:, k, :].unsqueeze(1), (128, KC, cols)), ALU.mult))
                        own.join()
                        for k in range(2):
                            own.fire(nc.vector.tensor_reduce(
                                wcat[:, :, cols + heads * k:cols + heads * (k + 1)],
                                weighed[:, k, :, :].rearrange("p c (h d) -> p c h d", d=dim), AX.X, ALU.add))
                        own.join()

                def put(t):
                    return tab[:, t, 0:values].rearrange("p (h d) -> p h d", d=dim + 1)[:, :, 0:dim]

                self.project(f"{name}_proj", [
                    ([(self.XT, wcat[:, :, 0:cols])], None, put, lambda ap: ap.rearrange("p (h d) -> p h d", d=dim)),
                    ([(self.XT, wcat[:, :, cols:cols + heads])], None, lambda t: tab[:, t, values:values + heads], lambda ap: ap),
                    ([(self.XT, wcat[:, :, cols + heads:])], None, lambda t: keytab[:, t, :], lambda ap: ap),
                ], [(other, tab)])
            self.stream(f"{name}_edges", e, heads, values, other, None, last_state, "additive",
                        keytab[:].rearrange("p t h -> p (t h)"))
            nodes = r.sb("nodes", [NP, NT, values + heads])
            inner, v = self.stage(f"{name}_loops")
            with inner:
                own_dve = v.sem("own_dve")
                block = inner.enter_context(nc.Block())

                @block.vector
                def _(dve):
                    own = InOrder(dve, own_dve)
                    own(nc.vector.tensor_tensor(own_score[:], tab[:, :, values:], keytab[:], ALU.add))
                    own(nc.vector.scalar_tensor_tensor(out=own_score[:], in0=own_score[:], scalar=0.2,
                                                       in1=own_score[:], op0=ALU.mult, op1=ALU.max))
            self.merge(f"{name}_edges", e, heads, values, last_state, nodes, tab[:, :, 0:values], own_score)
            result(nodes[:, :, 0:values].rearrange("p t (h d) -> p t h d", d=dim + 1))

    def layer0_graph(self):
        nc, A = self.nc, self.A
        heads, dim = A["L0_gnn_att_src"].shape[1], A["L0_gnn_att_src"].shape[2]

        def result(nodes):
            stack, r = self.stage("L0g_result")
            with stack:
                share = r.sb("share", [NP, NT, heads])
                mean = r.sb("mean", [NP, NT, D])
                bias = r.sb("bias", [NP, D])
                own_dve, loaded = r.sem("own_dve"), r.sem("loaded")
                block = stack.enter_context(nc.Block())

                @block.sync
                def _(sp):
                    sp.dma_start(bias[:], A["L0_gnn_bias"].partition_broadcast(NP)).then_inc(loaded, 16)

                @block.vector
                def _(dve):
                    own = InOrder(dve, own_dve)
                    own(nc.vector.reciprocal(share[:], nodes[:, :, :, dim]))
                    own(nc.vector.tensor_tensor(
                        mean[:].rearrange("p t (h d) -> p t h d", d=dim), nodes[:, :, :, 0:dim],
                        bc(share[:].unsqueeze(3), (NP, NT, heads, dim)), ALU.mult))
                    own(nc.vector.tensor_tensor(self.X[:], self.X[:], mean[:], ALU.add))
                    dve.wait_ge(loaded, 16)
                    own(nc.vector.tensor_tensor(self.X[:], self.X[:], bc(bias[:].unsqueeze(1), (NP, NT, D)), ALU.add))

        self.normalise("L0g_norm", self.X)
        self.additive_attention("L0g", self.by_dst, A["L0_gnn_W"],
                                A["L0_gnn_att_src"].rearrange("a h d -> (a h d)"),
                                A["L0_gnn_att_dst"].rearrange("a h d -> (a h d)"), heads, dim, result)

    def transpose_rows(self, name, src, dst):
        nc = self.nc
        stack, r = self.stage(name)
        with stack:
            tp = [r.ps(f"tp{k}", [128, 512]) for k in range(4)]
            turned, copied = r.sem("turned"), r.sem("copied")
            groups = [(t, min(t + 4, NT), c) for t in range(0, NT, 4) for c in range(KC)]
            block = stack.enter_context(nc.Block())

            @block.tensor
            def _(pe):
                for n, (a, b, c) in enumerate(groups):
                    if n >= 4:
                        pe.wait_ge(copied, n - 3)
                    for t in range(a, b):
                        last = nc.tensor.transpose(tp[n % 4][:, (t - a) * NP:(t - a + 1) * NP],
                                                   src[:, t, c * 128:(c + 1) * 128], self.ident[0:NP, 0:NP])
                    last.then_inc(turned, 1)

            @block.scalar
            def _(act):
                for n, (a, b, c) in enumerate(groups):
                    act.wait_ge(turned, n + 1)
                    nc.scalar.copy(dst[:, c, a * NP:b * NP], tp[n % 4][:, 0:(b - a) * NP]).then_inc(copied, 1)

    def add_normalised(self, name, src, gamma_dram, beta_dram):
        nc = self.nc
        stack, r = self.stage(name)
        with stack:
            sd, rstd = r.sb("sd", [NP, NT]), r.sb("rstd", [NP, NT])
            gamma, beta = r.sb("gamma", [NP, D]), r.sb("beta", [NP, D])
            own_dve, loaded = r.sem("own_dve"), r.sem("loaded")
            var_ready, sd_ready = r.sem("var_ready"), r.sem("sd_ready")
            block = stack.enter_context(nc.Block())

            @block.sync
            def _(sp):
                sp.dma_start(gamma[:], gamma_dram.partition_broadcast(NP)).then_inc(loaded, 16)
                sp.dma_start(beta[:], beta_dram.partition_broadcast(NP)).then_inc(loaded, 16)

            @block.scalar
            def _(act):
                act.wait_ge(var_ready, 1)
                nc.scalar.activation(sd[:], rstd[:], ACT.Sqrt).then_inc(sd_ready, 1)

            @block.vector
            def _(dve):
                own = InOrder(dve, own_dve)
                mv = self.rows_statistics(dve, own, src, r)
                own(nc.vector.tensor_scalar_add(rstd[:], mv[:, :, 1], 1e-5))
                dve.sem_inc(var_ready, 1)
                dve.wait_ge(sd_ready, 1)
                own(nc.vector.reciprocal(rstd[:], sd[:]))
                for t in range(NT):
                    own.fire(nc.vector.tensor_scalar(src[:, t, :], src[:, t, :], mv[:, t, 0:1], rstd[:, t:t + 1],
                                                     ALU.subtract, ALU.mult))
                own.join()
                dve.wait_ge(loaded, 32)
                own(nc.vector.tensor_tensor(src[:], src[:], bc(gamma[:].unsqueeze(1), (NP, NT, D)), ALU.mult))
                own(nc.vector.tensor_tensor(src[:], src[:], bc(beta[:].unsqueeze(1), (NP, NT, D)), ALU.add))
                own(nc.vector.tensor_tensor(self.X[:], self.X[:], src[:], ALU.add))

    def top_two(self, own, r, scores, slots, experts):
        nc = self.nc
        shape = (NP, slots, experts)
        equal, at = r.sb("equal", list(shape)), r.sb("at", list(shape))
        hots = [r.sb(f"hot{k}", list(shape)) for k in range(2)]
        tops = [r.sb(f"top{k}", [NP, slots]) for k in range(2)]
        place = [r.sb(f"place{k}", [NP, slots]) for k in range(2)]
        for k in range(2):
            own(nc.vector.tensor_reduce(tops[k][:], scores[:], AX.X, ALU.max))
            own(nc.vector.tensor_tensor(equal[:], scores[:], bc(tops[k][:].unsqueeze(2), shape), ALU.is_equal))
            own(nc.vector.scalar_tensor_tensor(
                out=at[:], in0=equal[:], scalar=-64.0, in1=bc(self.small[0:NP, 0:experts].unsqueeze(1), shape),
                op0=ALU.mult, op1=ALU.add))
            own(nc.vector.tensor_reduce(place[k][:], at[:], AX.X, ALU.min))
            own(nc.vector.tensor_tensor(hots[k][:], at[:], bc(place[k][:].unsqueeze(2), shape), ALU.is_equal))
            if k == 0:
                own(nc.vector.scalar_tensor_tensor(out=scores[:], in0=hots[0][:], scalar=-BIG, in1=scores[:],
                                                   op0=ALU.mult, op1=ALU.add))
        return hots, tops, place

    def gate_scores(self, name, w_dram, b_dram, scores):
        nc, experts = self.nc, w_dram.shape[1]
        stack, r = self.stage(name)
        with stack:
            w, b = r.sb("w", [128, KC, experts]), r.sb("b", [NP, experts])
            inner, v = self.stage(f"{name}_load")
            with inner:
                loaded = v.sem("loaded")
                block = inner.enter_context(nc.Block())

                @block.sync
                def _(sp):
                    self.load_weight(sp, loaded, w[:], w_dram)
                    sp.dma_start(b[:], b_dram.partition_broadcast(NP)).then_inc(loaded, 16)
                    sp.wait_ge(loaded, 32)
            self.project(f"{name}_proj", [([(self.XT, w[:])], b[:], lambda t: scores[:, t, :], lambda ap: ap)])

    def transposed_rows_of(self, name, items):
        nc = self.nc
        stack, r = self.stage(name)
        with stack:
            raw = [r.sb(f"raw{k}", [v.shape[0], 128]) for k, (v, _) in enumerate(items)]
            ps = [r.ps(f"ps{k}", [128, v.shape[0]]) for k, (v, _) in enumerate(items)]
            loaded, turned = r.sem("loaded"), r.sem("turned")
            block = stack.enter_context(nc.Block())

            @block.sync
            def _(sp):
                for k, (v, _) in enumerate(items):
                    sp.dma_start(raw[k][:], v).then_inc(loaded, 16)

            @block.tensor
            def _(pe):
                pe.wait_ge(loaded, 16 * len(items))
                for k, (v, _) in enumerate(items):
                    n = v.shape[0]
                    nc.tensor.transpose(ps[k][:], raw[k][:], self.ident[0:n, 0:n]).then_inc(turned, 1)

            @block.scalar
            def _(act):
                for k, (_, tile) in enumerate(items):
                    act.wait_ge(turned, k + 1)
                    last = nc.scalar.copy(tile, ps[k][:])

    def experts(self, name, turns, w1, b1, w2, b2, gate, acc, scale=None, shift=None, chosen=None):
        nc, XT = self.nc, self.XT
        count, hidden = w1.shape[0], w1.shape[2]
        hc = hidden // 128
        blocks = NT // FFN_TILES
        left = 512 - 3 * NP
        stack, r = self.stage(name)
        with stack:
            w1s, w2s = r.sb("w1s", [128, KC, hidden]), r.sb("w2s", [128, hc, D])
            b1s, b2s = r.sb("b1s", [128, count * hc]), r.sb("b2s", [NP, D])
            hid = [r.sb(f"hid{k}", [128, hc, TOK]) for k in range(2)]
            items = [(b1.rearrange("e (c k) -> (e c) k", k=128), b1s[:])]
            if scale is not None:
                xe = r.sb("xe", [128, KC, NODES])
                scales = r.sb("scales", [128, 2, count * KC])
                items += [(v.rearrange("e (c k) -> (e c) k", k=128), scales[:, n, :])
                          for n, v in enumerate((scale, shift))]
            self.transposed_rows_of(f"{name}_bias", items)
            x_in = XT if scale is None else xe
            up = [r.ps(f"up{k}", [128, 1024]) for k in range(2)]
            down = [r.ps(f"down{k}", [NP, 512]) for k in range(4)]
            w1_in, w2_in, b2_in = r.sem("w1_in"), r.sem("w2_in"), r.sem("b2_in")
            up_done, gelu_done, down_done, summed = (r.sem(n) for n in ("up_done", "gelu_done", "down_done", "summed"))
            own_dve, scaled = r.sem("own_dve"), r.sem("scaled")
            expert_begun, bias_in = r.sem("expert_begun"), r.sem("bias_in")
            b1e = r.sb("b1e", [128, hc])
            per = blocks * hc
            block = stack.enter_context(nc.Block())

            def bank(n):
                return down[n % 4][:, 0:D]

            def picker(engine):
                if chosen is None:
                    return lambda i: i
                values = [engine.value_load(chosen[0:1, k:k + 1], min_val=0, max_val=count - 1) for k in range(turns)]
                return lambda i: values[i]

            @block.sync
            def _(sp):
                expert = picker(sp)

                def load(i):
                    e = expert(i)
                    if not isinstance(i, int) or i > 0:
                        sp.wait_ge(up_done, per * i)
                    sp.dma_start(w1s[:], w1[bass.ds(e, 1)].rearrange("e (c k) h -> k (e c) h", k=128)).then_inc(w1_in, 16)
                    if not isinstance(i, int) or i > 0:
                        sp.wait_ge(down_done, NT * i)
                        sp.wait_ge(summed, NT * i)
                    sp.dma_start(w2s[:], w2[bass.ds(e, 1)].rearrange("e (c k) d -> k (e c) d", k=128)).then_inc(w2_in, 16)
                    sp.dma_start(b2s[:], b2[bass.ds(e, 1)].rearrange("e d -> (e d)").partition_broadcast(NP)).then_inc(b2_in, 16)

                loop(sp, turns, lambda i, first, last: load(i))

            @block.tensor
            def _(pe):
                def upward(i, first, b):
                    if b == 0:
                        pe.wait_ge(w1_in, 16 * (i + 1))
                        if scale is not None:
                            pe.wait_ge(scaled, i + 1)
                    for h in range(hc):
                        m = b * hc + h
                        if not first or m >= 2:
                            pe.wait_ge(gelu_done, per * i + m - 1)
                        for c in range(KC):
                            for lo, hi, at in ((0, 3 * NP, left), (3 * NP, TOK, 512)):
                                last = nc.tensor.matmul(
                                    up[m % 2][:, at:at + hi - lo], w1s[:, c, 128 * h:128 * (h + 1)],
                                    x_in[:, c, b * TOK + lo:b * TOK + hi], start=(c == 0), stop=(c == KC - 1))
                        last.then_inc(up_done, 1)

                def downward(i, first, b):
                    if b == 0:
                        pe.wait_ge(w2_in, 16 * (i + 1))
                    pe.wait_ge(gelu_done, per * i + hc * (b + 1))
                    for k in range(FFN_TILES):
                        n = b * FFN_TILES + k
                        if n >= 4:
                            pe.wait_ge(summed, NT * i + n - 3)
                        elif n == 0 and not first:
                            pe.wait_ge(summed, NT * i)
                        for h in range(hc):
                            last = nc.tensor.matmul(bank(n), hid[b % 2][:, h, k * NP:(k + 1) * NP], w2s[:, h, :],
                                                    start=(h == 0), stop=(h == hc - 1))
                        last.then_inc(down_done, 1)

                def turn(i, first, last):
                    upward(i, first, 0)
                    for b in range(1, blocks):
                        upward(i, first, b)
                        downward(i, first, b - 1)
                    downward(i, first, blocks - 1)
                loop(pe, turns, turn)

            @block.scalar
            def _(act):
                expert = picker(act)

                def turn(i, first, last):
                    if not first:
                        act.wait_ge(gelu_done, per * i)
                    act.sem_inc(expert_begun, 1)
                    nc.scalar.copy(b1e[:], b1s[:, bass.ds(expert(i) * hc, hc)]).then_inc(bias_in, 1)
                    act.wait_ge(bias_in, i + 1)
                    for b in range(blocks):
                        for h in range(hc):
                            m = b * hc + h
                            act.wait_ge(up_done, per * i + m + 1)
                            if h == 0:
                                if b >= 2:
                                    act.wait_ge(down_done, NT * i + FFN_TILES * (b - 1))
                                elif not first:
                                    act.wait_ge(down_done, NT * i)
                            nc.scalar.activation(hid[b % 2][:, h, :], up[m % 2][:, left:left + TOK], ACT.Gelu,
                                                 bias=b1e[:, h:h + 1]).then_inc(gelu_done, 1)
                loop(act, turns, turn)

            @block.vector
            def _(dve):
                own = InOrder(dve, own_dve)

                def scale_rows(i):
                    for c in range(KC):
                        own.fire(nc.vector.tensor_scalar(
                            xe[:, c, :], XT[:, c, :], scales[:, 0, bass.ds(KC * i + c, 1)],
                            scales[:, 1, bass.ds(KC * i + c, 1)], ALU.mult, ALU.add))
                    own.join()
                    dve.sem_inc(scaled, 1)

                def turn(i, first, last):
                    own.restart()
                    if not first:
                        dve.wait_ge(summed, NT * i)
                    if first and scale is not None:
                        scale_rows(0)
                    dve.wait_ge(b2_in, 16 * (i + 1))
                    for t in range(NT):
                        own.fire(nc.vector.scalar_tensor_tensor(out=acc[:, t, :], in0=b2s[:], scalar=gate(t, i),
                                                                in1=acc[:, t, :], op0=ALU.mult, op1=ALU.add))
                    own.join()
                    for t in range(NT):
                        if t == NT - 2 * FFN_TILES and scale is not None and not last:
                            dve.wait_ge(up_done, per * (i + 1))
                            scale_rows(i + 1)
                        dve.wait_ge(down_done, NT * i + t + 1)
                        nc.vector.scalar_tensor_tensor(out=acc[:, t, :], in0=bank(t), scalar=gate(t, i),
                                                       in1=acc[:, t, :], op0=ALU.mult, op1=ALU.add).then_inc(summed, 1)
                loop(dve, turns, turn)
                dve.wait_ge(summed, NT * turns)

    def routed_experts(self, name, hots, gates, w1, b1, w2, b2, scale=None, shift=None):
        nc, XH = self.nc, self.XH
        count, hidden = w1.shape[0], w1.shape[2]
        hc = hidden // 128
        tiles = -(-(2 * NODES + count * (SLOTS - 1)) // SLOTS)
        tiles += tiles % 2
        assert SLOTS == 1 << SLOTS_SHIFT and tiles <= 64
        rows = self.table(f"{name}_rows", D)
        ids = nc.dram_tensor(f"{name}_ids", [tiles * SLOTS, 1], I32, kind="Internal").ap()
        answers = nc.dram_tensor(f"{name}_answers", [tiles * SLOTS, D], F32, kind="Internal").ap()
        outer, o = self.stage(name)
        with outer:
            place = o.sb("place", [NP, 2, NT], I32)
            share = o.sb("share", [NP, 2, NT])
            tile_expert = o.sb("tile_expert", [NP, tiles], I32)
            self.route(name, hots, gates, count, tiles, rows, ids, place, share, tile_expert)
            self.expert_tiles(name, tiles, tile_expert, rows, ids, answers, w1, b1, w2, b2, scale, shift)
            stack, r = self.stage(f"{name}_combine")
            with stack:
                back = r.sb("back", [NP, 2, NT, D])
                own_dve = r.sem("own_dve")
                fetched = [self.moved_sem(f"{name}_fetched{c}") for c in range(2)]
                block = stack.enter_context(nc.Block())

                @block.gpsimd
                def _(pool):
                    for c in range(2):
                        for t in range(NT):
                            pool.indirect_dma_start(
                                back[:, c, t, :], None, answers,
                                bass.IndirectOffsetOnAxis(ap=place[:, c, t:t + 1], axis=0)).then_inc(fetched[c], 16)

                @block.vector
                def _(dve):
                    own = InOrder(dve, own_dve)
                    for c in range(2):
                        dve.wait_ge(fetched[c], 16 * NT)
                        own.join()
                        for t in range(NT):
                            own.fire(nc.vector.scalar_tensor_tensor(
                                out=self.X[:, t, :], in0=back[:, c, t, :], scalar=share[:, c, t:t + 1],
                                in1=self.X[:, t, :], op0=ALU.mult, op1=ALU.add))
                    own.join()

    def route(self, name, hots, gates, count, tiles, rows, ids, place, share, tile_expert):
        nc = self.nc
        stack, r = self.stage(f"{name}_route")
        with stack:
            shape = (NP, NT, count)
            both, where = r.sb("both", list(shape)), r.sb("where", list(shape))
            picked = [r.sb(f"picked{c}", list(shape)) for c in range(4)]
            run = r.sb("run", [NP, NT + 1, count])
            ones = r.sb("ones", [NP, NP])
            needs = r.sb("needs", [NP, count], I32)
            needsf, base = r.sb("needsf", [NP, count]), r.sb("base", [NP, count])
            start = r.sb("start", [NP, count + 1])
            begun = r.sb("begun", [NP, tiles, count])
            last_begun = r.sb("last_begun", [NP, tiles])
            placef = r.sb("placef", [NP, 2, NT])
            diagonal, own_first = r.sb("diagonal", [NP, NP]), r.sb("own_first", [NP, 1])
            number = r.sb("number", [NP, NT], I32)
            blank = r.sb("blank", [128, tiles * SLOTS // 128], I32)
            sums = r.ps("sums", [NP, 2, count])
            own_dve, blank_made, blanked, summed, ran, placed, started, stored = (
                r.sem(n) for n in ("own_dve", "blank_made", "blanked", "summed", "ran", "placed", "started", "stored"))
            listed = self.moved_sem(f"{name}_listed")
            block = stack.enter_context(nc.Block())

            @block.sync
            def _(sp):
                sp.wait_ge(blank_made, 1)
                sp.dma_start(ids.rearrange("(p k) w -> p (k w)", p=128), blank[:]).then_inc(blanked, 16)
                sp.dma_start(rows.rearrange("(p t) w -> p t w", t=NT), self.XH[:]).then_inc(stored, 16)
                sp.wait_ge(stored, 16)

            @block.tensor
            def _(pe):
                pe.wait_ge(ran, 1)
                nc.tensor.matmul(sums[:, 0, :], self.upper[0:NP, 0:NP], run[:, NT, :], start=True, stop=True)
                nc.tensor.matmul(sums[:, 1, :], ones[:], run[:, NT, :], start=True, stop=True).then_inc(summed, 1)

            @block.vector
            def _(dve):
                own = InOrder(dve, own_dve)
                tt, ts = nc.vector.tensor_tensor, nc.vector.tensor_scalar
                own(nc.vector.memset(blank[:], 0.0))
                dve.sem_inc(blank_made, 1)
                own.fire(nc.vector.memset(ones[:], 1.0))
                own.fire(nc.vector.memset(run[:, 0, :], 0.0))
                own.fire(nc.vector.memset(start[:, 0:1], 0.0))
                own.fire(tt(diagonal[:], self.ident[0:NP, 0:NP], self.hi_values[0:NP, :], ALU.mult))
                own(tt(both[:], hots[0][:], hots[1][:], ALU.add))
                for t in range(NT):
                    own(tt(run[:, t + 1, :], run[:, t, :], both[:, t, :], ALU.add))
                dve.sem_inc(ran, 1)
                own(nc.vector.tensor_reduce(own_first[:], diagonal[:], AX.X, ALU.add))
                own.fire(ts(number[:], self.lo_values[0:NP, :], own_first[:, 0:1], None, ALU.add))
                for c in range(2):
                    own.fire(tt(picked[2 + c][:], gates[:], hots[c][:], ALU.mult))
                own.join()
                for c in range(2):
                    own.fire(nc.vector.tensor_reduce(share[:, c, :], picked[2 + c][:], AX.X, ALU.add))
                dve.wait_ge(summed, 1)
                own(ts(needs[:], sums[:, 1, :], float(SLOTS - 1), None, ALU.add))
                own(ts(needs[:], needs[:], SLOTS_SHIFT, None, ALU.arith_shift_right))
                own(nc.vector.tensor_copy(needsf[:], needs[:]))
                for e in range(count):
                    own(tt(start[:, e + 1:e + 2], start[:, e:e + 1], needsf[:, e:e + 1], ALU.add))
                own.fire(tt(begun[:], bc(start[:, 0:count].unsqueeze(1), (NP, tiles, count)),
                            bc(self.small[0:NP, 0:tiles].unsqueeze(2), (NP, tiles, count)), ALU.is_le))
                own(ts(base[:], start[:, 0:count], float(SLOTS), None, ALU.mult))
                own(tt(base[:], base[:], sums[:, 0, :], ALU.add))
                own(tt(where[:], run[:, 0:NT, :], bc(base[:].unsqueeze(1), shape), ALU.add))
                for c in range(2):
                    own.fire(tt(picked[c][:], where[:], hots[c][:], ALU.mult))
                own.join()
                for c in range(2):
                    own.fire(nc.vector.tensor_reduce(placef[:, c, :], picked[c][:], AX.X, ALU.add))
                own.join()
                own(nc.vector.tensor_copy(place[:], placef[:]))
                dve.sem_inc(placed, 1)
                own(nc.vector.tensor_reduce(last_begun[:], begun[:], AX.X, ALU.add))
                own(ts(tile_expert[:], last_begun[:], -1.0, None, ALU.add))

            @block.gpsimd
            def _(pool):
                pool.wait_ge(blanked, 16)
                pool.wait_ge(placed, 1)
                pool.sem_inc(started, 1)
                for c in range(2):
                    for t in range(NT):
                        pool.indirect_dma_start(
                            ids, bass.IndirectOffsetOnAxis(ap=place[:, c, t:t + 1], axis=0),
                            number[:, t:t + 1], None).then_inc(listed, 16)
                pool.wait_ge(listed, 16 * 2 * NT)

    def expert_tiles(self, name, tiles, tile_expert, rows, ids, answers, w1, b1, w2, b2, scale, shift):
        nc = self.nc
        count, hidden = w1.shape[0], w1.shape[2]
        hc, subs = hidden // 128, SLOTS // 128
        two = range(2)
        stack, r = self.stage(f"{name}_tiles")
        with stack, nc.allow_non_contiguous_dma(reason="the slots' node numbers"):
            b1s = r.sb("b1s", [128, count * hc])
            items = [(b1.rearrange("e (c k) -> (e c) k", k=128), b1s[:])]
            if scale is not None:
                scales = r.sb("scales", [128, 2, count * KC])
                items += [(v.rearrange("e (c k) -> (e c) k", k=128), scales[:, n, :])
                          for n, v in enumerate((scale, shift))]
            self.transposed_rows_of(f"{name}_bias", items)
            all_nodes = r.sb("all_nodes", [128, tiles * subs], I32)
            nodes = [r.sb(f"nodes{h}", [128, subs], I32) for h in two]
            xg = [r.sb(f"xg{h}", [128, subs, D]) for h in two]
            xt = [r.sb(f"xt{h}", [128, KC, SLOTS]) for h in two]
            w1s = [r.sb(f"w1s{h}", [128, KC, hidden]) for h in two]
            w2s = [r.sb(f"w2s{h}", [128, hc, D]) for h in two]
            b1e = [r.sb(f"b1e{h}", [128, hc]) for h in two]
            b2s = [r.sb(f"b2s{h}", [128, D]) for h in two]
            scale_e = [r.sb(f"scale_e{h}", [128, 2, KC]) for h in two]
            hid = [r.sb(f"hid{h}", [128, hc, SLOTS]) for h in two]
            y = [r.sb(f"y{h}", [128, subs, D]) for h in two]
            xt_ps = r.ps("xt_ps", [128, KC, SLOTS])
            up = [r.ps(f"up{k}", [128, 512]) for k in range(4)]
            down = [r.ps(f"down{k}", [128, 512]) for k in range(subs)]
            w1_in, w2_in, b2_in, stored = (
                [r.sem(f"{n}{h}") for h in two] for n in ("w1_in", "w2_in", "b2_in", "stored"))
            all_in, nodes_in, nodes_picked = r.sem("all_in"), r.sem("nodes_in"), r.sem("nodes_picked")
            gathered = [self.moved_sem(f"{name}_gathered{h}") for h in two]
            started, turned, xt_in, up_done, gelu_done, down_done, summed = (
                r.sem(n) for n in ("started", "turned", "xt_in", "up_done", "gelu_done", "down_done", "summed"))
            picked, consts_in, own_dve = r.sem("picked"), r.sem("consts_in"), r.sem("own_dve")
            ids_v = ids.rearrange("(i q) w -> q (i w)", q=128)
            answers_v = answers.rearrange("(i s q) d -> i q s d", s=subs, q=128)
            per_consts = 1 if scale is None else 2
            block = stack.enter_context(nc.Block())

            def expert_of(engine, i, h):
                return engine.value_load(tile_expert[0:1, bass.ds(2 * i + h, 1)], min_val=0, max_val=count - 1)

            @block.sync
            def _(sp):
                sp.dma_start(all_nodes[:], ids_v).then_inc(all_in, 16)

                def turn(i, first, last):
                    for h in two:
                        n = 2 * i + h
                        e = expert_of(sp, i, h)
                        if not first:
                            sp.wait_ge(up_done, hc * (n - 1))
                        sp.dma_start(w1s[h][:], w1[bass.ds(e, 1)].rearrange("e (c k) h -> k (e c) h", k=128))\
                          .then_inc(w1_in[h], 16)
                        if not first:
                            sp.wait_ge(down_done, subs * (n - 1))
                            sp.wait_ge(summed, subs * (n - 1))
                        sp.dma_start(w2s[h][:], w2[bass.ds(e, 1)].rearrange("e (c k) d -> k (e c) d", k=128))\
                          .then_inc(w2_in[h], 16)
                        sp.dma_start(b2s[h][:], b2[bass.ds(e, 1)].rearrange("e d -> (e d)").partition_broadcast(128))\
                          .then_inc(b2_in[h], 16)
                loop(sp, tiles // 2, turn)

            @block.gpsimd
            def _(pool):
                def turn(i, first, last):
                    for h in two:
                        pool.wait_ge(nodes_in, 2 * i + h + 1)
                        pool.sem_inc(started, 1)
                        for k in range(subs):
                            pool.indirect_dma_start(
                                xg[h][:, k, :], None, rows,
                                bass.IndirectOffsetOnAxis(ap=nodes[h][:, k:k + 1], axis=0)).then_inc(gathered[h], 16)
                loop(pool, tiles // 2, turn)

            @block.tensor
            def _(pe):
                def turn_rows(i, h, start):
                    pe.wait_ge(gathered[h], 16 * subs * (i + 1))
                    if not start:
                        pe.wait_ge(xt_in, 2 * i + h)
                    for c in range(KC):
                        for k in range(subs):
                            ins = nc.tensor.transpose(xt_ps[:, c, 128 * k:128 * (k + 1)],
                                                      xg[h][:, k, 128 * c:128 * (c + 1)], self.ident[:])
                    ins.then_inc(turned, 1)

                def upward(i, h, start):
                    n = 2 * i + h
                    pe.wait_ge(w1_in[h], 16 * (i + 1))
                    pe.wait_ge(xt_in, n + 1)
                    for m in range(hc):
                        if not start or m >= 4:
                            pe.wait_ge(gelu_done, hc * n + m - 3)
                        for c in range(KC):
                            ins = nc.tensor.matmul(up[m % 4][:, 0:SLOTS], w1s[h][:, c, 128 * m:128 * (m + 1)],
                                                   xt[h][:, c, :], start=(c == 0), stop=(c == KC - 1))
                        ins.then_inc(up_done, 1)

                def downward(i, h, start):
                    n = 2 * i + h
                    pe.wait_ge(w2_in[h], 16 * (i + 1))
                    pe.wait_ge(gelu_done, hc * (n + 1))
                    for k in range(subs):
                        if not start:
                            pe.wait_ge(summed, subs * (n - 1) + k + 1)
                        for m in range(hc):
                            ins = nc.tensor.matmul(down[k][:, 0:D], hid[h][:, m, 128 * k:128 * (k + 1)], w2s[h][:, m, :],
                                                   start=(m == 0), stop=(m == hc - 1))
                        ins.then_inc(down_done, 1)

                turn_rows(0, 0, True)
                upward(0, 0, True)
                turn_rows(0, 1, False)

                def turn(i, first, last):
                    for h in two:
                        if not (last and h == 1):
                            upward(i + h, 1 - h, False)
                        if not last:
                            turn_rows(i + 1, h, False)
                        downward(i, h, first and h == 0)
                loop(pe, tiles // 2, turn)

            @block.scalar
            def _(act):
                def pick_consts(i, h, start):
                    n = 2 * i + h
                    e = expert_of(act, i, h)
                    if not start:
                        act.wait_ge(gelu_done, hc * (n - 1))
                        act.wait_ge(xt_in, n - 1)
                    act.sem_inc(picked, 1)
                    nc.scalar.copy(b1e[h][:], b1s[:, bass.ds(e * hc, hc)]).then_inc(consts_in, 1)
                    if scale is not None:
                        nc.scalar.copy(scale_e[h][:], scales[:, :, bass.ds(e * KC, KC)]).then_inc(consts_in, 1)

                def store(i, h):
                    act.wait_ge(summed, subs * (2 * i + h + 1))
                    act.dma_start(answers_v[bass.ds(2 * i + h, 1)].rearrange("a q s d -> q (a s) d"), y[h][:])\
                       .then_inc(stored[h], 16)

                def pick_nodes(i, h, start):
                    if not start:
                        act.wait_ge(gathered[h], 16 * subs * i)
                        act.wait_ge(turned, 2 * i + h - 1)
                    act.sem_inc(nodes_picked, 1)
                    nc.scalar.copy(nodes[h][:], all_nodes[:, bass.ds(subs * (2 * i + h), subs)]).then_inc(nodes_in, 1)

                act.wait_ge(all_in, 16)
                for h in two:
                    pick_nodes(0, h, True)
                    pick_consts(0, h, True)

                def turn(i, first, last):
                    for h in two:
                        n = 2 * i + h
                        if not last:
                            pick_nodes(i + 1, h, False)
                        act.wait_ge(consts_in, per_consts * (n + 1))
                        for m in range(hc):
                            act.wait_ge(up_done, hc * n + m + 1)
                            if m == 0 and not first:
                                act.wait_ge(down_done, subs * (n - 1))
                            nc.scalar.activation(hid[h][:, m, :], up[m % 4][:, 0:SLOTS], ACT.Gelu,
                                                 bias=b1e[h][:, m:m + 1]).then_inc(gelu_done, 1)
                        if not last:
                            pick_consts(i + 1, h, False)
                        if not (first and h == 0):
                            store(i - 1 + h, 1 - h)
                loop(act, tiles // 2, turn)
                store(tiles // 2 - 1, 1)
                for h in two:
                    act.wait_ge(stored[h], 16 * (tiles // 2))

            @block.vector
            def _(dve):
                def turn_in(i, h, start):
                    n = 2 * i + h
                    dve.wait_ge(turned, n + 1)
                    if not start:
                        dve.wait_ge(up_done, hc * (n - 1))
                    if scale is None:
                        nc.vector.tensor_copy(xt[h][:], xt_ps[:]).then_inc(xt_in, 1)
                        return
                    dve.wait_ge(consts_in, per_consts * (n + 1))
                    for c in range(KC):
                        nc.vector.tensor_scalar(xt[h][:, c, :], xt_ps[:, c, :], scale_e[h][:, 0, c:c + 1],
                                                scale_e[h][:, 1, c:c + 1], ALU.mult, ALU.add).then_inc(own_dve, 1)
                    dve.wait_ge(own_dve, KC * (n + 1))
                    dve.sem_inc(xt_in, 1)

                turn_in(0, 0, True)
                turn_in(0, 1, True)

                def turn(i, first, last):
                    for h in two:
                        n = 2 * i + h
                        if not last:
                            turn_in(i + 1, h, False)
                        dve.wait_ge(b2_in[h], 16 * (i + 1))
                        if not first:
                            dve.wait_ge(stored[h], 16 * i)
                        for k in range(subs):
                            dve.wait_ge(down_done, subs * n + k + 1)
                            nc.vector.tensor_tensor(y[h][:, k, :], down[k][:, 0:D], b2s[h][:], ALU.add).then_inc(summed, 1)
                loop(dve, tiles // 2, turn)

    def layer0_experts(self):
        nc, A = self.nc, self.A
        count = A["L0_ffn_Wg"].shape[1]
        self.normalise("L0f_norm", self.X)
        outer, o = self.stage("L0f")
        with outer:
            gates = o.sb("gates", [NP, NT, count])
            hots = [o.sb(f"hot{k}", [NP, NT, count]) for k in range(2)]
            self.gate_scores("L0f_gate", A["L0_ffn_Wg"], A["L0_ffn_bg"], gates)
            stack, r = self.stage("L0f_top")
            with stack:
                own_dve = r.sem("own_dve")
                block = stack.enter_context(nc.Block())

                @block.vector
                def _(dve):
                    own = InOrder(dve, own_dve)
                    for hot, b in zip(hots, self.top_two(own, r, gates, NT, count)[0]):
                        own(nc.vector.tensor_copy(hot[:], b[:]))
                    own(nc.vector.tensor_tensor(gates[:], hots[0][:], hots[1][:], ALU.add))
            self.routed_experts("L0f_experts", hots, gates, A["L0_ffn_W1"], A["L0_ffn_b1"], A["L0_ffn_W2"],
                                A["L0_ffn_b2"])

    def layer1_graph(self):
        nc, A = self.nc, self.A
        self.normalise("L1g_norm", self.X)
        rows = self.table("L1g_rows", D)
        outer, o = self.stage("L1g")
        with outer:
            last_state = o.sb("last_state", [NP, D])
            stack, r = self.stage("L1g_table")
            with stack:
                tab = r.sb("tab", [NP, NT, D])
                made, stored = r.sem("made"), r.sem("stored")
                block = stack.enter_context(nc.Block())

                @block.vector
                def _(dve):
                    nc.vector.tensor_tensor(tab[:], self.XH[:], bc(self.isout[:].unsqueeze(2), (NP, NT, D)),
                                            ALU.mult).then_inc(made, 1)

                @block.sync
                def _(sp):
                    sp.wait_ge(made, 1)
                    sp.dma_start(rows.rearrange("(p t) w -> p t w", t=NT), tab[:]).then_inc(stored, 16)
                    sp.wait_ge(stored, 16)
            self.stream("L1g_edges", self.by_dst, 0, D, rows, None, last_state, "sum")
            nodes = o.sb("nodes", [NP, NT, D])
            self.merge("L1g_edges", self.by_dst, 0, D, last_state, nodes)
            total = o.sb("total", [NP, NT, D])
            stack, r = self.stage("L1g_mix")
            with stack:
                own_dve = r.sem("own_dve")
                block = stack.enter_context(nc.Block())

                @block.vector
                def _(dve):
                    own = InOrder(dve, own_dve)
                    own(nc.vector.tensor_tensor(nodes[:], nodes[:], bc(self.isout[:].unsqueeze(2), (NP, NT, D)), ALU.mult))
                    own(nc.vector.tensor_tensor(total[:], self.XH[:], nodes[:], ALU.add))
                    own(nc.vector.tensor_tensor(nodes[:], self.XH[:], nodes[:], ALU.mult))
            mixed_t = o.sb("mixed_t", [128, KC, NODES])
            self.transpose_rows("L1g_turn0", total, self.XT)
            self.transpose_rows("L1g_turn1", nodes, mixed_t)
            w1, w2, b = o.sb("w1", [128, KC, D]), o.sb("w2", [128, KC, D]), o.sb("b", [NP, D])
            stack, r = self.stage("L1g_load")
            with stack:
                loaded = r.sem("loaded")
                block = stack.enter_context(nc.Block())

                @block.sync
                def _(sp):
                    self.load_weight(sp, loaded, w1[:], A["L1_gnn_W1"])
                    self.load_weight(sp, loaded, w2[:], A["L1_gnn_W2"])
                    sp.dma_start(b[:], A["L1_gnn_b"].partition_broadcast(NP)).then_inc(loaded, 16)
                    sp.wait_ge(loaded, 48)
            self.project("L1g_proj", [([(self.XT, w1[:]), (mixed_t, w2[:])], None, lambda t: total[:, t, :], lambda ap: ap)])
            stack, r = self.stage("L1g_result")
            with stack:
                square, norm, root = r.sb("square", [NP, NT]), r.sb("norm", [NP, NT]), r.sb("root", [NP, NT])
                own_dve, square_ready, root_ready = r.sem("own_dve"), r.sem("square_ready"), r.sem("root_ready")
                block = stack.enter_context(nc.Block())

                @block.vector
                def _(dve):
                    own = InOrder(dve, own_dve)
                    own(nc.vector.tensor_tensor(total[:], total[:], bc(self.by_dst.has[:].unsqueeze(2), (NP, NT, D)), ALU.mult))
                    own(nc.vector.tensor_tensor(total[:], total[:], bc(b[:].unsqueeze(1), (NP, NT, D)), ALU.add))
                    own(nc.vector.scalar_tensor_tensor(
                        out=total[:].rearrange("p t d -> p (t d)"), in0=total[:].rearrange("p t d -> p (t d)"),
                        scalar=0.01, in1=total[:].rearrange("p t d -> p (t d)"), op0=ALU.mult, op1=ALU.max))
                    own(nc.vector.tensor_tensor(nodes[:], total[:], total[:], ALU.mult))
                    own(nc.vector.tensor_reduce(square[:], nodes[:], AX.X, ALU.add))
                    dve.sem_inc(square_ready, 1)
                    dve.wait_ge(root_ready, 1)
                    own(nc.vector.tensor_scalar_max(norm[:], root[:], 1e-12))
                    own(nc.vector.reciprocal(norm[:], norm[:]))
                    own(nc.vector.tensor_tensor(total[:], total[:], bc(norm[:].unsqueeze(2), (NP, NT, D)), ALU.mult))
                    own(nc.vector.tensor_tensor(self.X[:], self.X[:], total[:], ALU.add))

                @block.scalar
                def _(act):
                    act.wait_ge(square_ready, 1)
                    nc.scalar.activation(root[:], square[:], ACT.Sqrt).then_inc(root_ready, 1)

    def layer1_experts(self):
        nc, A = self.nc, self.A
        heads, count = A["L1_ffn_att_src"].shape
        wide = heads * count
        self.normalise("L1f_norm", self.X)
        outer, o = self.stage("L1f")
        with outer:
            gates = o.sb("gates", [NP, NT, count])

            def result(nodes):
                stack, r = self.stage("L1f_result")
                with stack:
                    agg, dev = r.sb("agg", [NP, NT, wide]), r.sb("dev", [NP, NT, wide])
                    share = r.sb("share", [NP, NT, heads])
                    mean, var = r.sb("mean", [NP, NT]), r.sb("var", [NP, NT])
                    root, ratio = r.sb("root", [NP, NT]), r.sb("ratio", [NP, NT])
                    scores = r.sb("scores", [NP, NT, count])
                    rows = r.sb("rows", [NP, 3, wide])
                    own_dve, loaded = r.sem("own_dve"), r.sem("loaded")
                    var_ready, root_ready, gap_ready, ratio_ready = (
                        r.sem(n) for n in ("var_ready", "root_ready", "gap_ready", "ratio_ready"))
                    block = stack.enter_context(nc.Block())

                    @block.sync
                    def _(sp):
                        for k, n in enumerate(("b_gat", "ln_gamma", "ln_beta")):
                            sp.dma_start(rows[:, k, :], A[f"L1_ffn_{n}"].partition_broadcast(NP)).then_inc(loaded, 16)

                    @block.scalar
                    def _(act):
                        act.wait_ge(var_ready, 1)
                        nc.scalar.activation(root[:], var[:], ACT.Sqrt).then_inc(root_ready, 1)
                        act.wait_ge(gap_ready, 1)
                        nc.scalar.activation(ratio[:], mean[:], ACT.Exp).then_inc(ratio_ready, 1)

                    @block.vector
                    def _(dve):
                        own = InOrder(dve, own_dve)
                        tt = nc.vector.tensor_tensor

                        def row(k):
                            return bc(rows[:, k, :].unsqueeze(1), (NP, NT, wide))

                        def each(ap):
                            return bc(ap.unsqueeze(2), (NP, NT, wide))

                        own(nc.vector.tensor_scalar_add(share[:], nodes[:, :, :, count], 1e-16))
                        own(nc.vector.reciprocal(share[:], share[:]))
                        own(tt(agg[:].rearrange("p t (h d) -> p t h d", d=count), nodes[:, :, :, 0:count],
                               bc(share[:].unsqueeze(3), (NP, NT, heads, count)), ALU.mult))
                        dve.wait_ge(loaded, 48)
                        own(tt(agg[:], agg[:], row(0), ALU.add))
                        own(nc.vector.tensor_reduce(mean[:], agg[:], AX.X, ALU.add))
                        own(nc.vector.tensor_scalar(mean[:], mean[:], 1.0 / wide, None, ALU.mult))
                        own(tt(agg[:], agg[:], each(mean[:]), ALU.subtract))
                        own(tt(dev[:], agg[:], agg[:], ALU.mult))
                        own(nc.vector.tensor_reduce(var[:], dev[:], AX.X, ALU.add))
                        own(nc.vector.tensor_scalar(var[:], var[:], 1.0 / wide, 1e-5, ALU.mult, ALU.add))
                        dve.sem_inc(var_ready, 1)
                        dve.wait_ge(root_ready, 1)
                        own(nc.vector.reciprocal(var[:], root[:]))
                        own(tt(agg[:], agg[:], each(var[:]), ALU.mult))
                        own(tt(agg[:], agg[:], row(1), ALU.mult))
                        own(tt(agg[:], agg[:], row(2), ALU.add))
                        own(nc.vector.tensor_reduce(scores[:], agg[:].rearrange("p t (h d) -> p t d h", d=count),
                                                    AX.X, ALU.add))
                        own(nc.vector.tensor_scalar(scores[:], scores[:], 1.0 / heads, None, ALU.mult))
                        hots, tops, _ = self.top_two(own, r, scores, NT, count)
                        own(tt(mean[:], tops[1][:], tops[0][:], ALU.subtract))
                        dve.sem_inc(gap_ready, 1)
                        dve.wait_ge(ratio_ready, 1)
                        own(nc.vector.tensor_scalar_add(var[:], ratio[:], 1.0))
                        own(nc.vector.reciprocal(var[:], var[:]))
                        own(tt(ratio[:], ratio[:], var[:], ALU.mult))
                        own.fire(tt(hots[0][:], hots[0][:], bc(var[:].unsqueeze(2), (NP, NT, count)), ALU.mult))
                        own.fire(tt(hots[1][:], hots[1][:], bc(ratio[:].unsqueeze(2), (NP, NT, count)), ALU.mult))
                        own.join()
                        own(tt(gates[:], hots[0][:], hots[1][:], ALU.add))

            self.additive_attention("L1f_gat", self.by_gate, A["L1_ffn_W_gat"],
                                    A["L1_ffn_att_src"].rearrange("h d -> (h d)"),
                                    A["L1_ffn_att_dst"].rearrange("h d -> (h d)"), heads, count, result)
            self.experts("L1f_experts", count, A["L1_ffn_W1"], A["L1_ffn_b1"], A["L1_ffn_W2"], A["L1_ffn_b2"],
                         lambda t, i: gates[:, t, bass.ds(i, 1)], self.X)

    def layer2_graph(self):
        nc, A, XT = self.nc, self.A, self.XT
        rels, dim = A["L2_gnn_rel_w"].shape
        heads = D // dim
        values = heads * (dim + 1)
        self.normalise("L2g_norm", self.X)
        other, keys = self.table("L2g_other", values + D), self.table("L2g_keys", D)
        root = float(dim) ** -0.5
        assert root == 0.125
        outer, o = self.stage("L2g")
        with outer:
            last_state = o.sb("last_state", [NP, values + heads])
            relations = o.sb("relations", [2 * rels, D])
            stack, r = self.stage("L2g_tables")
            with stack:
                tab, keytab = r.sb("tab", [NP, NT, values + D]), r.sb("keytab", [NP, NT, D])
                wq, wv, wk = (r.sb(n, [128, KC, D]) for n in ("wq", "wv", "wk"))
                bq, bv, bk = (r.sb(n, [NP, D]) for n in ("bq", "bv", "bk"))
                inner, v = self.stage("L2g_load")
                with inner, nc.allow_non_contiguous_dma(reason="vectors of 256 words, one to a partition"):
                    rel, emb = v.sb("rel", [2 * rels, dim]), v.sb("emb", [128, KC])
                    loaded, own_dve = v.sem("loaded"), v.sem("own_dve")
                    block = inner.enter_context(nc.Block())

                    @block.sync
                    def _(sp):
                        for to, n in ((wq, "Wq"), (wk, "Wk"), (wv, "Wv")):
                            self.load_weight(sp, loaded, to[:], A[f"L2_gnn_{n}"])
                        for k in range(2):
                            sp.dma_start(rel[rels * k:rels * (k + 1), :], A["L2_gnn_rel_w"]).then_inc(loaded, 16)
                        for to, n in ((bq, "bq"), (bk, "bk"), (bv, "bv")):
                            sp.dma_start(to[:], A[f"L2_gnn_{n}"].partition_broadcast(NP)).then_inc(loaded, 16)
                        sp.dma_start(emb[:], A["L2_gnn_query_emb"].rearrange("(c k) -> k c", k=128)).then_inc(loaded, 16)

                    @block.vector
                    def _(dve):
                        own = InOrder(dve, own_dve)
                        ts = nc.vector.tensor_scalar
                        own.fire(nc.vector.memset(tab[:], 1.0))
                        dve.wait_ge(loaded, 144)
                        own(ts(emb[:], emb[:], 0.1, None, ALU.mult))
                        for c in range(KC):
                            own.fire(ts(XT[:, c, :], XT[:, c, :], emb[:, c:c + 1], None, ALU.add))
                        own.fire(ts(relations[:].rearrange("r (h d) -> r h d", d=dim),
                                    bc(rel[:].unsqueeze(1), (2 * rels, heads, dim)), 0.2, None, ALU.mult))
                        own.fire(ts(wq[:], wq[:], root, None, ALU.mult))
                        own.fire(ts(bq[:], bq[:], root, None, ALU.mult))
                        own.join()

                def head_view(ap):
                    return ap.rearrange("p (h d) -> p h d", d=dim)

                self.project("L2g_proj", [
                    ([(XT, wv[:])], bv[:], lambda t: tab[:, t, 0:values].rearrange("p (h d) -> p h d", d=dim + 1)[:, :, 0:dim],
                     head_view),
                    ([(XT, wk[:])], bk[:], lambda t: tab[:, t, values:], lambda ap: ap),
                    ([(XT, wq[:])], bq[:], lambda t: keytab[:, t, :], lambda ap: ap),
                ], [(other, tab), (keys, keytab)])
            self.stream("L2g_edges", self.by_dst, heads, values, other, keys, last_state, "relation",
                        relations[:])
            nodes = o.sb("nodes", [NP, NT, values + heads])
            self.merge("L2g_edges", self.by_dst, heads, values, last_state, nodes)
            mean = o.sb("mean", [NP, NT, D])
            stack, r = self.stage("L2g_mean")
            with stack:
                v = r.sb("v", [NP, NT, values])
                share, without = r.sb("share", [NP, NT, heads]), r.sb("without", [NP, NT])
                own_dve, loaded = r.sem("own_dve"), r.sem("loaded")
                block = stack.enter_context(nc.Block())

                @block.sync
                def _(sp):
                    sp.dma_start(v[:], other.rearrange("(p t) w -> p t w", t=NT)[:, :, 0:values]).then_inc(loaded, 16)

                @block.vector
                def _(dve):
                    own = InOrder(dve, own_dve)
                    tt = nc.vector.tensor_tensor
                    heads_of = nodes[:, :, 0:values].rearrange("p t (h d) -> p t h d", d=dim + 1)
                    mean_of = mean[:].rearrange("p t (h d) -> p t h d", d=dim)
                    own(nc.vector.reciprocal(share[:], heads_of[:, :, :, dim]))
                    own(tt(share[:], share[:], bc(self.by_dst.has[:].unsqueeze(2), (NP, NT, heads)), ALU.mult))
                    own(tt(mean_of, heads_of[:, :, :, 0:dim], bc(share[:].unsqueeze(3), (NP, NT, heads, dim)), ALU.mult))
                    own(nc.vector.tensor_scalar(without[:], self.by_dst.has[:], -1.0, 1.0, ALU.mult, ALU.add))
                    dve.wait_ge(loaded, 16)
                    own(tt(v[:], v[:], bc(without[:].unsqueeze(2), (NP, NT, values)), ALU.mult))
                    own(tt(mean_of, mean_of, v[:].rearrange("p t (h d) -> p t h d", d=dim + 1)[:, :, :, 0:dim], ALU.add))
            self.transpose_rows("L2g_turn", mean, XT)
            wo, bo = o.sb("wo", [128, KC, D]), o.sb("bo", [NP, D])
            stack, r = self.stage("L2g_again")
            with stack:
                loaded = r.sem("loaded")
                block = stack.enter_context(nc.Block())

                @block.sync
                def _(sp):
                    self.load_weight(sp, loaded, wo[:], A["L2_gnn_Wo"])
                    sp.dma_start(bo[:], A["L2_gnn_bo"].partition_broadcast(NP)).then_inc(loaded, 16)
                    sp.wait_ge(loaded, 32)
            self.project("L2g_out", [([(XT, wo[:])], bo[:], lambda t: mean[:, t, :], lambda ap: ap)])
            stack, r = self.stage("L2g_residual")
            with stack:
                own_dve = r.sem("own_dve")
                block = stack.enter_context(nc.Block())

                @block.vector
                def _(dve):
                    own = InOrder(dve, own_dve)
                    own(nc.vector.tensor_tensor(mean[:], mean[:], self.XH[:], ALU.add))
            self.add_normalised("L2g_add", mean, A["L2_gnn_gamma"], A["L2_gnn_beta"])

    def layer2_experts(self):
        nc, A = self.nc, self.A
        count = A["L2_ffn_Wr"].shape[1]
        self.normalise("L2f_norm", self.X)
        outer, o = self.stage("L2f")
        with outer:
            gates = o.sb("gates", [NP, NT, count])
            hots = [o.sb(f"hot{k}", [NP, NT, count]) for k in range(2)]
            self.gate_scores("L2f_gate", A["L2_ffn_Wr"], A["L2_ffn_br"], gates)
            stack, r = self.stage("L2f_top")
            with stack:
                shape = (NP, NT, count)
                powers, probs = r.sb("powers", list(shape)), r.sb("probs", list(shape))
                one = r.sb("one", [NP, NT])
                own_dve, args_ready, powers_ready = r.sem("own_dve"), r.sem("args_ready"), r.sem("powers_ready")
                block = stack.enter_context(nc.Block())

                @block.scalar
                def _(act):
                    act.wait_ge(args_ready, 1)
                    nc.scalar.activation(powers[:], gates[:], ACT.Exp).then_inc(powers_ready, 1)

                @block.vector
                def _(dve):
                    own = InOrder(dve, own_dve)
                    tt = nc.vector.tensor_tensor
                    own(nc.vector.tensor_reduce(one[:], gates[:], AX.X, ALU.max))
                    own(tt(gates[:], gates[:], bc(one[:].unsqueeze(2), shape), ALU.subtract))
                    dve.sem_inc(args_ready, 1)
                    dve.wait_ge(powers_ready, 1)
                    own(nc.vector.tensor_reduce(one[:], powers[:], AX.X, ALU.add))
                    own(nc.vector.reciprocal(one[:], one[:]))
                    own(tt(powers[:], powers[:], bc(one[:].unsqueeze(2), shape), ALU.mult))
                    own(nc.vector.tensor_copy(probs[:], powers[:]))
                    best, tops, _ = self.top_two(own, r, probs, NT, count)
                    for hot, b in zip(hots, best):
                        own(nc.vector.tensor_copy(hot[:], b[:]))
                    own(tt(one[:], tops[0][:], tops[1][:], ALU.add))
                    own(nc.vector.reciprocal(one[:], one[:]))
                    own(tt(gates[:], powers[:], bc(one[:].unsqueeze(2), shape), ALU.mult))
            self.normalise("L2f_norm2", self.XH)
            self.routed_experts("L2f_experts", hots, gates, A["L2_ffn_W1"], A["L2_ffn_b1"], A["L2_ffn_W2"],
                                A["L2_ffn_b2"], A["L2_ffn_ln_g"], A["L2_ffn_ln_b"])

    def layer3_graph(self):
        nc, A, XT = self.nc, self.A, self.XT
        heads, dim = 16, 8
        wide = heads * dim
        vdim = D // heads
        values = heads * (vdim + 1)
        self.normalise("L3g_norm", self.X)
        other, keys = self.table("L3g_other", values + wide), self.table("L3g_keys", wide)
        outer, o = self.stage("L3g")
        with outer:
            last_state = o.sb("last_state", [NP, values + heads])
            rpe = o.sb("rpe", [128, 2 * wide])
            stack, r = self.stage("L3g_tables")
            with stack:
                tab, keytab = r.sb("tab", [NP, NT, values + wide]), r.sb("keytab", [NP, NT, wide])
                w, b = r.sb("w", [128, KC, 2 * wide + D]), r.sb("b", [NP, 2 * wide + D])
                inner, v = self.stage("L3g_load")
                with inner:
                    loaded, own_dve = v.sem("loaded"), v.sem("own_dve")
                    block = inner.enter_context(nc.Block())

                    @block.sync
                    def _(sp):
                        self.load_weight(sp, loaded, w[:], A["L3_gnn_Wqkv"])
                        sp.dma_start(b[:], A["L3_gnn_bqkv"].partition_broadcast(NP)).then_inc(loaded, 16)
                        for q in range(0, 128, ROW):
                            for k, n in enumerate(("q", "k")):
                                at = slice(wide * k, wide * (k + 1))
                                sp.dma_start(rpe[q:q + ATTR, at], A[f"L3_gnn_W{n}_rpe"]).then_inc(loaded, 16)
                                sp.dma_start(rpe[q + ATTR:q + ATTR + 1, at],
                                             A[f"L3_gnn_b{n}_rpe"].partition_broadcast(1)).then_inc(loaded, 16)
                        sp.wait_ge(loaded, 16 * 18)

                    @block.vector
                    def _(dve):
                        own = InOrder(dve, own_dve)
                        own.fire(nc.vector.memset(tab[:], 1.0))
                        dve.wait_ge(loaded, 16 * 18)
                        for part in (w[:, :, 0:wide], b[:, 0:wide]):
                            own.fire(nc.vector.tensor_scalar(part, part, float(dim) ** -0.5, None, ALU.mult))
                        own.join()
                self.project("L3g_proj", [
                    ([(XT, w[:, :, 0:wide])], b[:, 0:wide], lambda t: keytab[:, t, :], lambda ap: ap),
                    ([(XT, w[:, :, wide:2 * wide])], b[:, wide:2 * wide], lambda t: tab[:, t, values:], lambda ap: ap),
                    ([(XT, w[:, :, 2 * wide:])], b[:, 2 * wide:],
                     lambda t: tab[:, t, 0:values].rearrange("p (h d) -> p h d", d=vdim + 1)[:, :, 0:vdim],
                     lambda ap: ap.rearrange("p (h d) -> p h d", d=vdim)),
                ], [(other, tab), (keys, keytab)])
            self.stream("L3g_edges", self.by_src, heads, values, other, keys, last_state, "attributes", rpe)
            nodes = o.sb("nodes", [NP, NT, values + heads])
            self.merge("L3g_edges", self.by_src, heads, values, last_state, nodes)
            stack, r = self.stage("L3g_result")
            with stack:
                share, mean = r.sb("share", [NP, NT, heads]), r.sb("mean", [NP, NT, D])
                own_dve = r.sem("own_dve")
                block = stack.enter_context(nc.Block())

                @block.vector
                def _(dve):
                    own = InOrder(dve, own_dve)
                    tt = nc.vector.tensor_tensor
                    heads_of = nodes[:, :, 0:values].rearrange("p t (h d) -> p t h d", d=vdim + 1)
                    own(nc.vector.tensor_scalar_add(share[:], heads_of[:, :, :, vdim], 1e-16))
                    own(nc.vector.reciprocal(share[:], share[:]))
                    own(tt(share[:], share[:], bc(self.by_src.has[:].unsqueeze(2), (NP, NT, heads)), ALU.mult))
                    own(tt(mean[:].rearrange("p t (h d) -> p t h d", d=vdim), heads_of[:, :, :, 0:vdim],
                           bc(share[:].unsqueeze(3), (NP, NT, heads, vdim)), ALU.mult))
                    own(tt(self.X[:], self.X[:], mean[:], ALU.add))

    def layer3_experts(self):
        nc, A = self.nc, self.A
        count = A["L3_ffn_Wr"].shape[1]
        capacity = float(-(-NODES * 5 // (4 * count)))
        self.normalise("L3f_norm", self.X)
        outer, o = self.stage("L3f")
        with outer:
            gates, chosen = o.sb("gates", [NP, 2]), o.sb("chosen", [NP, 2], I32)
            stack, r = self.stage("L3f_route")
            with stack:
                shape = (NP, 1, count)
                wr, br = r.sb("wr", [128, KC, count]), r.sb("br", [NP, count])
                ones = r.sb("ones", [NP, 1])
                mean, wide = r.sb("mean", [128, KC]), r.sb("wide", [128, KC, NP])
                p, load, one = r.sb("p", list(shape)), r.sb("load", list(shape)), r.sb("one", [NP, 1])
                pick = r.sb("pick", [NP, 2])
                mean_ps, logit_ps = r.ps("mean_ps", [128, KC]), r.ps("logit_ps", [NP, count])
                own_dve, loaded, ones_made, summed, wide_ready, logits, arg_ready, exp_ready = (
                    r.sem(n) for n in ("own_dve", "loaded", "ones_made", "summed", "wide_ready", "logits",
                                       "arg_ready", "exp_ready"))
                block = stack.enter_context(nc.Block())

                @block.sync
                def _(sp):
                    self.load_weight(sp, loaded, wr[:], A["L3_ffn_Wr"])
                    sp.dma_start(br[:], A["L3_ffn_br"].partition_broadcast(NP)).then_inc(loaded, 16)

                @block.tensor
                def _(pe):
                    pe.wait_ge(ones_made, 1)
                    for c in range(KC):
                        for t in range(NT):
                            last = nc.tensor.matmul(mean_ps[:, c:c + 1], self.XH[:, t, 128 * c:128 * (c + 1)], ones[:],
                                                    start=(t == 0), stop=(t == NT - 1))
                    last.then_inc(summed, 1)
                    pe.wait_ge(wide_ready, 1)
                    pe.wait_ge(loaded, 32)
                    for c in range(KC):
                        last = nc.tensor.matmul(logit_ps[:], wide[:, c, :], wr[:, c, :], start=(c == 0), stop=(c == KC - 1))
                    last.then_inc(logits, 1)

                @block.scalar
                def _(act):
                    for k in range(2):
                        act.wait_ge(arg_ready, k + 1)
                        nc.scalar.activation(p[:], load[:], ACT.Exp).then_inc(exp_ready, 1)
                    act.wait_ge(arg_ready, 3)
                    nc.scalar.activation(pick[:, 1:2], one[:], ACT.Exp).then_inc(exp_ready, 1)

                @block.vector
                def _(dve):
                    own = InOrder(dve, own_dve)
                    tt, ts = nc.vector.tensor_tensor, nc.vector.tensor_scalar
                    own(nc.vector.memset(ones[:], 1.0))
                    dve.sem_inc(ones_made, 1)
                    dve.wait_ge(summed, 1)
                    own(ts(mean[:], mean_ps[:], 1.0 / NODES, None, ALU.mult))
                    own(nc.vector.tensor_copy(wide[:], bc(mean[:].unsqueeze(2), (128, KC, NP))))
                    dve.sem_inc(wide_ready, 1)
                    dve.wait_ge(logits, 1)
                    dve.wait_ge(loaded, 32)
                    own(tt(p[:, 0, :], logit_ps[:], br[:], ALU.add))

                    def softmax(k):
                        own(nc.vector.tensor_reduce(one[:], p[:, 0, :], AX.X, ALU.max))
                        own(tt(load[:, 0, :], p[:, 0, :], bc(one[:], (NP, count)), ALU.subtract))
                        dve.sem_inc(arg_ready, 1)
                        dve.wait_ge(exp_ready, k)
                        own(nc.vector.tensor_reduce(one[:], p[:, 0, :], AX.X, ALU.add))
                        own(nc.vector.reciprocal(one[:], one[:]))
                        own(tt(p[:, 0, :], p[:, 0, :], bc(one[:], (NP, count)), ALU.mult))

                    softmax(1)
                    own(ts(load[:], p[:], float(NODES), 1e-30, ALU.mult, ALU.max))
                    own(nc.vector.reciprocal(load[:], load[:]))
                    own(ts(load[:], load[:], capacity, 1.0, ALU.mult, ALU.min))
                    own(tt(p[:], p[:], load[:], ALU.mult))
                    softmax(2)
                    _, tops, place = self.top_two(own, r, p, 1, count)
                    for k in range(2):
                        own(ts(one[:], place[k][:], 64.0, None, ALU.add))
                        own(nc.vector.tensor_copy(chosen[:, k:k + 1], one[:]))
                    own(tt(one[:], tops[1][:], tops[0][:], ALU.subtract))
                    dve.sem_inc(arg_ready, 1)
                    dve.wait_ge(exp_ready, 3)
                    own(ts(one[:], pick[:, 1:2], 1.0, None, ALU.add))
                    own(nc.vector.reciprocal(gates[:, 0:1], one[:]))
                    own(tt(gates[:, 1:2], pick[:, 1:2], gates[:, 0:1], ALU.mult))
            self.experts("L3f_experts", 2, A["L3_ffn_W1"], A["L3_ffn_b1"], A["L3_ffn_W2"], A["L3_ffn_b2"],
                         lambda t, i: gates[:, i:i + 1], self.XH, chosen=chosen)
            self.add_normalised("L3f_add", self.XH, A["L3_ffn_gamma"], A["L3_ffn_beta"])


def build(nc, arrays, out):
    program = Program(nc, arrays, out)
    with ExitStack() as stack:
        room = Room(nc, stack, "all")
        program.setup(room)
        program.prepare_edges(room)
        program.layer0_graph()
        program.layer0_experts()
        program.layer1_graph()
        program.layer1_experts()
        program.layer2_graph()
        program.layer2_experts()
        program.layer3_graph()
        program.layer3_experts()
        program.finish()


def kernel(**inputs):
    import concourse.bacc as bacc
    from concourse.bass_utils import run_bass_kernel_spmd

    nc = bacc.Bacc("TRN2", target_bir_lowering=False, num_devices=1)
    given = {name: np.ascontiguousarray(a) for name, a in inputs.items()}
    arrays = {name: nc.dram_tensor(f"in_{name}", a.shape, mybir.dt.from_np(a.dtype), kind="ExternalInput").ap()
              for name, a in given.items()}
    out = nc.dram_tensor("out", (NODES, D), F32, kind="ExternalOutput").ap()
    build(nc, arrays, out)
    r = run_bass_kernel_spmd(nc, [{f"in_{name}": a for name, a in given.items()}], core_ids=[0])
    return r.results[0]["out"]
```
